# Optimizing a Trainium2 kernel written in Bass

```python
import numpy as np
import jax
import jax.numpy as jnp

def _softmax(x, axis=-1):
    return jax.nn.softmax(x, axis=axis)

def _gelu(x):
    return jax.nn.gelu(x, approximate=True)

def _silu(x):
    return jax.nn.silu(x)

def _sigmoid(x):
    return jax.nn.sigmoid(x)

def _layernorm(x, axis=-1, eps=1e-05):
    m = jnp.mean(x, axis=axis, keepdims=True)
    v = jnp.var(x, axis=axis, keepdims=True)
    return (x - m) / jnp.sqrt(v + eps)

def _scatter_add(tgt, idx, src, axis=0):
    return tgt.at[idx].add(src)

def _segment_sum(src, seg, n):
    return jax.ops.segment_sum(src, seg, n)
kernel_name = 'mk_hybrid_d2_jaxref_r8_0c78fb'

def setup_inputs(seed: int=0):
    np.random.seed(seed)
    _w = jnp.asarray

    def _L0_attn_a_setup():
        import jax, jax.numpy as jnp
        import numpy as np
        B, T, DIM = (2, 512, 128)
        DEPTH, HEADS = (4, 8)
        DH = DIM // HEADS
        NLOCAL, WINDOW, BUCKET = (4, 128, 64)
        MULT = 4

        def layer_norm(x, g, b, eps=1e-05):
            m = jnp.mean(x, -1, keepdims=True)
            v = jnp.mean(jnp.square(x - m), -1, keepdims=True)
            return (x - m) * jax.lax.rsqrt(v + eps) * g + b

        def causal_linear_attn(q, k, v):
            b, h, n, e = q.shape
            u = n // BUCKET
            q = jax.nn.softmax(q, axis=-1)
            k = jax.nn.elu(k) + 1.0
            bq = q.reshape(b, h, u, BUCKET, e)
            bk = k.reshape(b, h, u, BUCKET, e)
            bv = v.reshape(b, h, u, BUCKET, e)
            k_cum = jnp.cumsum(bk.sum(axis=-2), axis=-2)
            ctx = jnp.einsum('bhund,bhune->bhude', bk, bv)
            ctx = jnp.cumsum(ctx, axis=2)
            ctx = ctx / (k_cum[..., None] + 1e-06)
            ctx = jnp.pad(ctx, ((0, 0), (0, 0), (1, 0), (0, 0), (0, 0)))[:, :, :-1]
            out = jnp.einsum('bhund,bhude->bhune', bq, ctx)
            return out.reshape(b, h, n, e)

        def local_attn(q, k, v):
            b, lh, t, e = q.shape
            bh = b * lh
            nb = t // WINDOW
            bq = q.reshape(bh, nb, WINDOW, e)
            bk = k.reshape(bh, nb, WINDOW, e)
            bv = v.reshape(bh, nb, WINDOW, e)

            def look_around(x):
                padded = jnp.pad(x, ((0, 0), (1, 0), (0, 0), (0, 0)))
                return jnp.concatenate([padded[:, :-1], padded[:, 1:]], axis=2)
            bk2 = look_around(bk)
            bv2 = look_around(bv)
            tix = jnp.arange(t).reshape(1, nb, WINDOW)
            tpad = jnp.pad(tix, ((0, 0), (1, 0), (0, 0)), constant_values=-1)
            kix = jnp.concatenate([tpad[:, :-1], tpad[:, 1:]], axis=2)
            dots = jnp.einsum('bwie,bwje->bwij', bq, bk2) * e ** (-0.5)
            mask_value = -jnp.finfo(dots.dtype).max
            causal_mask = tix[:, :, :, None] < kix[:, :, None, :]
            pad_mask = (kix == -1)[:, :, None, :]
            dots = jnp.where(causal_mask | pad_mask, mask_value, dots)
            attn = jax.nn.softmax(dots, axis=-1)
            out = jnp.einsum('bwij,bwje->bwie', attn, bv2)
            return out.reshape(b, lh, t, e)

        def self_attention(x, Wq, Wk, Wv, Wo, bo):
            b, t, _ = x.shape
            mh = lambda z: z.reshape(b, t, HEADS, DH).transpose(0, 2, 1, 3)
            q, k, v = (mh(x @ Wq), mh(x @ Wk), mh(x @ Wv))
            lo = local_attn(q[:, :NLOCAL], k[:, :NLOCAL], v[:, :NLOCAL])
            go = causal_linear_attn(q[:, NLOCAL:], k[:, NLOCAL:], v[:, NLOCAL:])
            out = jnp.concatenate([lo, go], axis=1)
            out = out.transpose(0, 2, 1, 3).reshape(b, t, DIM)
            return out @ Wo + bo
        key = jax.random.key(seed)
        ks = jax.random.split(key, 8)
        s = 0.02
        rn = lambda k, shape: jax.random.normal(k, shape, dtype=jnp.float32) * s
        return {'x': jax.random.normal(ks[0], (B, T, DIM), dtype=jnp.float32), 'Wq': rn(ks[1], (DEPTH, DIM, DIM)), 'Wk': rn(ks[2], (DEPTH, DIM, DIM)), 'Wv': rn(ks[3], (DEPTH, DIM, DIM)), 'Wo': rn(ks[4], (DEPTH, DIM, DIM)), 'bo': jnp.zeros((DEPTH, DIM), jnp.float32), 'ln1_g': jnp.ones((DEPTH, DIM), jnp.float32), 'ln1_b': jnp.zeros((DEPTH, DIM), jnp.float32), 'W1': rn(ks[5], (DEPTH, DIM, DIM * MULT)), 'b1': jnp.zeros((DEPTH, DIM * MULT), jnp.float32), 'W2': rn(ks[6], (DEPTH, DIM * MULT, DIM)), 'b2': jnp.zeros((DEPTH, DIM), jnp.float32), 'ln2_g': jnp.ones((DEPTH, DIM), jnp.float32), 'ln2_b': jnp.zeros((DEPTH, DIM), jnp.float32)}
    _L0_attn_a_in = _L0_attn_a_setup()

    def _L0_attn_b_setup():
        import jax, jax.numpy as jnp
        import numpy as np
        N_HEAD = 16
        key = jax.random.key(seed)
        ks = jax.random.split(key, 5)
        B, T, C = (4, 128, 128)
        d = C // N_HEAD
        x = jax.random.normal(ks[0], (B, T, C), dtype=jnp.float32)
        w_attn = jax.random.normal(ks[1], (C, 3 * C), dtype=jnp.float32) * 0.02
        w_proj = jax.random.normal(ks[2], (C, C), dtype=jnp.float32) * 0.02
        embk = 0.02 * jax.random.normal(ks[3], (T, d), dtype=jnp.float32)
        embv = 0.02 * jax.random.normal(ks[4], (T, d), dtype=jnp.float32)
        return {'x': x, 'w_attn': w_attn, 'w_proj': w_proj, 'embk': embk, 'embv': embv}
    _L0_attn_b_in = _L0_attn_b_setup()

    def _L0_ffn_setup():
        import jax, jax.numpy as jnp
        import numpy as np
        IN_DIM = 128
        OUT_DIM = 128
        NUM_EXPERTS = 8
        TOP_K = 2
        key = jax.random.key(seed)
        ks = jax.random.split(key, 5)
        s = 1.0 / np.sqrt(IN_DIM)
        x = jax.random.normal(ks[0], (4, 256, IN_DIM), dtype=jnp.float32)
        Wg = jax.random.uniform(ks[1], (IN_DIM, NUM_EXPERTS), jnp.float32, -s, s)
        bg = jnp.zeros((NUM_EXPERTS,), jnp.float32)
        We = jax.random.uniform(ks[2], (NUM_EXPERTS, OUT_DIM, IN_DIM), jnp.float32, -s, s)
        be = jax.random.uniform(ks[3], (NUM_EXPERTS, OUT_DIM), jnp.float32, -s, s)
        return {'x': x, 'Wg': Wg, 'bg': bg, 'We': We, 'be': be}
    _L0_ffn_in = _L0_ffn_setup()

    def _L1_attn_a_setup():
        import jax, jax.numpy as jnp
        import numpy as np
        NUM_HEADS = 16
        MAX_REL = 128

        def _rel_embeds(table, q_len, k_len):
            dist = jnp.arange(q_len)[:, None] - jnp.arange(k_len)[None, :]
            idx = jnp.clip(dist, -MAX_REL, MAX_REL) + MAX_REL
            return table[idx]
        key = jax.random.key(seed)
        ks = jax.random.split(key, 11)
        B, T, E = (4, 128, 128)
        D = E // NUM_HEADS
        P = 2 * MAX_REL + 1
        s = 0.02
        return {'hidden_states': jax.random.normal(ks[0], (B, T, E), jnp.float32), 'Wq': jax.random.normal(ks[1], (E, E), jnp.float32) * s, 'bq': jax.random.normal(ks[2], (E,), jnp.float32) * s, 'Wk': jax.random.normal(ks[3], (E, E), jnp.float32) * s, 'bk': jax.random.normal(ks[4], (E,), jnp.float32) * s, 'Wv': jax.random.normal(ks[5], (E, E), jnp.float32) * s, 'bv': jax.random.normal(ks[6], (E,), jnp.float32) * s, 'Wo': jax.random.normal(ks[7], (E, E), jnp.float32) * s, 'bo': jax.random.normal(ks[8], (E,), jnp.float32) * s, 'rel_k_emb': jax.random.normal(ks[9], (P, D), jnp.float32) * s, 'rel_v_emb': jax.random.normal(ks[10], (P, D), jnp.float32) * s}
    _L1_attn_a_in = _L1_attn_a_setup()

    def _L1_attn_b_setup():
        import jax, jax.numpy as jnp
        import numpy as np
        B, L, DM = (4, 256, 128)
        key = jax.random.key(seed)
        ks = jax.random.split(key, 13)
        n = lambda k, shape, s=1.0: jax.random.normal(k, shape, dtype=jnp.float32) * s
        W_SCALE = 0.02
        K_SCALE = 0.02
        return {'u': n(ks[0], (B, L, DM)), 'Wq': n(ks[1], (DM, DM), W_SCALE), 'bq': n(ks[2], (DM,), W_SCALE), 'Wk': n(ks[3], (DM, DM), W_SCALE), 'bk': n(ks[4], (DM,), W_SCALE), 'Wv': n(ks[5], (DM, DM), W_SCALE), 'bv': n(ks[6], (DM,), W_SCALE), 'k_kernel': n(ks[7], (DM, L), K_SCALE), 'k_D': n(ks[8], (DM,)), 'ssm_kernel': n(ks[9], (DM, L), K_SCALE), 'D': n(ks[10], (DM,)), 'Wo': n(ks[11], (DM, DM), W_SCALE), 'bo': n(ks[12], (DM,), W_SCALE)}
    _L1_attn_b_in = _L1_attn_b_setup()

    def _L1_ffn_setup():
        import jax, jax.numpy as jnp
        import numpy as np
        DIM = 128
        DEPTH = 2
        HEADS = 8
        DIM_HEAD = 64
        WINDOW = 64
        INNER = HEADS * DIM_HEAD
        HID = int(DIM * 4 * 2 / 3)
        B, N = (2, 1024)
        QK_SCALE = 8.0

        def shift_token(t):
            t1, t2 = jnp.split(t, 2, axis=-1)
            t2 = jnp.pad(t2, ((0, 0), (1, 0), (0, 0)))[:, :-1]
            return jnp.concatenate([t1, t2], axis=-1)

        def l2norm(t):
            return t / jnp.clip(jnp.linalg.norm(t, axis=-1, keepdims=True), 1e-12)

        def rotate_half(x):
            x1, x2 = jnp.split(x, 2, axis=-1)
            return jnp.concatenate([-x2, x1], axis=-1)

        def rotary_xpos(q, k):
            n = q.shape[-2]
            half_idx = jnp.arange(0, DIM_HEAD, 2, dtype=jnp.float32)
            inv_freq = 1.0 / 10000.0 ** (half_idx / DIM_HEAD)
            t = jnp.arange(n, dtype=jnp.float32)
            freqs = t[:, None] * inv_freq[None, :]
            freqs = jnp.concatenate([freqs, freqs], axis=-1)
            base = (half_idx + 0.4 * DIM_HEAD) / (1.4 * DIM_HEAD)
            power = (t - n // 2) / float(WINDOW // 2)
            scale = base[None, :] ** power[:, None]
            scale = jnp.concatenate([scale, scale], axis=-1)
            cos, sin = (jnp.cos(freqs), jnp.sin(freqs))
            q = q * cos * scale + rotate_half(q) * sin * scale
            k = k * cos / scale + rotate_half(k) * sin / scale
            return (q, k)

        def local_attention(q, k, v):
            b, h, n, d = q.shape
            w = n // WINDOW
            bq = q.reshape(b, h, w, WINDOW, d) * QK_SCALE
            bk = k.reshape(b, h, w, WINDOW, d)
            bv = v.reshape(b, h, w, WINDOW, d)

            def look_around(t):
                p = jnp.pad(t, ((0, 0), (0, 0), (1, 0), (0, 0), (0, 0)))
                return jnp.concatenate([p[:, :, :w], p[:, :, 1:]], axis=3)
            bk, bv = (look_around(bk), look_around(bv))
            bt = jnp.arange(n).reshape(w, WINDOW)
            btp = jnp.pad(bt, ((1, 0), (0, 0)), constant_values=-1)
            btk = jnp.concatenate([btp[:w], btp[1:]], axis=1)
            sim = jnp.einsum('bhwid,bhwjd->bhwij', bq, bk)
            i = bt[:, :, None]
            j = btk[:, None, :]
            mask = (i < j) | (i > j + WINDOW) | (j == -1)
            sim = jnp.where(mask, -jnp.finfo(sim.dtype).max, sim)
            attn = jax.nn.softmax(sim, axis=-1)
            out = jnp.einsum('bhwij,bhwjd->bhwid', attn, bv)
            return out.reshape(b, h, n, d)

        def _layer(x, wqkv, qs, ksc, wo, lg, lb, w1, b1, w2, b2):
            b, n, _ = x.shape
            h = shift_token(x)
            qkv = h @ wqkv
            q, k, v = jnp.split(qkv, 3, axis=-1)
            to_heads = lambda t: t.reshape(b, n, HEADS, DIM_HEAD).transpose(0, 2, 1, 3)
            q, k, v = (to_heads(q), to_heads(k), to_heads(v))
            q = l2norm(q) * qs
            k = l2norm(k) * ksc
            q, k = rotary_xpos(q, k)
            o = local_attention(q, k, v)
            o = o.transpose(0, 2, 1, 3).reshape(b, n, INNER)
            x = x + o @ wo
            h = shift_token(x)
            mu = h.mean(-1, keepdims=True)
            var = h.var(-1, keepdims=True)
            h = (h - mu) / jnp.sqrt(var + 1e-05) * lg + lb
            h = h @ w1 + b1
            a, g = jnp.split(h, 2, axis=-1)
            h = a * jax.nn.gelu(g, approximate=False)
            x = x + h @ w2 + b2
            return x
        key = jax.random.key(seed)
        ks = jax.random.split(key, 6)
        return {'x': jax.random.normal(ks[0], (B, N, DIM), jnp.float32), 'wqkv': jax.random.normal(ks[1], (DEPTH, DIM, 3 * INNER), jnp.float32) * 0.02, 'q_scale': jnp.ones((DEPTH, DIM_HEAD), jnp.float32), 'k_scale': jnp.ones((DEPTH, DIM_HEAD), jnp.float32), 'wo': jax.random.normal(ks[2], (DEPTH, INNER, DIM), jnp.float32) * 0.02, 'ln_g': jnp.ones((DEPTH, DIM), jnp.float32), 'ln_b': jnp.zeros((DEPTH, DIM), jnp.float32), 'w1': jax.random.normal(ks[3], (DEPTH, DIM, 2 * HID), jnp.float32) * 0.02, 'b1': jnp.zeros((DEPTH, 2 * HID), jnp.float32), 'w2': jax.random.normal(ks[4], (DEPTH, HID, DIM), jnp.float32) * 0.02, 'b2': jnp.zeros((DEPTH, DIM), jnp.float32)}
    _L1_ffn_in = _L1_ffn_setup()
    _d = {'L0_attn_a_x': _L0_attn_a_in['x'], 'L0_attn_a_Wq': _L0_attn_a_in['Wq'], 'L0_attn_a_Wk': _L0_attn_a_in['Wk'], 'L0_attn_a_Wv': _L0_attn_a_in['Wv'], 'L0_attn_a_Wo': _L0_attn_a_in['Wo'], 'L0_attn_a_bo': _L0_attn_a_in['bo'], 'L0_attn_a_ln1_g': _L0_attn_a_in['ln1_g'], 'L0_attn_a_ln1_b': _L0_attn_a_in['ln1_b'], 'L0_attn_a_W1': _L0_attn_a_in['W1'], 'L0_attn_a_b1': _L0_attn_a_in['b1'], 'L0_attn_a_W2': _L0_attn_a_in['W2'], 'L0_attn_a_b2': _L0_attn_a_in['b2'], 'L0_attn_a_ln2_g': _L0_attn_a_in['ln2_g'], 'L0_attn_a_ln2_b': _L0_attn_a_in['ln2_b'], 'L0_attn_b_w_attn': _L0_attn_b_in['w_attn'], 'L0_attn_b_w_proj': _L0_attn_b_in['w_proj'], 'L0_attn_b_embk': _L0_attn_b_in['embk'], 'L0_attn_b_embv': _L0_attn_b_in['embv'], 'L0_ffn_Wg': _L0_ffn_in['Wg'], 'L0_ffn_bg': _L0_ffn_in['bg'], 'L0_ffn_We': _L0_ffn_in['We'], 'L0_ffn_be': _L0_ffn_in['be'], 'L1_attn_a_Wq': _L1_attn_a_in['Wq'], 'L1_attn_a_bq': _L1_attn_a_in['bq'], 'L1_attn_a_Wk': _L1_attn_a_in['Wk'], 'L1_attn_a_bk': _L1_attn_a_in['bk'], 'L1_attn_a_Wv': _L1_attn_a_in['Wv'], 'L1_attn_a_bv': _L1_attn_a_in['bv'], 'L1_attn_a_Wo': _L1_attn_a_in['Wo'], 'L1_attn_a_bo': _L1_attn_a_in['bo'], 'L1_attn_a_rel_k_emb': _L1_attn_a_in['rel_k_emb'], 'L1_attn_a_rel_v_emb': _L1_attn_a_in['rel_v_emb'], 'L1_attn_b_Wq': _L1_attn_b_in['Wq'], 'L1_attn_b_bq': _L1_attn_b_in['bq'], 'L1_attn_b_Wk': _L1_attn_b_in['Wk'], 'L1_attn_b_bk': _L1_attn_b_in['bk'], 'L1_attn_b_Wv': _L1_attn_b_in['Wv'], 'L1_attn_b_bv': _L1_attn_b_in['bv'], 'L1_attn_b_k_kernel': _L1_attn_b_in['k_kernel'], 'L1_attn_b_k_D': _L1_attn_b_in['k_D'], 'L1_attn_b_ssm_kernel': _L1_attn_b_in['ssm_kernel'], 'L1_attn_b_D': _L1_attn_b_in['D'], 'L1_attn_b_Wo': _L1_attn_b_in['Wo'], 'L1_attn_b_bo': _L1_attn_b_in['bo'], 'L1_ffn_wqkv': _L1_ffn_in['wqkv'], 'L1_ffn_q_scale': _L1_ffn_in['q_scale'], 'L1_ffn_k_scale': _L1_ffn_in['k_scale'], 'L1_ffn_wo': _L1_ffn_in['wo'], 'L1_ffn_ln_g': _L1_ffn_in['ln_g'], 'L1_ffn_ln_b': _L1_ffn_in['ln_b'], 'L1_ffn_w1': _L1_ffn_in['w1'], 'L1_ffn_b1': _L1_ffn_in['b1'], 'L1_ffn_w2': _L1_ffn_in['w2'], 'L1_ffn_b2': _L1_ffn_in['b2']}
    _x0 = _d['L0_attn_a_x']
    _d['L0_attn_a_x'] = jax.random.normal(jax.random.fold_in(jax.random.key(seed), 1), (4, 512, 128), dtype=_x0.dtype)
    del _x0
    return _d

def reference(L0_attn_a_x, L0_attn_a_Wq, L0_attn_a_Wk, L0_attn_a_Wv, L0_attn_a_Wo, L0_attn_a_bo, L0_attn_a_ln1_g, L0_attn_a_ln1_b, L0_attn_a_W1, L0_attn_a_b1, L0_attn_a_W2, L0_attn_a_b2, L0_attn_a_ln2_g, L0_attn_a_ln2_b, L0_attn_b_w_attn, L0_attn_b_w_proj, L0_attn_b_embk, L0_attn_b_embv, L0_ffn_Wg, L0_ffn_bg, L0_ffn_We, L0_ffn_be, L1_attn_a_Wq, L1_attn_a_bq, L1_attn_a_Wk, L1_attn_a_bk, L1_attn_a_Wv, L1_attn_a_bv, L1_attn_a_Wo, L1_attn_a_bo, L1_attn_a_rel_k_emb, L1_attn_a_rel_v_emb, L1_attn_b_Wq, L1_attn_b_bq, L1_attn_b_Wk, L1_attn_b_bk, L1_attn_b_Wv, L1_attn_b_bv, L1_attn_b_k_kernel, L1_attn_b_k_D, L1_attn_b_ssm_kernel, L1_attn_b_D, L1_attn_b_Wo, L1_attn_b_bo, L1_ffn_wqkv, L1_ffn_q_scale, L1_ffn_k_scale, L1_ffn_wo, L1_ffn_ln_g, L1_ffn_ln_b, L1_ffn_w1, L1_ffn_b1, L1_ffn_w2, L1_ffn_b2):

    def _L0_attn_a_ref(x, Wq, Wk, Wv, Wo, bo, ln1_g, ln1_b, W1, b1, W2, b2, ln2_g, ln2_b):
        import jax, jax.numpy as jnp
        import numpy as np
        B, T, DIM = (2, 512, 128)
        DEPTH, HEADS = (4, 8)
        DH = DIM // HEADS
        NLOCAL, WINDOW, BUCKET = (4, 128, 64)
        MULT = 4

        def layer_norm(x, g, b, eps=1e-05):
            m = jnp.mean(x, -1, keepdims=True)
            v = jnp.mean(jnp.square(x - m), -1, keepdims=True)
            return (x - m) * jax.lax.rsqrt(v + eps) * g + b

        def causal_linear_attn(q, k, v):
            b, h, n, e = q.shape
            u = n // BUCKET
            q = jax.nn.softmax(q, axis=-1)
            k = jax.nn.elu(k) + 1.0
            bq = q.reshape(b, h, u, BUCKET, e)
            bk = k.reshape(b, h, u, BUCKET, e)
            bv = v.reshape(b, h, u, BUCKET, e)
            k_cum = jnp.cumsum(bk.sum(axis=-2), axis=-2)
            ctx = jnp.einsum('bhund,bhune->bhude', bk, bv)
            ctx = jnp.cumsum(ctx, axis=2)
            ctx = ctx / (k_cum[..., None] + 1e-06)
            ctx = jnp.pad(ctx, ((0, 0), (0, 0), (1, 0), (0, 0), (0, 0)))[:, :, :-1]
            out = jnp.einsum('bhund,bhude->bhune', bq, ctx)
            return out.reshape(b, h, n, e)

        def local_attn(q, k, v):
            b, lh, t, e = q.shape
            bh = b * lh
            nb = t // WINDOW
            bq = q.reshape(bh, nb, WINDOW, e)
            bk = k.reshape(bh, nb, WINDOW, e)
            bv = v.reshape(bh, nb, WINDOW, e)

            def look_around(x):
                padded = jnp.pad(x, ((0, 0), (1, 0), (0, 0), (0, 0)))
                return jnp.concatenate([padded[:, :-1], padded[:, 1:]], axis=2)
            bk2 = look_around(bk)
            bv2 = look_around(bv)
            tix = jnp.arange(t).reshape(1, nb, WINDOW)
            tpad = jnp.pad(tix, ((0, 0), (1, 0), (0, 0)), constant_values=-1)
            kix = jnp.concatenate([tpad[:, :-1], tpad[:, 1:]], axis=2)
            dots = jnp.einsum('bwie,bwje->bwij', bq, bk2) * e ** (-0.5)
            mask_value = -jnp.finfo(dots.dtype).max
            causal_mask = tix[:, :, :, None] < kix[:, :, None, :]
            pad_mask = (kix == -1)[:, :, None, :]
            dots = jnp.where(causal_mask | pad_mask, mask_value, dots)
            attn = jax.nn.softmax(dots, axis=-1)
            out = jnp.einsum('bwij,bwje->bwie', attn, bv2)
            return out.reshape(b, lh, t, e)

        def self_attention(x, Wq, Wk, Wv, Wo, bo):
            b, t, _ = x.shape
            mh = lambda z: z.reshape(b, t, HEADS, DH).transpose(0, 2, 1, 3)
            q, k, v = (mh(x @ Wq), mh(x @ Wk), mh(x @ Wv))
            lo = local_attn(q[:, :NLOCAL], k[:, :NLOCAL], v[:, :NLOCAL])
            go = causal_linear_attn(q[:, NLOCAL:], k[:, NLOCAL:], v[:, NLOCAL:])
            out = jnp.concatenate([lo, go], axis=1)
            out = out.transpose(0, 2, 1, 3).reshape(b, t, DIM)
            return out @ Wo + bo
        for i in range(DEPTH):
            x = x + self_attention(layer_norm(x, ln1_g[i], ln1_b[i]), Wq[i], Wk[i], Wv[i], Wo[i], bo[i])
            h = layer_norm(x, ln2_g[i], ln2_b[i])
            x = x + (jax.nn.gelu(h @ W1[i] + b1[i], approximate=False) @ W2[i] + b2[i])
        return x

    def _L0_attn_b_ref(x, w_attn, w_proj, embk, embv):
        import jax, jax.numpy as jnp
        import numpy as np
        N_HEAD = 16
        B, T, C = x.shape
        H = N_HEAD
        d = C // H
        qkv = x @ w_attn
        q, k, v = jnp.split(qkv, 3, axis=2)
        q = q.reshape(B, T, H, d).transpose(0, 2, 1, 3)
        k = k.reshape(B, T, H, d).transpose(0, 2, 1, 3)
        v = v.reshape(B, T, H, d).transpose(0, 2, 1, 3)
        idx = jnp.arange(T)
        rel = jnp.tril(idx[:, None] - idx[None, :])
        rk = embk[rel]
        rv = embv[rel]
        scale = 1.0 / np.sqrt(d).astype(np.float32)
        att = jnp.einsum('bhtd,bhsd->bhts', q, k) * scale + jnp.einsum('bhtd,tsd->bhts', q, rk)
        causal = idx[None, :] <= idx[:, None]
        att = jnp.where(causal[None, None], att, -jnp.inf)
        att = jax.nn.softmax(att, axis=-1)
        y = jnp.einsum('bhts,bhsd->bhtd', att, v) + jnp.einsum('bhts,tsd->bhtd', att, rv)
        y = y.transpose(0, 2, 1, 3).reshape(B, T, C)
        return y @ w_proj

    def _L0_ffn_ref(x, Wg, bg, We, be):
        import jax, jax.numpy as jnp
        import numpy as np
        IN_DIM = 128
        OUT_DIM = 128
        NUM_EXPERTS = 8
        TOP_K = 2
        gate = jax.nn.softmax(x @ Wg + bg, axis=-1)
        topk_vals, topk_idx = jax.lax.top_k(gate, TOP_K)
        onehot = jax.nn.one_hot(topk_idx, NUM_EXPERTS, dtype=gate.dtype)
        gate_sparse = jnp.einsum('bsk,bske->bse', topk_vals, onehot)
        gate_sparse = gate_sparse / jnp.sum(gate_sparse, axis=-1, keepdims=True)
        y = jnp.einsum('bsi,eoi->bseo', x, We) + be[None, None, :, :].transpose(0, 1, 2, 3)
        out = jnp.einsum('bseo,bse->bso', y, gate_sparse)
        return out

    def _L1_attn_a_ref(hidden_states, Wq, bq, Wk, bk, Wv, bv, Wo, bo, rel_k_emb, rel_v_emb):
        import jax, jax.numpy as jnp
        import numpy as np
        NUM_HEADS = 16
        MAX_REL = 128

        def _rel_embeds(table, q_len, k_len):
            dist = jnp.arange(q_len)[:, None] - jnp.arange(k_len)[None, :]
            idx = jnp.clip(dist, -MAX_REL, MAX_REL) + MAX_REL
            return table[idx]
        B, T, E = hidden_states.shape
        H = NUM_HEADS
        D = E // H
        scaling = jnp.sqrt(jnp.asarray(D, hidden_states.dtype))
        q = hidden_states @ Wq.T + bq
        k = hidden_states @ Wk.T + bk
        v = hidden_states @ Wv.T + bv
        qh = q.reshape(B, T, H, D).transpose(0, 2, 1, 3)
        kh = k.reshape(B, T, H, D).transpose(0, 2, 1, 3)
        vh = v.reshape(B, T, H, D).transpose(0, 2, 1, 3)
        score1 = jnp.einsum('bhqd,bhkd->bhqk', qh, kh)
        rel_k = _rel_embeds(rel_k_emb, T, T)
        s2 = jnp.einsum('bhqd,qkd->qbhk', qh, rel_k)
        s2 = s2.reshape(T, H, B, T).transpose(2, 1, 0, 3)
        scores = (score1 + s2) / scaling
        attn = jax.nn.softmax(scores, axis=-1)
        w1 = jnp.einsum('bhqk,bhkd->bhqd', attn, vh)
        rel_v = _rel_embeds(rel_v_emb, T, T)
        se = attn.reshape(B * H, T, T).transpose(1, 0, 2)
        w2 = jnp.einsum('qnk,qkd->qnd', se, rel_v)
        w2 = w2.reshape(T, H, B, D).transpose(2, 1, 0, 3)
        out = (w1 + w2).transpose(0, 2, 1, 3).reshape(B, T, E)
        return out @ Wo.T + bo

    def _L1_attn_b_ref(u, Wq, bq, Wk, bk, Wv, bv, k_kernel, k_D, ssm_kernel, D, Wo, bo):
        import jax, jax.numpy as jnp
        import numpy as np
        B, L, DM = (4, 256, 128)
        Lseq = u.shape[1]
        fft_size = 2 * Lseq
        q = jnp.einsum('blh,dh->bdl', u, Wq) + bq[None, :, None]
        k = jnp.einsum('blh,dh->bdl', u, Wk) + bk[None, :, None]
        v = jnp.einsum('blh,dh->bdl', u, Wv) + bv[None, :, None]
        k_kernel_f = jnp.fft.rfft(k_kernel, n=fft_size)
        k_f = jnp.fft.rfft(k, n=fft_size)
        shift_k = jnp.fft.irfft(k_kernel_f[None] * k_f, n=fft_size)[..., :Lseq]
        k = shift_k + k_D[None, :, None] * k
        kv = k * v
        kv_f = jnp.fft.rfft(kv, n=fft_size)
        ssm_kernel_f = jnp.fft.rfft(ssm_kernel, n=fft_size)
        y = jnp.fft.irfft(kv_f * ssm_kernel_f[None], n=fft_size)[..., :Lseq]
        y = y + kv * D[None, :, None]
        y = y * q
        y = jnp.swapaxes(y, 1, 2)
        return jnp.einsum('blh,oh->blo', y, Wo) + bo

    def _L1_ffn_ref(x, wqkv, q_scale, k_scale, wo, ln_g, ln_b, w1, b1, w2, b2):
        import jax, jax.numpy as jnp
        import numpy as np
        DIM = 128
        DEPTH = 2
        HEADS = 8
        DIM_HEAD = 64
        WINDOW = 64
        INNER = HEADS * DIM_HEAD
        HID = int(DIM * 4 * 2 / 3)
        B, N = (2, 1024)
        QK_SCALE = 8.0

        def shift_token(t):
            t1, t2 = jnp.split(t, 2, axis=-1)
            t2 = jnp.pad(t2, ((0, 0), (1, 0), (0, 0)))[:, :-1]
            return jnp.concatenate([t1, t2], axis=-1)

        def l2norm(t):
            return t / jnp.clip(jnp.linalg.norm(t, axis=-1, keepdims=True), 1e-12)

        def rotate_half(x):
            x1, x2 = jnp.split(x, 2, axis=-1)
            return jnp.concatenate([-x2, x1], axis=-1)

        def rotary_xpos(q, k):
            n = q.shape[-2]
            half_idx = jnp.arange(0, DIM_HEAD, 2, dtype=jnp.float32)
            inv_freq = 1.0 / 10000.0 ** (half_idx / DIM_HEAD)
            t = jnp.arange(n, dtype=jnp.float32)
            freqs = t[:, None] * inv_freq[None, :]
            freqs = jnp.concatenate([freqs, freqs], axis=-1)
            base = (half_idx + 0.4 * DIM_HEAD) / (1.4 * DIM_HEAD)
            power = (t - n // 2) / float(WINDOW // 2)
            scale = base[None, :] ** power[:, None]
            scale = jnp.concatenate([scale, scale], axis=-1)
            cos, sin = (jnp.cos(freqs), jnp.sin(freqs))
            q = q * cos * scale + rotate_half(q) * sin * scale
            k = k * cos / scale + rotate_half(k) * sin / scale
            return (q, k)

        def local_attention(q, k, v):
            b, h, n, d = q.shape
            w = n // WINDOW
            bq = q.reshape(b, h, w, WINDOW, d) * QK_SCALE
            bk = k.reshape(b, h, w, WINDOW, d)
            bv = v.reshape(b, h, w, WINDOW, d)

            def look_around(t):
                p = jnp.pad(t, ((0, 0), (0, 0), (1, 0), (0, 0), (0, 0)))
                return jnp.concatenate([p[:, :, :w], p[:, :, 1:]], axis=3)
            bk, bv = (look_around(bk), look_around(bv))
            bt = jnp.arange(n).reshape(w, WINDOW)
            btp = jnp.pad(bt, ((1, 0), (0, 0)), constant_values=-1)
            btk = jnp.concatenate([btp[:w], btp[1:]], axis=1)
            sim = jnp.einsum('bhwid,bhwjd->bhwij', bq, bk)
            i = bt[:, :, None]
            j = btk[:, None, :]
            mask = (i < j) | (i > j + WINDOW) | (j == -1)
            sim = jnp.where(mask, -jnp.finfo(sim.dtype).max, sim)
            attn = jax.nn.softmax(sim, axis=-1)
            out = jnp.einsum('bhwij,bhwjd->bhwid', attn, bv)
            return out.reshape(b, h, n, d)

        def _layer(x, wqkv, qs, ksc, wo, lg, lb, w1, b1, w2, b2):
            b, n, _ = x.shape
            h = shift_token(x)
            qkv = h @ wqkv
            q, k, v = jnp.split(qkv, 3, axis=-1)
            to_heads = lambda t: t.reshape(b, n, HEADS, DIM_HEAD).transpose(0, 2, 1, 3)
            q, k, v = (to_heads(q), to_heads(k), to_heads(v))
            q = l2norm(q) * qs
            k = l2norm(k) * ksc
            q, k = rotary_xpos(q, k)
            o = local_attention(q, k, v)
            o = o.transpose(0, 2, 1, 3).reshape(b, n, INNER)
            x = x + o @ wo
            h = shift_token(x)
            mu = h.mean(-1, keepdims=True)
            var = h.var(-1, keepdims=True)
            h = (h - mu) / jnp.sqrt(var + 1e-05) * lg + lb
            h = h @ w1 + b1
            a, g = jnp.split(h, 2, axis=-1)
            h = a * jax.nn.gelu(g, approximate=False)
            x = x + h @ w2 + b2
            return x
        for l in range(DEPTH):
            x = _layer(x, wqkv[l], q_scale[l], k_scale[l], wo[l], ln_g[l], ln_b[l], w1[l], b1[l], w2[l], b2[l])
        return x
    x = L0_attn_a_x
    x = x + _L0_attn_a_ref(_layernorm(x, axis=-1), L0_attn_a_Wq, L0_attn_a_Wk, L0_attn_a_Wv, L0_attn_a_Wo, L0_attn_a_bo, L0_attn_a_ln1_g, L0_attn_a_ln1_b, L0_attn_a_W1, L0_attn_a_b1, L0_attn_a_W2, L0_attn_a_b2, L0_attn_a_ln2_g, L0_attn_a_ln2_b)
    x = x + _L0_ffn_ref(_layernorm(x, axis=-1), L0_ffn_Wg, L0_ffn_bg, L0_ffn_We, L0_ffn_be)
    x = x + _L0_attn_b_ref(_layernorm(x, axis=-1), L0_attn_b_w_attn, L0_attn_b_w_proj, L0_attn_b_embk, L0_attn_b_embv)
    x = x + _L0_ffn_ref(_layernorm(x, axis=-1), L0_ffn_Wg, L0_ffn_bg, L0_ffn_We, L0_ffn_be)
    x = x + _L1_attn_a_ref(_layernorm(x, axis=-1), L1_attn_a_Wq, L1_attn_a_bq, L1_attn_a_Wk, L1_attn_a_bk, L1_attn_a_Wv, L1_attn_a_bv, L1_attn_a_Wo, L1_attn_a_bo, L1_attn_a_rel_k_emb, L1_attn_a_rel_v_emb)
    x = x + _L1_ffn_ref(_layernorm(x, axis=-1), L1_ffn_wqkv, L1_ffn_q_scale, L1_ffn_k_scale, L1_ffn_wo, L1_ffn_ln_g, L1_ffn_ln_b, L1_ffn_w1, L1_ffn_b1, L1_ffn_w2, L1_ffn_b2)
    x = x + _L1_attn_b_ref(_layernorm(x, axis=-1), L1_attn_b_Wq, L1_attn_b_bq, L1_attn_b_Wk, L1_attn_b_bk, L1_attn_b_Wv, L1_attn_b_bv, L1_attn_b_k_kernel, L1_attn_b_k_D, L1_attn_b_ssm_kernel, L1_attn_b_D, L1_attn_b_Wo, L1_attn_b_bo)
    x = x + _L1_ffn_ref(_layernorm(x, axis=-1), L1_ffn_wqkv, L1_ffn_q_scale, L1_ffn_k_scale, L1_ffn_wo, L1_ffn_ln_g, L1_ffn_ln_b, L1_ffn_w1, L1_ffn_b1, L1_ffn_w2, L1_ffn_b2)
    return x

_drawn_inputs = setup_inputs


def setup_inputs(seed=0):
    import zlib

    import numpy as np

    out = dict(_drawn_inputs(seed))
    spreads = {'L0_attn_a_bo': (0.0, 0.1),
     'L0_attn_a_ln1_g': (1.0, 0.6),
     'L0_attn_a_ln1_b': (0.0, 0.411),
     'L0_attn_a_b1': (0.0, 0.1),
     'L0_attn_a_b2': (0.0, 0.1),
     'L0_attn_a_ln2_g': (1.0, 0.552),
     'L0_attn_a_ln2_b': (0.0, 0.526),
     'L0_ffn_bg': (0.0, 0.1),
     'L1_ffn_q_scale': (1.0, 0.6),
     'L1_ffn_k_scale': (1.0, 0.6),
     'L1_ffn_ln_g': (1.0, 0.6),
     'L1_ffn_ln_b': (0.0, 0.8),
     'L1_ffn_b1': (0.0, 0.8),
     'L1_ffn_b2': (0.0, 0.1)}
    factors = {'L0_attn_a_Wq': 8.0,
     'L0_attn_a_Wk': 8.0,
     'L0_attn_b_w_attn': 5.501,
     'L0_attn_b_w_proj': 5.069,
     'L0_attn_b_embk': 8.0,
     'L0_attn_b_embv': 6.8,
     'L1_attn_a_Wq': 8.0,
     'L1_attn_a_bq': 8.0,
     'L1_attn_a_Wk': 8.0,
     'L1_attn_a_bk': 8.0,
     'L1_attn_a_Wv': 8.0,
     'L1_attn_a_bv': 8.0,
     'L1_attn_a_Wo': 8.0,
     'L1_attn_a_bo': 5.859,
     'L1_attn_a_rel_k_emb': 8.0,
     'L1_attn_a_rel_v_emb': 8.0,
     'L1_attn_b_Wq': 8.0,
     'L1_attn_b_bq': 8.0,
     'L1_attn_b_Wk': 8.0,
     'L1_attn_b_bk': 8.0,
     'L1_attn_b_Wv': 8.0,
     'L1_attn_b_bv': 8.0,
     'L1_attn_b_k_kernel': 8.0,
     'L1_attn_b_k_D': 8.0,
     'L1_attn_b_ssm_kernel': 8.0,
     'L1_attn_b_D': 8.0,
     'L1_attn_b_Wo': 8.0,
     'L1_attn_b_bo': 8.0,
     'L1_ffn_wqkv': 2.914,
     'L1_ffn_wo': 2.779,
     'L1_ffn_w1': 5.943,
     'L1_ffn_w2': 5.783}
    for name, (base, spread) in spreads.items():
        noise = np.random.default_rng([zlib.crc32(name.encode()), seed]).standard_normal(out[name].shape)
        drawn = base * np.exp(spread * noise) if base else spread * noise
        out[name] = jnp.asarray(drawn.astype(out[name].dtype))
    for name, factor in factors.items():
        out[name] = (out[name] * factor).astype(out[name].dtype)
    return out
```

```python
from contextlib import ExitStack

import concourse.bass as bass
from concourse import mybir

F32 = mybir.dt.float32
ALU = mybir.AluOpType
ACT = mybir.ActivationFunctionType
AX = mybir.AxisListType

P = 128
C = 4
T = 512
NT = T // P
BANKS = 8
NEG = -1.0e30
EPS = 1e-5

DEPTH_A, DH_A, LOC, BUCKET = 4, 16, 4, 64
NB_A = T // BUCKET
HID_A = 4 * P
HEADS_R, D_R, QG = 16, 8, 8
GROUPS = T // QG
CHUNKS = C * GROUPS // 4
ET_W = 2 * T - QG
EV_W = (T - P) + T
EXPERTS = 8
DEPTH_W, HEADS_W, D_W, WIN = 2, 8, 64, 64
PAIRS = HEADS_W // 2
HID_W, HT_W = 341, 3
TAPS, DFT = 256, 384
FT = DFT // P


def columns(parts):
    at, out = 0, {}
    for name, width in parts:
        out[name] = (at, width)
        at += width
    return out, at


CONST, CONST_W = columns([
    ("ident", 128), ("mean", 128), ("ones", 128), ("pair_ones", 128), ("head_mask", 128), ("pick_query", 8),
    ("query_mask", 64), ("spread_mask", 16), ("repeat", 64), ("diag_query", 128), ("local_mask", 256),
    ("swap_mask", 64), ("pick_pair", 32), ("quarter_mask", 32), ("window_mask", 192), ("linear_mask", 64), ("lower", 64), ("eps", 4)])
WA, WA_W = columns([
    ("q_loc", 128), ("k_loc", 128), ("qkv", 256), ("o", 128), ("w1", HID_A), ("w2", HID_A),
    ("bo", 1), ("g1", 1), ("b1n", 1), ("b1", 4), ("b2", 1), ("g2", 1), ("b2n", 1)])
WE, WE_W = columns([("experts", EXPERTS * P), ("gate", EXPERTS), ("be", P), ("bg", EXPERTS)])
WR, WR_W = columns([("q", 128), ("k", 128), ("v", 128), ("o", 128), ("bq", 1), ("bk", 1), ("bv", 1), ("bo", 1)])
WW, WW_W = columns([
    ("q", 512), ("q_rot", 512), ("k", 512), ("k_rot", 512), ("v", 512), ("o", 512),
    ("w1a", HT_W * P), ("w1g", HT_W * P), ("w2", HT_W * P),
    ("qs", 1), ("qs_rot", 1), ("ks", 1), ("ks_rot", 1), ("g", 1), ("b", 1), ("b1a", HT_W), ("b1g", HT_W), ("b2", 1)])
WH, WH_W = columns([("q", 128), ("k", 128), ("v", 128), ("o", 128), ("kernels", 2 * TAPS),
                    ("bq", 1), ("bk", 1), ("bv", 1), ("bo", 1), ("k_D", 1), ("D", 1)])
SLOT = max(WA_W, WE_W, WR_W, WW_W, WH_W)

LOADS = ["A0", "A1", "A2", "A3", "E", "R0", "E", "R1", "W0", "W1", "H", "W0", "W1"]


class Step:

    def __init__(self, kind, n, k, load, stream, norm, shift, affine, rotations, c=0, w=0, i=0, half=0, which=0, conv=0,
                 x="", pt=0, hp=0, src="", via="", dst="", gain=None, table=None, name=""):
        self.kind, self.n, self.k = kind, n, k
        self.load, self.stream, self.norm, self.shift = load, stream, norm, shift
        self.affine, self.rotations = affine, rotations
        self.c, self.w, self.i = c, w, i
        self.half, self.which, self.conv = half, which, conv
        self.x, self.pt, self.hp = x, pt, hp
        self.src, self.via, self.dst = src, via, dst
        self.gain, self.table, self.name = gain, table, name


STREAM = (("stream_done", 1, 1),)


def each(name, per, n=None):
    return tuple((name, per, i + 1) for i in range(n or per))


LAST_READ = {
    "enter": STREAM,
    "norm": each("norm_centered", C) + each("norm_rstd", C),
    "a_project": (("a_local_copied", LOC + 1, LOC), ("a_local_copied", LOC + 1, LOC + 1)) + each("a_token_copied", 2),
    "a_context": (("a_q_turned", 1, 1), ("a_context_read", 1, 1)),
    "a_scores": each("a_scored", LOC),
    "a_turn": (("a_turned_act", 1, 1), ("a_turned_dve", 1, 1)),
    "a_values": (("a_normalised", 1, 1),),
    "a_out": (("a_heads", 1, 1),) + STREAM,
    "a_mlp": each("a_gelu", 4) + STREAM,
    "gate": (("gate_copied", 1, 1),) + each("gate_turned", C),
    "expert": tuple(("expert_scaled", 16, 2 * (4 * e + 3) + a + 1) for a in range(2) for e in range(2)),
    "expert_out": STREAM,
    "r_project": (("r_q_copied", 1, 1),) + each("r_kv_copied", 2),
    "r_out": STREAM,
    "w_rotate": (("w_cos", 1, 1), ("w_sin", 1, 1)),
    "w_length": (("w_inverse", 1, 1),),
    "w_value": each("w_v_copied", NT),
    "w_scores": each("w_scored", 2),
    "w_turn": (("w_turned", 1, 1),),
    "w_values": (("w_normalised", 1, 1),),
    "w_heads": (("w_heads_copied", 1, 1),),
    "w_out": STREAM,
    "w_mlp": tuple((x, HT_W, j + 1) for j in range(HT_W) for x in ("w_gelu", "w_gated")) + STREAM,
    "h_kernels": (("h_taps", 1, 1),) + each("h_spectra", 4),
    "h_project": each("h_projected", 3),
    "h_turn": (("h_turned", 1, 1),),
    "h_forward": each("h_transformed", 2),
    "h_inverse": (("h_convolved", 1, 1),),
    "h_out": STREAM,
    "leave": (("token_out_done", 1, 1),)}


def make_plan():
    plan, seen, released = [], {}, []
    state = {"tile": 0, "stream": 0, "norm": 0, "load": -1}

    def add(kind, **more):
        n = seen.get(kind, 0)
        seen[kind] = n + 1
        step = Step(kind, n, state["tile"], load=state["load"], stream=state["stream"], norm=seen.get("norm", 0) - 1,
                    shift=seen.get("shift", 0) - 1, affine=seen.get("affine", 0),
                    rotations=seen.get("w_rotate", 0), **more)
        if more.get("gain"):
            seen["affine"] = seen.get("affine", 0) + 1
        for name, a, b in LAST_READ.get(kind, ()):
            released.append((name, state["stream"] + 1 if name == "stream_done" else a * n + b))
        state["tile"] += len(LAST_READ.get(kind, ()))
        if kind in ("enter", "a_out", "a_mlp", "expert_out", "r_out", "w_out", "w_mlp", "h_out", "fold"):
            state["stream"] += 1
        plan.append(step)
        return step

    def weights():
        state["load"] += 1
        add("weights", name=LOADS[state["load"]])

    def stage_a():
        for layer in range(DEPTH_A):
            weights()
            add("norm", src="inner", via="stream" if layer else "norm", dst="normed", gain=("g1", "b1n"), table=WA)
            for i in range(C * NT + 3):
                c, w = divmod(i, NT)
                if i == 0:
                    add("a_project", c=0)
                if i < C * NT:
                    add("a_scores", c=c, w=w, i=i)
                if i == 0:
                    add("a_linear", c=0)
                if w == 3 and c + 1 < C:
                    add("a_linear", c=c + 1)
                if 1 <= i <= C * NT:
                    add("a_turn", c=(i - 1) // NT, w=(i - 1) % NT, i=i - 1)
                if 2 <= i <= C * NT + 1:
                    add("a_values", c=(i - 2) // NT, w=(i - 2) % NT, i=i - 2)
                if w == 1 and c < C:
                    add("a_context", c=c)
                if w == 2 and c + 1 < C:
                    add("a_project", c=c + 1)
                if w == 2 and 1 <= c:
                    add("a_out", c=c - 1)
            add("norm", src="inner", via="stream", dst="normed", gain=("g2", "b2n"), table=WA)
            for c in range(C):
                add("a_mlp", c=c)
        for c in range(C):
            add("fold", c=c)

    def stage_e():
        weights()
        add("norm", src="outer", via="stream", dst="normed", gain=None, table=None)
        add("gate")
        for c in range(C):
            for half in range(2):
                add("expert", c=c, half=half)
            add("expert_out", c=c)

    def stage_r(which):
        weights()
        add("norm", src="outer", via="stream", dst="normed", gain=None, table=None)
        for c in range(C):
            add("r_project", c=c, which=which)
        add("core", which=which)
        for c in range(C):
            add("r_out", c=c, which=which)

    def stage_w():
        for layer in range(DEPTH_W):
            weights()
            add("shift", via="stream" if layer else "norm")
            for c in range(C):
                order = [(x, pt) for pt in range(PAIRS) for x in ("q", "k")]
                for j in range(len(order) + 1):
                    if j < len(order):
                        add("w_rotate", c=c, x=order[j][0], pt=order[j][1])
                    if j:
                        add("w_length", c=c, x=order[j - 1][0], pt=order[j - 1][1])
                add("w_value", c=c)
                units = [(i, hp) for i in range(NT) for hp in range(PAIRS)]
                for j in range(len(units) + 4):
                    if j < len(units):
                        add("w_scores", c=c, i=units[j][0], hp=units[j][1])
                    if 1 <= j <= len(units):
                        add("w_turn", c=c, i=units[j - 1][0], hp=units[j - 1][1])
                    if 2 <= j <= len(units) + 1:
                        add("w_values", c=c, i=units[j - 2][0], hp=units[j - 2][1])
                    if 3 <= j <= len(units) + 2 and units[j - 3][1] == PAIRS - 1:
                        add("w_heads", c=c, i=units[j - 3][0])
                add("w_out", c=c)
            add("shift", via="stream")
            add("norm", src="shifted", via="shift", dst="normed", gain=("g", "b"), table=WW)
            for c in range(C):
                add("w_mlp", c=c)
        for c in range(C):
            add("fold", c=c)

    def stage_h():
        weights()
        add("h_kernels")
        add("norm", src="outer", via="stream", dst="normed", gain=None, table=None)
        for c in range(C):
            add("h_project", c=c)
        for conv in range(2):
            for c in range(C):
                add("h_turn", c=c, conv=conv)
                add("h_forward", c=c, conv=conv)
                if c:
                    add("h_inverse", c=c - 1, conv=conv)
            add("h_inverse", c=C - 1, conv=conv)
        for c in range(C):
            add("h_out", c=c)

    add("tables", which=0)
    for c in range(C):
        add("enter", c=c)
    add("norm", src="outer", via="stream", dst="inner", gain=None, table=None)
    stage_a()
    stage_e()
    stage_r(0)
    add("tables", which=1)
    stage_e()
    stage_r(1)
    add("tables", which=2)
    add("norm", src="outer", via="stream", dst="inner", gain=None, table=None)
    stage_w()
    stage_h()
    add("norm", src="outer", via="stream", dst="inner", gain=None, table=None)
    stage_w()
    for c in range(C):
        add("leave", c=c)
    return plan, released


def segments(which):
    if which == 0:
        per = GROUPS // NT
        return [(per, C, (lambda it, g, b=b: (it, per * b + g)), b + 1) for b in range(NT)]
    per = 8
    return [(per, GROUPS // per, (lambda it, g, c=c: (c, per * it + g)), NT) for c in range(C)]


def hybrid_network(nc, ins, scratch, out):
    plan, released = make_plan()
    ctx = ExitStack()
    with ctx:
        def sb(name, shape):
            return ctx.enter_context(nc.sbuf_tensor(name, shape, F32))

        sems = {}

        def sem(name):
            if name not in sems:
                sems[name] = ctx.enter_context(nc.semaphore(name))
            return sems[name]

        bank = [ctx.enter_context(nc.psum_tensor(f"bank{b}", [P, T], F32)) for b in range(BANKS)]
        tile_full = sem("tile_full")

        outer = sb("outer", [P, C, T])
        inner = sb("inner", [P, C, T])
        normed = sb("normed", [P, C, T])
        centered = sb("centered", [P, C, T])
        squared = sb("squared", [P, C, T])
        shifted = sb("shifted", [P, C, T])
        const = sb("const", [P, CONST_W])
        slots = [sb(f"slot{s}", [P, SLOT]) for s in range(2)]
        table = sb("table", [P, 8192])
        work = sb("work", [P, 18700])
        streams = {"outer": outer, "inner": inner, "normed": normed, "shifted": shifted}
        ET8 = sb("embk_rows", [D_R, 2 * T])

        cursor = [0]

        def carve(*shape):
            size = 1
            for s in shape:
                size *= s
            a = work[:, cursor[0]:cursor[0] + size]
            cursor[0] += size
            assert cursor[0] <= 18700, cursor[0]
            if len(shape) == 1:
                return a
            names = "abcd"[:len(shape)]
            return a.rearrange(f"p ({' '.join(names)}) -> p {' '.join(names)}",
                               **{n: s for n, s in zip(names[1:], shape[1:])})

        KL = carve(2, T)
        TM = carve(2, NT, 260)
        EB, EE = carve(NT, 128), carve(NT, 128)
        QN, KF = carve(NT, 64), carve(NT, 64)
        QT = carve(T)
        CN = carve(NB_A, 64)
        SA, PA = carve(2, LOC, 256), carve(2, LOC, 256)
        TA = carve(2, 2, T)
        ON = carve(2, NT, P)
        AT = carve(T)
        small_a = carve(16, 16)
        qmax, qsum = carve(16), carve(16)
        kcum = carve(8)
        cursor[0] = max(cursor[0], 8192)
        QL = carve(2, LOC, T)
        HB = work[:, 0:8192].rearrange("p (a b c) -> p a b c", a=4, b=4)
        CN0 = CN
        cursor[0] = 0
        GL, GE, GG = carve(16, 8), carve(16, 8), carve(16, 8)
        CMP, CEQ = carve(16, 64), carve(16, 64)
        gmax, gsum, gsum2 = carve(16), carve(16), carve(16)
        rank = carve(16, 8)
        GS = carve(16, 8)
        GST = carve(C * T)
        ACC = carve(2, NT, P)
        cursor[0] = 0
        QR, KR, VR = carve(C, T), carve(C, T), carve(C, T)
        A4, B4 = carve(2, T), carve(2, T)
        PR, PTR = carve(2, T), carve(2, T)
        O2M, W2, TZ, ZR = carve(2, 64), carve(2, 8), carve(2, P), carve(2, P)
        NBR, RSR, RIR = carve(4), carve(8), carve(8)
        AX4, Z2 = carve(2, T), carve(2, 32)
        position_heads = shifted
        key_table = table[:, 0:ET_W]
        value_table = table[:, 1024:1024 + EV_W * D_R]
        cursor[0] = 0
        QW, KW = carve(2, PAIRS, T), carve(PAIRS, T)
        VW = carve(NT, T)
        R1, R2 = carve(2, T), carve(2, T)
        SW, PW = carve(2, 2, 256), carve(2, 2, 256)
        TW = carve(2, T)
        OW = carve(2, T)
        AW = carve(PAIRS, T)
        small_w = carve(4, 8)
        HW = work[:, 0:HT_W * T * 2].rearrange("p (a b c) -> p a b c", a=2, b=HT_W)
        GW = work[:, 2 * HT_W * T:4 * HT_W * T].rearrange("p (a b c) -> p a b c", a=2, b=HT_W)
        SQW = centered
        RNW = squared
        rotary = table[:, 6144:8192].rearrange("p (a t) -> p a t", a=4)
        cursor[0] = 0
        QH, KH, VH = carve(C, T), carve(C, T), carve(C, T)
        KTH = carve(2, NT, P)
        XH = carve(2, 2, DFT)
        M1, M2, YH = carve(2, 2, DFT), carve(2, 2, DFT), carve(2, 2, DFT)
        SPEC = carve(2, 2, DFT)
        KNT = carve(2, T)
        forward_dft = table[:, 0:NT * 2 * DFT].rearrange("p (a f) -> p a f", a=NT)
        inverse_dft = table[:, NT * 2 * DFT:NT * 2 * DFT + 2 * FT * T].rearrange("p (a t) -> p a t", a=2 * FT)
        token_io = squared[:, :, :].rearrange("p c (a f) -> p c a f", a=NT)
        token_out = centered[:, :, :].rearrange("p c (a f) -> p c a f", a=NT)

        def k_(name):
            a, w = CONST[name]
            return const[:, a:a + w]

        ident = k_("ident")
        eps_col = k_("eps")

        def wt(step, table_, name, lo=0, width=None):
            a, w = table_[name]
            s = slots[step.load % 2]
            return s[:, a + lo:a + lo + (w if width is None else width)]

        def bc(ap, shape):
            return ap.broadcast_to(shape)

        def tile_of(k):
            return bank[k % BANKS]

        block = ctx.enter_context(nc.Block())

        def source_ready(eng, s, c):
            if s.via == "shift":
                eng.wait_ge(sem("shift_done"), C * s.shift + c + 1)
            elif s.via == "norm":
                eng.wait_ge(sem("norm_done"), C * (s.norm - (s.kind == "norm")) + c + 1)
            else:
                eng.wait_ge(sem("stream_done"), s.stream - C + c + 1)

        def reached(eng, name, count):
            if not isinstance(count, int) or count > 0:
                eng.wait_ge(sem(name), count)

        def core_steps(eng, which):
            start, before = C * GROUPS * which, None
            for per, rounds, place, nk in segments(which):
                def group(it, g, start=start, per=per, place=place, nk=nk):
                    return start + it * per + g, g, start // 4 + it * (per // 4) + g // 4, place(it, g), nk

                def at(it, g, lag, before=before, per=per, group=group):
                    if g >= lag:
                        return group(it, g - lag)
                    if not isinstance(it, int) or it > 0:
                        return group(it - 1, per + g - lag)
                    return before(g - lag) if before else None

                def st_of(it, g, at=at):
                    def st(work_, lag):
                        d = at(it, g, lag)
                        if d is not None:
                            work_(*d)
                    return st

                for g in range(per):
                    yield st_of(0, g)
                with eng.Fori(1, rounds) as it:
                    for g in range(per):
                        yield st_of(it, g)
                before = lambda back, group=group, rounds=rounds, per=per: group(rounds - 1, per + back)
                start += per * rounds
            for g in range(4):
                def st(work_, lag, g=g):
                    if g < lag:
                        work_(*before(g - lag))
                yield st

        def weights_here(eng, s):
            eng.wait_ge(sem(f"slot{s.load % 2}_loaded"), 16 * (s.load // 2 + 1))

        @block.sync
        def _(sp):
            stage_ends = {}
            for s in plan:
                if s.load >= 0 and s.kind not in ("weights", "tables"):
                    stage_ends[s.load] = s.stream + (s.kind in ("fold", "a_mlp", "expert_out", "r_out", "w_mlp", "h_out"))

            def tables(s):
                if s.which < 2:
                    w = s.which
                    if w == 1:
                        sp.wait_ge(sem("r_head_copied"), CHUNKS)
                        sp.wait_ge(sem("key_table"), 16 * (QG + 1))
                    rows = ins["embk"][w].shape[1]
                    lo = T - rows if w == 0 else T - 1 - P
                    sp.dma_start(ET8[0:D_R, lo:lo + rows], ins["embk"][w]).then_inc(sem("embk_loaded"), 16)
                    padded = scratch[w]
                    embv = ins["embv"][w]
                    first = lo
                    sp.dma_start(padded[0:first, :], bc(embv[0:1, :], [first, D_R])).then_inc(sem("embv_padded"), 16)
                    sp.dma_start(padded[first:first + rows, :], embv).then_inc(sem("embv_padded"), 16)
                    last = 2 * T - 1 - first - rows
                    sp.dma_start(padded[first + rows:2 * T - 1, :], bc(embv[rows - 1:rows, :], [last, D_R]))\
                        .then_inc(sem("embv_padded"), 16)
                    sp.wait_ge(sem("embk_widened"), 2 * w + 2)
                    for j in range(QG):
                        sp.dma_start(key_table[D_R * j:D_R * j + D_R, :],
                                     ET8[0:D_R, QG - 1 - j:QG - 1 - j + ET_W]).then_inc(sem("key_table"), 16)
                    sp.dma_start(key_table[D_R * QG:P, :], ins["causal"][w]).then_inc(sem("key_table"), 16)
                    sp.wait_ge(sem("embv_padded"), 48 * (w + 1))
                    sp.dma_start(value_table, bass.AP(padded.tensor, 0, [[D_R, P], [1, EV_W * D_R]]))\
                        .then_inc(sem("value_table"), 16)
                else:
                    sp.wait_ge(sem("r_head_copied"), 2 * CHUNKS)
                    sp.dma_start(table[:, 6144:8192], ins["rotary"]).then_inc(sem("rotary_loaded"), 16)
                    sp.dma_start(table[:, 0:6144], ins["dft"]).then_inc(sem("dft_loaded"), 16)

            def weights(s):
                if s.load >= 2:
                    sp.wait_ge(sem("stream_done"), stage_ends[s.load - 2])
                src = ins["w" + s.name]
                sp.dma_start(slots[s.load % 2][:, 0:src.shape[1]], src).then_inc(sem(f"slot{s.load % 2}_loaded"), 16)

            def enter(s):
                x = ins["x"][s.c].rearrange("(a p) f -> p a f", p=P)
                sp.dma_start(token_io[:, s.c], x).then_inc(sem(f"x_loaded{s.c}"), 16)

            def leave(s):
                sp.wait_ge(sem("token_out_done"), s.n + 1)
                sp.dma_start(out[s.c].rearrange("(a p) f -> p a f", p=P), token_out[:, s.c])\
                    .then_inc(sem("out_written"), 16)

            sp.dma_start(const[:, :], ins["const"]).then_inc(sem("const_loaded"), 16)
            order = [s for s in plan if s.kind == "enter"] + [s for s in plan if s.kind == "weights"][:2]
            order += [s for s in plan if s.kind in ("weights", "tables", "leave") and s not in order]
            for s in order:
                {"tables": tables, "weights": weights, "enter": enter, "leave": leave}[s.kind](s)
            sp.wait_ge(sem("out_written"), 16 * C)

        @block.tensor
        def _(pe):
            def take(k):
                if k >= BANKS:
                    name, count = released[k - BANKS]
                    pe.wait_ge(sem(name), count)
                return tile_of(k)

            def mm(o, l, r, start=True, stop=True):
                return pe.matmul(o, l, r, start=start, stop=stop)

            def enter(s):
                pe.wait_ge(sem(f"x_loaded{s.c}"), 16)
                o = take(s.k)
                for a in range(NT):
                    last = pe.transpose(o[:, a * P:(a + 1) * P], token_io[:, s.c, a, :], ident)
                last.then_inc(tile_full, 1)

            def leave(s):
                pe.wait_ge(sem("stream_done"), s.stream - C + s.c + 1)
                o = take(s.k)
                for a in range(NT):
                    last = pe.transpose(o[:, a * P:(a + 1) * P], outer[:, s.c, a * P:(a + 1) * P], ident)
                last.then_inc(tile_full, 1)

            def norm(s):
                src = streams[s.src]
                for c in range(C):
                    source_ready(pe, s, c)
                    mm(take(s.k + c)[:, :], k_("mean"), src[:, c, :]).then_inc(tile_full, 1)
                for c in range(C):
                    pe.wait_ge(sem("norm_squared"), C * s.n + c + 1)
                    mm(take(s.k + C + c)[:, :], k_("mean"), squared[:, c, :]).then_inc(tile_full, 1)

            def a_project(s):
                pe.wait_ge(sem("norm_done"), C * s.norm + s.c + 1)
                y = normed[:, s.c, :]
                mm(take(s.k)[:, :], wt(s, WA, "q_loc"), y).then_inc(tile_full, 1)
                mm(take(s.k + 1)[:, :], wt(s, WA, "k_loc"), y).then_inc(tile_full, 1)
                for half in range(2):
                    o = take(s.k + 2 + half)
                    for a in range(2):
                        tt = 2 * half + a
                        last = mm(o[:, a * 256:(a + 1) * 256], y[:, tt * P:(tt + 1) * P], wt(s, WA, "qkv"))
                    last.then_inc(tile_full, 1)

            def a_context(s):
                b = s.c % 2
                pe.wait_ge(sem("a_linear_q"), s.n + 1)
                o = take(s.k)
                for a in range(NT):
                    last = pe.transpose(o[0:64, a * P:(a + 1) * P], QN[:, a, :], ident)
                last.then_inc(tile_full, 1)
                pe.wait_ge(sem("a_linear_k"), s.n + 1)
                o = take(s.k + 1)
                for u in range(1, NB_A):
                    dst = o[0:64, (u - 1) * 65:u * 65]
                    for a in range(u // 2):
                        last = mm(dst, KF[:, a, :], TM[:, b, a, 192:257], start=(a == 0), stop=(a == u // 2 - 1 and u % 2 == 0))
                    if u % 2:
                        a = u // 2
                        last = mm(dst, KF[0:64, a, :], TM[0:64, b, a, 192:257], start=(a == 0), stop=True)
                last.then_inc(tile_full, 1)

            def a_scores(s):
                b = s.c % 2
                pe.wait_ge(sem("a_local_copied"), (LOC + 1) * (s.n // NT + 1))
                lo = 0 if s.w else P
                for h in range(LOC):
                    mm(take(s.k + h)[:, lo:256], QL[:, b, h, s.w * P:(s.w + 1) * P],
                       KL[:, b, (s.w - 1) * P + lo:(s.w + 1) * P]).then_inc(tile_full, 1)

            def a_turn(s):
                i = s.i % 2
                pe.wait_ge(sem("a_exp"), s.n + 1)
                for half in range(2):
                    o = take(s.k + half)
                    for a in range(2):
                        for blk in range(0 if s.w else 1, 2):
                            last = pe.transpose(o[:, (2 * a + blk) * P:(2 * a + blk + 1) * P],
                                                PA[:, i, 2 * half + a, blk * P:(blk + 1) * P], ident)
                    last.then_inc(tile_full, 1)

            def a_values(s):
                i, b = s.i % 2, s.c % 2
                pe.wait_ge(sem("a_turned_act"), s.n + 1)
                pe.wait_ge(sem("a_turned_dve"), s.n + 1)
                o = take(s.k)
                for h in range(LOC):
                    for blk in range(0 if s.w else 1, 2):
                        mm(o[:, h * DH_A:(h + 1) * DH_A],
                           TA[:, i, h // 2, (2 * (h % 2) + blk) * P:(2 * (h % 2) + blk + 1) * P],
                           TM[:, b, s.w - 1 + blk, P + h * DH_A:P + (h + 1) * DH_A],
                           start=(blk == (0 if s.w else 1)), stop=(blk == 1))
                pe.wait_ge(sem("a_context_done"), s.n // NT + 1)
                pe.wait_ge(sem("a_q_turned"), s.n // NT + 1)
                for e in range(2):
                    u = 2 * s.w + e
                    last = mm(o[64 * e:64 * e + 64, 64:128], QT[0:64, u * 64:(u + 1) * 64], CN[0:64, u, :])
                last.then_inc(tile_full, 1)

            def a_out(s):
                b = s.c % 2
                pe.wait_ge(sem("a_normalised"), NT * (s.n + 1))
                o = take(s.k)
                for w in range(NT):
                    last = pe.transpose(o[:, w * P:(w + 1) * P], ON[:, b, w, :], ident)
                last.then_inc(tile_full, 1)
                pe.wait_ge(sem("a_heads"), s.n + 1)
                mm(take(s.k + 1)[:, :], wt(s, WA, "o"), AT).then_inc(tile_full, 1)

            def a_mlp(s):
                pe.wait_ge(sem("norm_done"), C * s.norm + s.c + 1)
                for j in range(4):
                    mm(take(s.k + j)[:, :], wt(s, WA, "w1", j * P, P), normed[:, s.c, :]).then_inc(tile_full, 1)
                o = take(s.k + 4)
                for j in range(4):
                    pe.wait_ge(sem("a_gelu"), 4 * s.n + j + 1)
                    last = mm(o[:, :], wt(s, WA, "w2", j * P, P), HB[:, s.c, j, :], start=(j == 0), stop=(j == 3))
                last.then_inc(tile_full, 1)

            def gate(s):
                o = take(s.k)
                for c in range(C):
                    pe.wait_ge(sem("norm_done"), C * s.norm + c + 1)
                    for a in range(NT):
                        dst = o[:, (c * NT + a) * 8:(c * NT + a + 1) * 8]
                        mm(dst, normed[:, c, a * P:(a + 1) * P], wt(s, WE, "gate"), stop=False)
                        last = mm(dst, k_("ones")[0:1, :], wt(s, WE, "bg")[0:1, :], start=False)
                last.then_inc(tile_full, 1)
                pe.wait_ge(sem("gate_done"), s.n + 1)
                for c in range(C):
                    o = take(s.k + 1 + c)
                    for a in range(NT):
                        last = pe.transpose(o[0:8, a * P:(a + 1) * P], GS[:, c * NT + a, :], ident)
                    last.then_inc(tile_full, 1)

            def expert(s):
                for a in range(2):
                    y = normed[:, s.c, (2 * s.half + a) * P:(2 * s.half + a + 1) * P]
                    for e in range(2):
                        mm(take(s.k + 2 * a + e)[:, :], y, wt(s, WE, "experts", e * T, T)).then_inc(tile_full, 1)

            def expert_out(s):
                o = take(s.k)
                pe.wait_ge(sem("gate_turned"), s.n + 1)
                mm(o[:, :], wt(s, WE, "be"), GST[:, s.c * T:(s.c + 1) * T], stop=False)
                pe.wait_ge(sem("expert_scaled"), 16 * 2 * (s.n + 1))
                for a in range(NT):
                    last = mm(o[:, a * P:(a + 1) * P], ACC[:, s.c % 2, a, :], ident, start=False, stop=(a == NT - 1))
                last.then_inc(tile_full, 1)

            def r_project(s):
                pe.wait_ge(sem("norm_done"), C * s.norm + s.c + 1)
                y = normed[:, s.c, :]
                mm(take(s.k)[:, :], wt(s, WR, "q"), y).then_inc(tile_full, 1)
                mm(take(s.k + 1)[:, :], wt(s, WR, "k"), y).then_inc(tile_full, 1)
                o = take(s.k + 2)
                for a in range(NT):
                    last = mm(o[:, a * P:(a + 1) * P], y[:, a * P:(a + 1) * P], wt(s, WR, "v"))
                last.then_inc(tile_full, 1)

            def core(s):
                for name, count in released[s.k - BANKS:s.k]:
                    pe.wait_ge(sem(name), count)
                pe.wait_ge(sem("r_q_copied"), C * (s.which + 1))
                pe.wait_ge(sem("r_kv_copied"), 2 * C * (s.which + 1))
                pe.wait_ge(sem("key_table"), 16 * (QG + 1) * (s.which + 1))
                pe.wait_ge(sem("value_table"), 16 * (s.which + 1))
                keys_flat = KR.rearrange("p a b -> p (a b)")
                values_flat = VR.rearrange("p a b -> p (a b)")

                def turn(G, g, Q, at, nk):
                    pe.wait_ge(sem("r_exp"), G + 1)
                    for b in range(nk):
                        last = pe.transpose(bank[2 + g % 2][:, b * P:(b + 1) * P], PR[:, g % 2, b * P:(b + 1) * P], ident)
                    last.then_inc(sem("r_turned"), 1)

                def values(G, g, Q, at, nk):
                    lane, tg = at
                    pe.wait_ge(sem("r_turn_copied"), G + 1)
                    reached(pe, "r_weighted", G - 1)
                    o = bank[4 + g % 2]
                    for b in range(nk):
                        mm(o[:, 0:P], PTR[:, g % 2, b * P:(b + 1) * P], values_flat[:, bass.ds(lane * T + b * P, P)],
                           start=(b == 0), stop=(b == nk - 1))
                    for b in range(nk):
                        last = mm(o[:, P:P + QG * D_R], PTR[:, g % 2, b * P:(b + 1) * P],
                                  value_table[:, bass.ds((T - QG + P * b) * D_R - tg * (QG * D_R), QG * D_R)],
                                  start=(b == 0), stop=(b == nk - 1))
                    last.then_inc(sem("r_values"), 1)

                def spread(G, g, Q, at, nk):
                    if g % 4 == 0:
                        pe.wait_ge(sem("r_spread"), Q + 1)
                        if s.which:
                            pe.wait_ge(sem("r_keys_spread"), Q + 1 - CHUNKS)
                        rows_ = A4 if s.which == 0 else AX4
                        mm(bank[6][0:QG * D_R, :], k_("repeat"), rows_[:, (g // 4) % 2, :]).then_inc(sem("r_repeated"), 1)

                def keys(G, g, Q, at, nk):
                    reached(pe, "r_exp", G - 1)
                    mm(bank[g % 2][:, 0:nk * P], A4[:, (g // 4) % 2, (g % 4) * P:(g % 4 + 1) * P],
                       keys_flat[:, bass.ds(at[0] * T, nk * P)], stop=False)

                def shifts(G, g, Q, at, nk):
                    pe.wait_ge(sem("r_diagonal"), Q + 1)
                    mm(bank[g % 2][:, 0:nk * P], B4[:, (g // 4) % 2, (g % 4) * P:(g % 4 + 1) * P],
                       key_table[:, bass.ds((T - QG) - at[1] * QG, nk * P)], start=False).then_inc(sem("r_scores"), 1)

                def heads(G, g, Q, at, nk):
                    pe.wait_ge(sem("r_masked"), G + 1)
                    if g % 4 == 0:
                        reached(pe, "r_head_copied", Q)
                    last = mm(bank[7][:, (g % 4) * QG:(g % 4 + 1) * QG], ZR[:, g % 2, :], k_("pick_query"))
                    if s.which:
                        last = mm(bank[7][32 * at[0]:32 * at[0] + 32, P + 32 * (g % 4):P + 32 * (g % 4) + 32],
                                  Z2[:, g % 2, :], k_("pick_pair"))
                    last.then_inc(sem("r_heads"), 1)

                for st in core_steps(pe, s.which):
                    st(turn, 2)
                    st(values, 3)
                    st(spread, 0)
                    st(keys, 0)
                    st(heads, 4)
                    st(shifts, 0)
                pe.wait_ge(sem("r_head_copied"), CHUNKS * (s.which + 1))

            def r_out(s):
                pe.wait_ge(sem("r_head_copied"), CHUNKS * (s.which + 1))
                o = take(s.k)[:, :]
                last = mm(o, wt(s, WR, "o"), centered[:, s.c, :], stop=not s.which)
                if s.which:
                    last = mm(o, wt(s, WR, "o"), position_heads[:, s.c, :], start=False)
                last.then_inc(tile_full, 1)

            def w_rotate(s):
                pe.wait_ge(sem("shift_done"), C * s.shift + s.c + 1)
                h = shifted[:, s.c, :]
                mm(take(s.k)[:, :], wt(s, WW, s.x, s.pt * P, P), h).then_inc(tile_full, 1)
                mm(take(s.k + 1)[:, :], wt(s, WW, s.x + "_rot", s.pt * P, P), h).then_inc(tile_full, 1)

            def w_length(s):
                pe.wait_ge(sem("w_squared"), s.n + 1)
                mm(take(s.k)[:, :], k_("pair_ones"), SQW[:, s.n % 4, :]).then_inc(tile_full, 1)

            def w_value(s):
                for a in range(NT):
                    mm(take(s.k + a)[:, :], shifted[:, s.c, a * P:(a + 1) * P], wt(s, WW, "v")).then_inc(tile_full, 1)

            def w_scores(s):
                pe.wait_ge(sem("w_scaled"), 8 * (s.n // 16 + 1))
                lo = 0 if s.i else WIN
                for a in range(2):
                    mm(take(s.k + a)[:, WIN + lo:256], QW[:, a, s.hp, s.i * P:(s.i + 1) * P],
                       KW[:, s.hp, s.i * P - WIN + lo:(s.i + 1) * P]).then_inc(tile_full, 1)

            def w_turn(s):
                pe.wait_ge(sem("w_exp"), s.n + 1)
                o = take(s.k)
                for a in range(2):
                    for blk in range(0 if s.i else 1, 2):
                        last = pe.transpose(o[:, (2 * a + blk) * P:(2 * a + blk + 1) * P],
                                            PW[:, s.n % 2, a, blk * P:(blk + 1) * P], ident)
                last.then_inc(tile_full, 1)

            def w_values(s):
                if s.i == 0 and s.hp == 0:
                    pe.wait_ge(sem("w_v_copied"), NT * (s.n // 16 + 1))
                pe.wait_ge(sem("w_turned"), s.n + 1)
                o = take(s.k)
                for a in range(2):
                    h = 2 * s.hp + a
                    for blk in range(0 if s.i else 1, 2):
                        last = mm(o[:, a * 64:(a + 1) * 64], TW[:, s.n % 2, (2 * a + blk) * P:(2 * a + blk + 1) * P],
                                  VW[:, s.i - 1 + blk, h * 64:(h + 1) * 64], start=(blk == (0 if s.i else 1)), stop=(blk == 1))
                last.then_inc(tile_full, 1)

            def w_heads(s):
                pe.wait_ge(sem("w_normalised"), PAIRS * (s.n + 1))
                o = take(s.k)
                for pt in range(PAIRS):
                    last = pe.transpose(o[:, pt * P:(pt + 1) * P], OW[:, s.i % 2, pt * P:(pt + 1) * P], ident)
                last.then_inc(tile_full, 1)

            def w_out(s):
                pe.wait_ge(sem("w_heads_copied"), NT * (s.n + 1))
                o = take(s.k)
                for pt in range(PAIRS):
                    last = mm(o[:, :], wt(s, WW, "o", pt * P, P), AW[:, pt, :], start=(pt == 0), stop=(pt == PAIRS - 1))
                last.then_inc(tile_full, 1)

            def w_mlp(s):
                pe.wait_ge(sem("norm_done"), C * s.norm + s.c + 1)
                for j in range(HT_W):
                    mm(take(s.k + 2 * j)[:, :], wt(s, WW, "w1g", j * P, P), normed[:, s.c, :]).then_inc(tile_full, 1)
                    mm(take(s.k + 2 * j + 1)[:, :], wt(s, WW, "w1a", j * P, P), normed[:, s.c, :]).then_inc(tile_full, 1)
                o = take(s.k + 2 * HT_W)
                for j in range(HT_W):
                    pe.wait_ge(sem("w_gated"), HT_W * s.n + j + 1)
                    last = mm(o[:, :], wt(s, WW, "w2", j * P, P), HW[:, s.n % 2, j, :], start=(j == 0), stop=(j == HT_W - 1))
                last.then_inc(tile_full, 1)

            def h_kernels(s):
                o = take(s.k)
                for a in range(4):
                    last = pe.transpose(o[:, a * P:(a + 1) * P], wt(s, WH, "kernels", a * P, P), ident)
                last.then_inc(tile_full, 1)
                pe.wait_ge(sem("h_taps"), 1)
                pe.wait_ge(sem("dft_loaded"), 16)
                for v in range(2):
                    for part in range(2):
                        o = take(s.k + 1 + 2 * v + part)
                        for f in range(FT):
                            for a in range(2):
                                last = mm(o[:, f * P:(f + 1) * P],
                                          forward_dft[:, a, part * DFT + f * P:part * DFT + (f + 1) * P],
                                          KNT[:, v, a * P:(a + 1) * P], start=(a == 0), stop=(a == 1))
                        last.then_inc(tile_full, 1)

            def h_project(s):
                pe.wait_ge(sem("norm_done"), C * s.norm + s.c + 1)
                for j, x in enumerate("kvq"):
                    mm(take(s.k + j)[:, :], wt(s, WH, x), normed[:, s.c, :]).then_inc(tile_full, 1)

            def h_turn(s):
                if s.conv == 0:
                    pe.wait_ge(sem("h_projected"), 3 * (s.c + 1))
                else:
                    pe.wait_ge(sem("h_kv"), s.c + 1)
                o = take(s.k)
                for a in range(NT):
                    last = pe.transpose(o[:, a * P:(a + 1) * P], KH[:, s.c, a * P:(a + 1) * P], ident)
                last.then_inc(tile_full, 1)

            def h_forward(s):
                pe.wait_ge(sem("h_turned"), s.n + 1)
                for part in range(2):
                    o = take(s.k + part)
                    for f in range(FT):
                        for a in range(NT):
                            last = mm(o[:, f * P:(f + 1) * P],
                                      forward_dft[:, a, part * DFT + f * P:part * DFT + (f + 1) * P],
                                      KTH[:, s.n % 2, a, :], start=(a == 0), stop=(a == NT - 1))
                    last.then_inc(tile_full, 1)

            def h_inverse(s):
                pe.wait_ge(sem("h_product"), 2 * (s.n + 1))
                o = take(s.k)
                for f in range(2 * FT):
                    last = mm(o[:, :], YH[:, s.n % 2, f // FT, (f % FT) * P:(f % FT + 1) * P], inverse_dft[:, f, :],
                              start=(f == 0), stop=(f == 2 * FT - 1))
                last.then_inc(tile_full, 1)

            def h_out(s):
                pe.wait_ge(sem("h_gated"), s.c + 1)
                mm(take(s.k)[:, :], wt(s, WH, "o"), VH[:, s.c, :]).then_inc(tile_full, 1)

            parts = dict(weights=lambda s: weights_here(pe, s), enter=enter, leave=leave, norm=norm, a_project=a_project, a_context=a_context,
                         a_scores=a_scores, a_turn=a_turn, a_values=a_values, a_out=a_out, a_mlp=a_mlp, gate=gate,
                         expert=expert, expert_out=expert_out, r_project=r_project, core=core, r_out=r_out,
                         w_rotate=w_rotate, w_length=w_length, w_value=w_value, w_scores=w_scores, w_turn=w_turn,
                         w_values=w_values, w_heads=w_heads, w_out=w_out, w_mlp=w_mlp, h_kernels=h_kernels,
                         h_project=h_project, h_turn=h_turn, h_forward=h_forward, h_inverse=h_inverse, h_out=h_out)
            pe.wait_ge(sem("const_loaded"), 16)
            for s in plan:
                if s.kind in parts:
                    parts[s.kind](s)

        @block.scalar
        def _(act):
            def full(k):
                act.wait_ge(tile_full, k + 1)
                return tile_of(k)

            def copy(dst, src):
                return act.activation(dst, src, ACT.Identity)

            def norm(s):
                for c in range(C):
                    act.wait_ge(sem("norm_centered"), C * s.n + c + 1)
                    act.activation(squared[:, c, :], centered[:, c, :], ACT.Square).then_inc(sem("norm_squared"), 1)
                for c in range(C):
                    k = s.k + C + c
                    ln = act.activation(full(k)[:, :], full(k)[:, :], ACT.Ln, bias=eps_col[:, 0:1])
                    ln.then_inc(sem("norm_log"), 1)
                for c in range(C):
                    k = s.k + C + c
                    act.wait_ge(sem("norm_log"), C * s.n + c + 1)
                    act.activation(squared[:, c, :], tile_of(k)[:, :], ACT.Exp, scale=-0.5)\
                        .then_inc(sem("norm_rstd"), 1)

            def a_project(s):
                b = s.c % 2
                if s.n == 0:
                    act.wait_ge(sem("a_q_cleared"), 1)
                for h in range(LOC):
                    r = slice(32 * h, 32 * h + DH_A)
                    copy(QL[r, b, h, :], full(s.k)[r, :]).then_inc(sem("a_local_copied"), 1)
                copy(KL[:, b, :], full(s.k + 1)[:, :]).then_inc(sem("a_local_copied"), 1)
                act.wait_ge(sem("a_shifted"), s.n + 1)
                act.activation(EE[:, :, :], EB[:, :, :], ACT.Exp).then_inc(sem("a_linear_exp"), 1)

            def a_context(s):
                copy(QT[0:64, :], full(s.k)[0:64, :]).then_inc(sem("a_q_turned"), 1)

            def a_scores(s):
                i, lo = s.i % 2, (0 if s.w else P)
                for h in range(LOC):
                    act.wait_ge(sem("a_scored"), LOC * s.n + h + 1)
                    last = act.activation(PA[:, i, h, lo:256], SA[:, i, h, lo:256], ACT.Exp, scale=-1.0,
                                          bias=small_a[:, s.i % 4, h:h + 1], accum_out=small_a[:, 4 + s.i % 4, h:h + 1])
                last.then_inc(sem("a_exp"), 1)

            def a_turn(s):
                i = s.i % 2
                src, dst = full(s.k), TA[:, i, 0, :]
                if s.w:
                    copy(dst, src[:, :]).then_inc(sem("a_turned_act"), 1)
                else:
                    copy(dst.rearrange("p (a b t) -> p a b t", a=2, b=2)[:, :, 1, :],
                         src[:, :].rearrange("p (a b t) -> p a b t", a=2, b=2)[:, :, 1, :]).then_inc(sem("a_turned_act"), 1)

            def a_out(s):
                copy(AT, full(s.k)[:, :]).then_inc(sem("a_heads"), 1)

            def a_mlp(s):
                for j in range(4):
                    act.activation(HB[:, s.c, j, :], full(s.k + j)[:, :], ACT.Gelu, bias=wt(s, WA, "b1", j, 1))\
                        .then_inc(sem("a_gelu"), 1)
                if s.c == C - 1:
                    act.preload_act_table_set("natural_log_exp_and_others")

            def gate(s):
                act.wait_ge(sem("gate_shifted"), s.n + 1)
                act.activation(GE, GL, ACT.Exp).then_inc(sem("gate_exp"), 1)
                for c in range(C):
                    copy(GST[0:8, c * T:(c + 1) * T], full(s.k + 1 + c)[0:8, :]).then_inc(sem("gate_turned"), 1)

            def r_project(s):
                act.wait_ge(tile_full, s.k + 2)
                if s.which == 0:
                    act.activation(KR[:, s.c, :], tile_of(s.k + 1)[:, :], ACT.Identity, scale=float(D_R) ** -0.5)\
                        .then_inc(sem("r_kv_copied"), 1)
                else:
                    act.activation(KR[:, s.c, :], tile_of(s.k + 1)[:, :], ACT.Identity, bias=wt(s, WR, "bk"))\
                        .then_inc(sem("r_kv_copied"), 1)
                copy(VR[:, s.c, :], full(s.k + 2)[:, :]).then_inc(sem("r_kv_copied"), 1)

            def core(s):
                def turned(G, g, Q, at, nk):
                    act.wait_ge(sem("r_turned"), G + 1)
                    copy(PTR[:, g % 2, 0:nk * P], bank[2 + g % 2][:, 0:nk * P]).then_inc(sem("r_turn_copied"), 1)

                def exps(G, g, Q, at, nk):
                    act.wait_ge(sem("r_max"), G + 1)
                    act.activation(PR[:, g % 2, 0:nk * P], bank[g % 2][:, 0:nk * P], ACT.Exp, bias=NBR[:, g % 4:g % 4 + 1],
                                   accum_out=RSR[:, g % 8:g % 8 + 1]).then_inc(sem("r_exp"), 1)

                for st in core_steps(act, s.which):
                    st(turned, 2)
                    st(exps, 0)

            def w_rotate(s):
                if s.c == 0 and s.pt == 0 and s.x == "q":
                    act.wait_ge(sem("norm_done"), C * (s.norm + 1))
                act.wait_ge(tile_full, s.k + 1)
                act.activation(SQW[:, s.n % 4, :], tile_of(s.k)[:, :], ACT.Square).then_inc(sem("w_squared"), 1)

            def w_length(s):
                act.wait_ge(tile_full, s.k + 1)
                act.activation(tile_of(s.k)[:, :], tile_of(s.k)[:, :], ACT.Ln, bias=eps_col[:, 1:2], scale=2.0 ** 30)\
                    .then_inc(sem("w_log"), 1)
                act.wait_ge(sem("w_log"), s.n + 1)
                if s.n >= 4:
                    act.wait_ge(sem("w_scaled"), s.n - 3)
                act.activation(RNW[:, s.n % 4, :], tile_of(s.k)[:, :], ACT.Exp, bias=eps_col[:, 2:3], scale=-0.5)\
                    .then_inc(sem("w_inverse"), 1)

            def w_value(s):
                for a in range(NT):
                    copy(VW[:, a, :], full(s.k + a)[:, :]).then_inc(sem("w_v_copied"), 1)

            def w_scores(s):
                lo = 64 if s.i else P
                for a in range(2):
                    act.wait_ge(sem("w_scored"), 2 * s.n + a + 1)
                    last = act.activation(PW[:, s.n % 2, a, lo:256], SW[:, s.n % 2, a, lo:256], ACT.Exp, scale=-1.0,
                                          bias=small_w[:, s.n % 4, a:a + 1], accum_out=small_w[:, s.n % 4, 2 + a:3 + a])
                last.then_inc(sem("w_exp"), 1)

            def w_turn(s):
                if s.n % 2 == 0:
                    return
                act.wait_ge(tile_full, s.k + 1)
                act.wait_ge(sem("w_turned"), s.n)
                v = "p (a b t) -> p a b t"
                lo = 0 if s.i else 1
                copy(TW[:, s.n % 2, :].rearrange(v, a=2, b=2)[:, :, lo:2, :], tile_of(s.k)[:, :].rearrange(v, a=2, b=2)[:, :, lo:2, :])\
                    .then_inc(sem("w_turned"), 1)

            def w_heads(s):
                copy(AW[:, :, s.i * P:(s.i + 1) * P], full(s.k)[:, :].rearrange("p (a t) -> p a t", a=PAIRS))\
                    .then_inc(sem("w_heads_copied"), 1)

            def w_mlp(s):
                for j in range(HT_W):
                    act.activation(GW[:, s.n % 2, j, :], full(s.k + 2 * j)[:, :], ACT.Gelu, bias=wt(s, WW, "b1g", j, 1))\
                        .then_inc(sem("w_gelu"), 1)
                if s.c == C - 1:
                    act.preload_act_table_set("natural_log_exp_and_others")

            def h_kernels(s):
                act.wait_ge(tile_full, s.k + 1)
                copy(KNT[:, :, 0:TAPS], tile_of(s.k)[:, :].rearrange("p (a t) -> p a t", a=2)).then_inc(sem("h_taps"), 1)
                for v in range(2):
                    for part in range(2):
                        copy(SPEC[:, v, part, :], full(s.k + 1 + 2 * v + part)[:, 0:DFT]).then_inc(sem("h_spectra"), 1)

            def h_project(s):
                act.activation(KH[:, s.c, :], full(s.k)[:, :], ACT.Identity, bias=wt(s, WH, "bk")).then_inc(sem("h_projected"), 1)
                act.activation(VH[:, s.c, :], full(s.k + 1)[:, :], ACT.Identity, bias=wt(s, WH, "bv")).then_inc(sem("h_projected"), 1)
                act.activation(QH[:, s.c, :], full(s.k + 2)[:, :], ACT.Identity, bias=wt(s, WH, "bq")).then_inc(sem("h_projected"), 1)

            def h_turn(s):
                copy(KTH[:, s.n % 2, :, :].rearrange("p a t -> p (a t)"), full(s.k)[:, :]).then_inc(sem("h_turned"), 1)

            def h_forward(s):
                for part in range(2):
                    copy(XH[:, s.n % 2, part, :], full(s.k + part)[:, 0:DFT]).then_inc(sem("h_transformed"), 1)

            parts = dict(weights=lambda s: weights_here(act, s), norm=norm, a_project=a_project, a_context=a_context, a_scores=a_scores, a_turn=a_turn,
                         a_out=a_out, a_mlp=a_mlp, gate=gate, r_project=r_project, core=core, w_rotate=w_rotate,
                         w_length=w_length, w_value=w_value, w_scores=w_scores, w_turn=w_turn, w_heads=w_heads,
                         w_mlp=w_mlp, h_kernels=h_kernels, h_project=h_project, h_turn=h_turn, h_forward=h_forward)
            act.preload_act_table_set("natural_log_exp_and_others")
            act.wait_ge(sem("const_loaded"), 16)
            for s in plan:
                if s.kind in parts:
                    parts[s.kind](s)

        @block.vector
        def _(dve):
            chain = [0]

            def link(instruction):
                chain[0] += 1
                instruction.then_inc(sem("vector_chain"), 1)
                dve.wait_ge(sem("vector_chain"), chain[0])

            def full(k):
                dve.wait_ge(tile_full, k + 1)
                return tile_of(k)

            def tables(s):
                if s.which == 2:
                    return
                w = s.which
                rows = ins["embk"][w].shape[1]
                lo = T - rows if w == 0 else T - 1 - P
                dve.wait_ge(sem("embk_loaded"), 16 * (w + 1))
                dve.tensor_copy(ET8[:, 0:lo], bc(ET8[:, lo:lo + 1], [D_R, lo])).then_inc(sem("embk_widened"), 1)
                hi = lo + rows
                dve.tensor_copy(ET8[:, hi:2 * T - 1], bc(ET8[:, hi - 1:hi], [D_R, 2 * T - 1 - hi]))\
                    .then_inc(sem("embk_widened"), 1)

            def enter(s):
                dve.tensor_copy(outer[:, s.c, :], full(s.k)[:, :]).then_inc(sem("stream_done"), 1)

            def leave(s):
                dve.tensor_copy(token_out[:, s.c].rearrange("p a f -> p (a f)"), full(s.k)[:, :])\
                    .then_inc(sem("token_out_done"), 1)

            def add_residual(s, k, stream, bias=None):
                o = full(k)[:, :]
                if bias is None:
                    step = dve.tensor_tensor(stream[:, s.c, :], o, stream[:, s.c, :], ALU.add)
                else:
                    step = dve.scalar_tensor_tensor(out=stream[:, s.c, :], in0=o, scalar=bias, in1=stream[:, s.c, :],
                                                    op0=ALU.add, op1=ALU.add)
                step.then_inc(sem("stream_done"), 1)

            def fold(s):
                dve.wait_ge(sem("stream_done"), s.stream)
                dve.tensor_tensor(outer[:, s.c, :], outer[:, s.c, :], inner[:, s.c, :], ALU.add)\
                    .then_inc(sem("stream_done"), 1)

            def norm(s):
                src, dst = streams[s.src], streams[s.dst]
                for c in range(C):
                    source_ready(dve, s, c)
                    dve.tensor_tensor(centered[:, c, :], src[:, c, :], full(s.k + c)[:, :], ALU.subtract)\
                        .then_inc(sem("norm_centered"), 1)
                for c in range(C):
                    dve.wait_ge(sem("norm_rstd"), C * s.n + c + 1)
                    if s.gain:
                        dve.scalar_tensor_tensor(out=dst[:, c, :], in0=centered[:, c, :], scalar=wt(s, s.table, s.gain[0]),
                                                 in1=squared[:, c, :], op0=ALU.mult, op1=ALU.mult)\
                            .then_inc(sem("norm_scaled"), 1)
                    else:
                        dve.tensor_tensor(dst[:, c, :], centered[:, c, :], squared[:, c, :], ALU.mult)\
                            .then_inc(sem("norm_done"), 1)

            def heads4(a):
                return a.rearrange("p a (h d) -> p a h d", h=4)

            def per_head(a):
                return bc(a.rearrange("p (a h) -> p a h", a=4).unsqueeze(3), [P, 4, 4, DH_A])

            def a_project(s):
                b = s.c % 2
                dve.memset(TM[:, b, :, 256:257], 1.0)
                for half in range(2):
                    dve.tensor_copy(TM[:, b, 2 * half:2 * half + 2, 0:256],
                                    full(s.k + 2 + half)[:, :].rearrange("p (a f) -> p a f", a=2))\
                        .then_inc(sem("a_token_copied"), 1)
                dve.wait_ge(sem("a_token_copied"), 2 * s.n + 2)
                q, k = TM[:, b, :, 0:64], TM[:, b, :, 64:128]
                link(dve.tensor_reduce(out=qmax.rearrange("p (a h) -> p a h", a=4), in_=heads4(q), axis=AX.X, op=ALU.max))
                dve.tensor_tensor(heads4(EB[:, :, 0:64]), heads4(q), per_head(qmax), ALU.subtract)
                dve.tensor_scalar(EB[:, :, 64:128], k, 0.0, None, ALU.min).then_inc(sem("a_shifted"), 1)

            def a_linear(s):
                b = s.c % 2
                dve.wait_ge(sem("a_linear_exp"), s.n + 1)
                link(dve.tensor_reduce(out=qsum.rearrange("p (a h) -> p a h", a=4), in_=heads4(EE[:, :, 0:64]),
                                       axis=AX.X, op=ALU.add))
                link(dve.reciprocal(qsum, qsum))
                dve.tensor_tensor(heads4(QN), heads4(EE[:, :, 0:64]), per_head(qsum), ALU.mult)\
                    .then_inc(sem("a_linear_q"), 1)
                dve.scalar_tensor_tensor(out=KF, in0=TM[:, b, :, 64:128], scalar=0.0, in1=EE[:, :, 64:128],
                                         op0=ALU.max, op1=ALU.add).then_inc(sem("a_linear_k"), 1)

            def a_context(s):
                o = full(s.k + 1)[0:64, 0:455].rearrange("p (u f) -> p u f", u=NB_A - 1)
                dve.memset(CN[0:64, 0, :], 0.0)
                link(dve.tensor_scalar(kcum[0:64, 0:7], o[:, :, 64], 1e-6, None, ALU.add))
                dve.reciprocal(kcum[0:64, 0:7], kcum[0:64, 0:7])
                dve.tensor_tensor(CN[0:64, 1:8, :], o[:, :, 0:64], bc(k_("linear_mask")[0:64].unsqueeze(1), [64, 7, 64]),
                                  ALU.mult).then_inc(sem("a_context_read"), 1)
                dve.wait_ge(sem("a_context_read"), s.n + 1)
                dve.tensor_tensor(CN[0:64, 1:8, :], CN[0:64, 1:8, :], bc(kcum[0:64, 0:7].unsqueeze(2), [64, 7, 64]),
                                  ALU.mult).then_inc(sem("a_context_done"), 1)

            def a_scores(s):
                i, lo = s.i % 2, (0 if s.w else P)
                for h in range(LOC):
                    dve.tensor_tensor_reduce(out=SA[:, i, h, lo:256], in0=full(s.k + h)[:, lo:256],
                                             in1=k_("local_mask")[:, lo:256], scale=-float(DH_A) ** -0.5, scalar=3e38,
                                             op0=ALU.add, op1=ALU.min, accum_out=small_a[:, s.i % 4, h:h + 1])\
                        .then_inc(sem("a_scored"), 1)

            def a_turn(s):
                v = "p (a b t) -> p a b t"
                lo = 0 if s.w else 1
                dve.tensor_copy(TA[:, s.i % 2, 1, :].rearrange(v, a=2, b=2)[:, :, lo:2, :],
                                full(s.k + 1)[:, :].rearrange(v, a=2, b=2)[:, :, lo:2, :])\
                    .then_inc(sem("a_turned_dve"), 1)

            def a_values(s):
                b = s.c % 2
                o = full(s.k)
                inverse = small_a[:, 8 + s.i % 2, 0:LOC]
                link(dve.reciprocal(inverse, small_a[:, 4 + s.i % 4, 0:LOC]))
                dve.tensor_tensor(ON[:, b, s.w, 0:64].rearrange("p (h d) -> p h d", h=LOC),
                                  o[:, 0:64].rearrange("p (h d) -> p h d", h=LOC),
                                  bc(inverse.unsqueeze(2), [P, LOC, DH_A]), ALU.mult)
                dve.tensor_copy(ON[:, b, s.w, 64:128], o[:, 64:128]).then_inc(sem("a_normalised"), 1)

            def a_out(s):
                add_residual(s, s.k + 1, inner, wt(s, WA, "bo"))

            def a_mlp(s):
                add_residual(s, s.k + 4, inner, wt(s, WA, "b2"))

            def gate(s):
                v = "p (t e) -> p t e"
                wide = [P, 16, EXPERTS]
                dve.tensor_copy(GG, full(s.k)[:, 0:P].rearrange(v, t=16)).then_inc(sem("gate_copied"), 1)
                dve.wait_ge(sem("gate_copied"), s.n + 1)
                link(dve.tensor_reduce(out=gmax, in_=GG, axis=AX.X, op=ALU.max))
                dve.tensor_tensor(GL, GG, bc(gmax.unsqueeze(2), wide), ALU.subtract).then_inc(sem("gate_shifted"), 1)
                dve.memset(GST, 0.0)
                dve.wait_ge(sem("gate_exp"), s.n + 1)
                link(dve.tensor_reduce(out=gsum, in_=GE, axis=AX.X, op=ALU.add))
                link(dve.reciprocal(gsum, gsum))
                link(dve.tensor_tensor(GG, GE, bc(gsum.unsqueeze(2), wide), ALU.mult))
                square = [P, 16, EXPERTS, EXPERTS]
                other, own = bc(GG.unsqueeze(2), square), bc(GG.unsqueeze(3), square)
                v4 = "p t (e o) -> p t e o"
                dve.tensor_tensor(CMP.rearrange(v4, e=8), other, own, ALU.is_gt)
                link(dve.tensor_tensor(CEQ.rearrange(v4, e=8), other, own, ALU.is_equal))
                link(dve.tensor_tensor(CEQ, CEQ, bc(k_("lower").unsqueeze(1), [P, 16, 64]), ALU.mult))
                link(dve.tensor_tensor(CMP, CMP, CEQ, ALU.add))
                link(dve.tensor_reduce(out=rank, in_=CMP.rearrange(v4, e=8), axis=AX.X, op=ALU.add))
                link(dve.scalar_tensor_tensor(out=GL, in0=rank, scalar=2.0, in1=GG, op0=ALU.is_lt, op1=ALU.mult))
                link(dve.tensor_reduce(out=gsum2, in_=GL, axis=AX.X, op=ALU.add))
                link(dve.reciprocal(gsum2, gsum2))
                dve.tensor_tensor(GS, GL, bc(gsum2.unsqueeze(2), wide), ALU.mult).then_inc(sem("gate_done"), 1)

            def expert(s):
                if s.half == 0 and s.c == 0:
                    dve.wait_ge(sem("gate_done"), s.n // (2 * C) + 1)
                for e in range(EXPERTS):
                    for a in range(2):
                        tt = 2 * s.half + a
                        o = full(s.k + 2 * a + e // 4)[:, (e % 4) * P:(e % 4 + 1) * P]
                        share = GS[:, s.c * NT + tt, e:e + 1]
                        acc = ACC[:, s.c % 2, tt, :]
                        if e == 0:
                            step = dve.tensor_scalar(acc, o, share, None, ALU.mult)
                        else:
                            dve.wait_ge(sem("expert_scaled"), 16 * s.n + 2 * (e - 1) + a + 1)
                            step = dve.scalar_tensor_tensor(out=acc, in0=o, scalar=share, in1=acc, op0=ALU.mult, op1=ALU.add)
                        step.then_inc(sem("expert_scaled"), 1)

            def expert_out(s):
                add_residual(s, s.k, outer)

            def r_project(s):
                if s.c == 0:
                    for b in range(2):
                        dve.tensor_copy(B4[64:P, b, :].rearrange("p (a f) -> p a f", a=4),
                                        bc(k_("diag_query")[64:P].unsqueeze(1), [64, 4, P]))
                o = full(s.k)[:, :]
                if s.which == 0:
                    dve.tensor_copy(QR[:, s.c, :], o).then_inc(sem("r_q_copied"), 1)
                else:
                    dve.tensor_scalar(QR[:, s.c, :], o, wt(s, WR, "bq"), float(D_R) ** -0.5, ALU.add, ALU.mult)\
                        .then_inc(sem("r_q_copied"), 1)

            def core(s):
                out_flat = centered[:, :, :].rearrange("p c t -> p (c t)")

                def diagonal(G, g, Q, at, nk):
                    if g % 4 == 0:
                        dve.wait_ge(sem("r_repeated"), Q + 1)
                        dve.tensor_tensor(B4[0:64, (g // 4) % 2, :].rearrange("p (a f) -> p a f", a=4),
                                          bank[6][0:64, :].rearrange("p (a f) -> p a f", a=4),
                                          bc(k_("diag_query")[0:64].unsqueeze(1), [64, 4, P]), ALU.mult)\
                            .then_inc(sem("r_diagonal"), 1)

                def weigh(G, g, Q, at, nk):
                    o = bank[4 + g % 2]
                    inverse = RIR[:, g % 8:g % 8 + 1]
                    dve.wait_ge(sem("r_values"), G + 1)
                    dve.reciprocal(inverse, RSR[:, g % 8:g % 8 + 1]).then_inc(sem("r_chain"), 1)
                    dve.wait_ge(sem("r_chain"), G * 3 + 1)
                    dve.scalar_tensor_tensor(out=O2M[:, g % 2, :], in0=o[:, P:P + 64], scalar=inverse,
                                             in1=k_("query_mask"), op0=ALU.mult, op1=ALU.mult).then_inc(sem("r_chain"), 1)
                    dve.wait_ge(sem("r_chain"), G * 3 + 2)
                    dve.tensor_reduce(out=W2[:, g % 2, :], in_=O2M[:, g % 2, :].rearrange("p (j d) -> p d j", j=QG),
                                      axis=AX.X, op=ALU.add).then_inc(sem("r_chain"), 1)
                    dve.wait_ge(sem("r_chain"), G * 3 + 3)
                    if s.which:
                        dve.scalar_tensor_tensor(out=ZR[:, g % 2, :], in0=o[:, 0:P], scalar=inverse, in1=k_("head_mask"),
                                                 op0=ALU.mult, op1=ALU.mult).then_inc(sem("r_weighted"), 1)
                        return
                    dve.scalar_tensor_tensor(out=TZ[:, g % 2, :].rearrange("p (h d) -> p h d", h=HEADS_R),
                                             in0=o[:, 0:P].rearrange("p (h d) -> p h d", h=HEADS_R), scalar=inverse,
                                             in1=bc(W2[:, g % 2, :].unsqueeze(1), [P, HEADS_R, D_R]),
                                             op0=ALU.mult, op1=ALU.add).then_inc(sem("r_weighted"), 1)

                def head_copy(G, g, Q, at, nk):
                    if g % 4 < 3:
                        return
                    dve.wait_ge(sem("r_heads"), G + 1)
                    dst = out_flat[:, bass.ds(at[0] * T + (at[1] - 3) * QG, 4 * QG)]
                    src = bank[7][:, 0:4 * QG]
                    if s.which == 0:
                        dve.tensor_copy(dst, src).then_inc(sem("r_head_copied"), 1)
                    else:
                        rows_ = slice(32 * at[0], 32 * at[0] + 32)
                        dve.tensor_copy(position_heads[rows_, :, bass.ds((at[1] - 3) * QG, 4 * QG)].rearrange("p l (q j) -> p l q j", q=4),
                                        bank[7][rows_, P:2 * P].rearrange("p (q l j) -> p l q j", q=4, l=C))
                        dve.tensor_scalar(dst, src, wt(s, WR, "bv"), None, ALU.add).then_inc(sem("r_head_copied"), 1)

                def maxima(G, g, Q, at, nk):
                    dve.wait_ge(sem("r_scores"), G + 1)
                    dve.tensor_reduce(out=NBR[:, g % 4:g % 4 + 1], in_=bank[g % 2][:, 0:nk * P], axis=AX.X, op=ALU.max,
                                      negate=True).then_inc(sem("r_max"), 1)

                for st in core_steps(dve, s.which):
                    st(diagonal, 0)
                    st(weigh, 3)
                    st(head_copy, 4)
                    st(maxima, 0)

            def r_out(s):
                add_residual(s, s.k, outer, wt(s, WR, "bo") if s.which else None)

            def w_rotate(s):
                t = 0 if s.x == "q" else 2
                if s.n == 0:
                    dve.wait_ge(sem("rotary_loaded"), 16)
                reached(dve, "w_scaled", s.n - 1)
                dve.wait_ge(sem("w_squared"), s.n + 1)
                dve.scalar_tensor_tensor(out=R1[:, s.n % 2, :], in0=full(s.k)[:, :], scalar=wt(s, WW, s.x + "s"),
                                         in1=rotary[:, t, :], op0=ALU.mult, op1=ALU.mult).then_inc(sem("w_cos"), 1)
                dve.scalar_tensor_tensor(out=R2[:, s.n % 2, :], in0=full(s.k + 1)[:, :], scalar=wt(s, WW, s.x + "s_rot"),
                                         in1=rotary[:, t + 1, :], op0=ALU.mult, op1=ALU.mult).then_inc(sem("w_sin"), 1)

            def w_length(s):
                dve.wait_ge(sem("w_added"), s.n + 1)
                dve.wait_ge(sem("w_inverse"), s.n + 1)
                if s.x == "q":
                    to = [(slice(64 * a, 64 * a + 64), QW[64 * a:64 * a + 64, a, s.pt, :]) for a in range(2)]
                else:
                    to = [(slice(0, P), KW[:, s.pt, :])]
                for rows_, dst in to:
                    last = dve.scalar_tensor_tensor(out=dst, in0=RNW[rows_, s.n % 4, :], scalar=1e12,
                                                    in1=R1[rows_, s.n % 2, :], op0=ALU.min, op1=ALU.mult)
                last.then_inc(sem("w_scaled"), 1)

            def w_scores(s):
                lo = 64 if s.i else P
                for a in range(2):
                    dve.tensor_tensor_reduce(out=SW[:, s.n % 2, a, lo:256], in0=full(s.k + a)[:, lo:256],
                                             in1=k_("window_mask")[:, lo - 64:192], scale=-8.0, scalar=3e38,
                                             op0=ALU.add, op1=ALU.min, accum_out=small_w[:, s.n % 4, a:a + 1])\
                        .then_inc(sem("w_scored"), 1)

            def w_turn(s):
                if s.n % 2:
                    return
                v = "p (a b t) -> p a b t"
                lo = 0 if s.i else 1
                o = full(s.k)
                if s.n:
                    dve.wait_ge(sem("w_turned"), s.n)
                dve.tensor_copy(TW[:, s.n % 2, :].rearrange(v, a=2, b=2)[:, :, lo:2, :],
                                o[:, :].rearrange(v, a=2, b=2)[:, :, lo:2, :]).then_inc(sem("w_turned"), 1)

            def w_values(s):
                o = full(s.k)
                inverse = small_w[:, s.n % 4, 4:6]
                link(dve.reciprocal(inverse, small_w[:, s.n % 4, 2:4]))
                dve.tensor_tensor(OW[:, s.i % 2, s.hp * P:(s.hp + 1) * P].rearrange("p (h d) -> p h d", h=2),
                                  o[:, 0:P].rearrange("p (h d) -> p h d", h=2), bc(inverse.unsqueeze(2), [P, 2, D_W]),
                                  ALU.mult).then_inc(sem("w_normalised"), 1)

            def w_out(s):
                add_residual(s, s.k, inner)

            def w_mlp(s):
                for j in range(HT_W):
                    o = full(s.k + 2 * j + 1)[:, :]
                    dve.wait_ge(sem("w_gelu"), HT_W * s.n + j + 1)
                    dve.scalar_tensor_tensor(out=HW[:, s.n % 2, j, :], in0=o, scalar=wt(s, WW, "b1a", j, 1),
                                             in1=GW[:, s.n % 2, j, :], op0=ALU.add, op1=ALU.mult).then_inc(sem("w_gated"), 1)
                add_residual(s, s.k + 2 * HT_W, inner, wt(s, WW, "b2"))

            def h_forward(s):
                dve.wait_ge(sem("h_spectra"), 4)
                dve.wait_ge(sem("h_transformed"), 2 * (s.n + 1))
                for part, m in ((0, M1), (1, M2)):
                    last = dve.tensor_tensor(m[:, s.n % 2], bc(XH[:, s.n % 2, part, :].unsqueeze(1), [P, 2, DFT]),
                                             SPEC[:, s.conv], ALU.mult)
                last.then_inc(sem("h_multiplied"), 1)

            def h_inverse(s):
                k = KH[:, s.c, :]
                dve.scalar_tensor_tensor(out=k, in0=k, scalar=wt(s, WH, "D" if s.conv else "k_D"), in1=full(s.k)[:, :],
                                         op0=ALU.mult, op1=ALU.add).then_inc(sem("h_convolved"), 1)
                dve.wait_ge(sem("h_convolved"), s.n + 1)
                if s.conv == 0:
                    dve.tensor_tensor(k, k, VH[:, s.c, :], ALU.mult).then_inc(sem("h_kv"), 1)
                else:
                    dve.tensor_tensor(VH[:, s.c, :], k, QH[:, s.c, :], ALU.mult).then_inc(sem("h_gated"), 1)

            def h_out(s):
                add_residual(s, s.k, outer, wt(s, WH, "bo"))

            parts = dict(weights=lambda s: weights_here(dve, s), tables=tables, enter=enter, leave=leave, norm=norm, fold=fold, a_project=a_project,
                         a_linear=a_linear, a_context=a_context, a_scores=a_scores, a_turn=a_turn, a_values=a_values,
                         a_out=a_out, a_mlp=a_mlp, gate=gate, expert=expert, expert_out=expert_out, r_project=r_project,
                         core=core, r_out=r_out, w_rotate=w_rotate, w_length=w_length, w_scores=w_scores, w_turn=w_turn,
                         w_values=w_values, w_out=w_out, w_mlp=w_mlp, h_forward=h_forward, h_inverse=h_inverse, h_out=h_out)
            dve.wait_ge(sem("const_loaded"), 16)
            for s in plan:
                if s.kind in parts:
                    parts[s.kind](s)

        @block.gpsimd
        def _(pool):
            half = P // 2

            def norm(s):
                if s.gain:
                    if s.affine == 0:
                        pool.memset(QL, 0.0).then_inc(sem("a_q_cleared"), 1)
                        pool.wait_ge(sem("a_q_cleared"), 1)
                    for c in range(C):
                        pool.wait_ge(sem("norm_scaled"), C * s.affine + c + 1)
                        a = streams[s.dst][:, c, :]
                        pool.tensor_scalar(a, a, wt(s, s.table, s.gain[1]), None, ALU.add).then_inc(sem("norm_done"), 1)

            def shift(s):
                source_ready(pool, s, 0)
                reached(pool, "w_added", s.rotations)
                if s.n == 0:
                    pool.memset(shifted[half:P, :, 0:1], 0.0).then_inc(sem("first_cleared"), 1)
                    pool.wait_ge(sem("first_cleared"), 1)
                if s.n % 2 == 0:
                    pool.memset(PW[:, :, :, 0:WIN], 0.0).then_inc(sem("pad_cleared"), 1)
                    pool.wait_ge(sem("pad_cleared"), s.n // 2 + 1)
                    for lane in range(C):
                        source_ready(pool, s, lane)
                    pool.memset(QW, 0.0).then_inc(sem("q_cleared"), 1)
                    pool.wait_ge(sem("q_cleared"), s.n // 2 + 1)
                for c in range(C):
                    source_ready(pool, s, c)
                    pool.tensor_copy(shifted[0:half, c, :], inner[0:half, c, :])
                    pool.tensor_copy(shifted[half:P, c, 1:T], inner[half:P, c, 0:T - 1]).then_inc(sem("shift_done"), 1)

            def core(s):
                queries, queries_by_lane = QR.rearrange("p a b -> p (a b)"), QR

                def spread(G, g, Q, at, nk):
                    if g % 4 == 0:
                        reached(pool, "r_scores", G - 4)
                        pool.tensor_tensor(A4[:, (g // 4) % 2, :].rearrange("p (t h) -> p t h", h=HEADS_R),
                                           bc(queries[:, bass.ds(at[0] * T + at[1] * QG, 4 * QG)].unsqueeze(2), [P, 4 * QG, HEADS_R]),
                                           bc(k_("spread_mask").unsqueeze(1), [P, 4 * QG, HEADS_R]), ALU.mult)\
                            .then_inc(sem("r_spread" if s.which == 0 else "r_keys_spread"), 1)
                        if s.which:
                            by_token = queries_by_lane[:, :, bass.ds(at[1] * QG, 4 * QG)].rearrange("p l t -> p t l")
                            mask = k_("swap_mask")[:, HEADS_R * at[0]:HEADS_R * (at[0] + 1)].rearrange("p (l m) -> p l m", l=C)
                            wide = [P, 4 * QG, C, HEADS_R // C]
                            pool.tensor_tensor(AX4[:, (g // 4) % 2, :].rearrange("p (t l m) -> p t l m", t=4 * QG, l=C),
                                               bc(by_token.unsqueeze(3), wide), bc(mask.unsqueeze(1), wide), ALU.mult)\
                                .then_inc(sem("r_spread"), 1)

                def own_head(G, g, Q, at, nk):
                    pool.wait_ge(sem("r_weighted"), G + 1)
                    if s.which:
                        pool.tensor_tensor(Z2[:, g % 2, :].rearrange("p (q d) -> p q d", q=4),
                                           bc(W2[:, g % 2, :].unsqueeze(1), [P, 4, D_R]),
                                           k_("quarter_mask").rearrange("p (q d) -> p q d", q=4), ALU.mult)\
                            .then_inc(sem("r_masked"), 1)
                        return
                    pool.tensor_tensor(ZR[:, g % 2, :], TZ[:, g % 2, :], k_("head_mask"), ALU.mult).then_inc(sem("r_masked"), 1)

                pool.wait_ge(sem("r_q_copied"), C * (s.which + 1))
                for st in core_steps(pool, s.which):
                    st(spread, 0)
                    st(own_head, 3)

            def w_rotate(s):
                if s.c == 0 and s.pt == 0 and s.x == "q":
                    pool.wait_ge(sem("shift_done"), C * (s.shift + 1))
                pool.wait_ge(sem("w_sin"), s.n + 1)
                pool.tensor_tensor(R1[:, s.n % 2, :], R1[:, s.n % 2, :], R2[:, s.n % 2, :], ALU.add).then_inc(sem("w_added"), 1)

            def h_forward(s):
                b = s.n % 2
                pool.wait_ge(sem("h_multiplied"), s.n + 1)
                pool.tensor_tensor(YH[:, b, 0, :], M1[:, b, 0, :], M2[:, b, 1, :], ALU.subtract).then_inc(sem("h_product"), 1)
                pool.tensor_tensor(YH[:, b, 1, :], M1[:, b, 1, :], M2[:, b, 0, :], ALU.add).then_inc(sem("h_product"), 1)

            parts = dict(weights=lambda s: weights_here(pool, s), norm=norm, shift=shift, core=core, w_rotate=w_rotate, h_forward=h_forward)
            pool.wait_ge(sem("const_loaded"), 16)
            for s in plan:
                if s.kind in parts:
                    parts[s.kind](s)


def shape_constants():
    import numpy as np

    p = np.arange(P)
    const = np.zeros((P, CONST_W), np.float32)

    def put(name, a):
        at, w = CONST[name]
        const[:a.shape[0], at:at + w] = a

    put("ident", np.eye(P))
    put("mean", np.full((P, P), 1.0 / P))
    put("ones", np.ones((P, P)))
    put("pair_ones", p[:, None] // D_W == p[None, :] // D_W)
    put("head_mask", p[:, None] % HEADS_R == p[None, :] // D_R)
    put("pick_query", p[:, None] // HEADS_R == np.arange(QG)[None, :])
    put("query_mask", p[:, None] // HEADS_R == QG - 1 - np.arange(64)[None, :] // D_R)
    put("spread_mask", p[:, None] // D_R == np.arange(HEADS_R)[None, :])
    put("repeat", p[:, None] % D_R == np.arange(64)[None, :] % D_R)
    put("diag_query", np.concatenate([np.arange(64)[:, None] // D_R == p[None, :] // HEADS_R,
                                      np.arange(QG)[:, None] == p[None, :] // HEADS_R]))
    lane_head = np.arange(C)[:, None] + 4 * (np.arange(HEADS_R)[None, :] % 4)
    put("swap_mask", p[:, None] // D_R == lane_head.reshape(1, -1))
    lane_query = np.arange(32)[None, :]
    put("pick_pair", (p[:, None] // HEADS_R == lane_query % QG) & (p[:, None] % 4 == lane_query // QG))
    put("quarter_mask", p[:, None] % HEADS_R // 4 == lane_query // D_R)
    s = np.arange(2 * P)
    put("local_mask", np.where(s[None, :] - P > p[:, None], NEG, 0.0))
    back = p[:, None] - (np.arange(P + WIN)[None, :] - WIN)
    put("window_mask", np.where((back < 0) | (back > WIN), NEG, 0.0))
    put("linear_mask", np.arange(64)[:, None] // DH_A == np.arange(64)[None, :] // DH_A)
    e = np.arange(EXPERTS)
    put("lower", np.broadcast_to((e[None, :] < e[:, None]).reshape(1, 64), (P, 64)))
    put("eps", np.broadcast_to(np.array([EPS, 2.0 ** -60, 15 * np.log(2.0), 0.0]), (P, 4)))

    far = np.arange(QG)[:, None] + (T - QG) - np.arange(ET_W)[None, :]
    causal = np.zeros((2, P - D_R * QG, ET_W), np.float32)
    causal[0, :QG] = np.where(far < 0, NEG, 0.0)

    d = p % D_W
    half_idx = (2 * (d % (D_W // 2))).astype(np.float32)
    inv_freq = (np.float32(1.0) / np.float32(10000.0) ** (half_idx / np.float32(D_W))).astype(np.float32)
    t = np.arange(T, dtype=np.float32)
    freqs = (t[None, :] * inv_freq[:, None]).astype(np.float32).astype(np.float64)
    base = (half_idx + 0.4 * D_W) / (1.4 * D_W)
    scale = base.astype(np.float64)[:, None] ** ((t - T // 2) / (WIN // 2))[None, :]
    sign = np.where(d < D_W // 2, -1.0, 1.0)[:, None]
    cos, sin = np.cos(freqs), np.sin(freqs) * sign
    rotary = np.stack([cos * scale, sin * scale, cos / scale, sin / scale], 1).reshape(P, 4 * T).astype(np.float32)

    theta = np.pi * (np.arange(DFT) + 0.5) / DFT
    turn = np.arange(T)[:, None] * theta[None, :]
    forward = np.concatenate([np.cos(turn), -np.sin(turn)], 1).reshape(NT, P, 2 * DFT).transpose(1, 0, 2)
    inverse = np.concatenate([np.cos(turn).T, -np.sin(turn).T], 0) / DFT
    inverse = inverse.reshape(2 * FT, P, T).transpose(1, 0, 2)
    dft = np.concatenate([forward.reshape(P, -1), inverse.reshape(P, -1)], 1).astype(np.float32)
    return {"const": const, "causal": causal, "rotary": rotary, "dft": dft}


def lay_out(inputs):
    import numpy as np

    arrays = {}

    def pack(name, names, width, parts):
        a = np.zeros((P, width), np.float32)
        for key, value in parts.items():
            at, w = names[key]
            value = value.reshape(value.shape[0], -1)
            a[:value.shape[0], at:at + value.shape[1]] = value
        arrays[name] = a

    def rows(w):
        tiles = -(-w.shape[0] // P)
        full = np.zeros((tiles * P, w.shape[1]), w.dtype)
        full[:w.shape[0]] = w
        return full.reshape(tiles, P, -1).transpose(1, 0, 2)

    def column(v):
        return rows(v[:, None])[:, :, 0]

    A = {k[10:]: v for k, v in inputs.items() if k.startswith("L0_attn_a_")}
    for i in range(DEPTH_A):
        def spaced(w):
            out = np.zeros((P, LOC, 32), w.dtype)
            out[:, :, :DH_A] = w[:, :LOC * DH_A].reshape(P, LOC, DH_A)
            return out
        linear = slice(LOC * DH_A, P)
        pack(f"wA{i}", WA, WA_W, {
            "q_loc": spaced(A["Wq"][i]), "k_loc": spaced(A["Wk"][i]),
            "qkv": np.concatenate([A["Wq"][i][:, linear], A["Wk"][i][:, linear], A["Wv"][i]], 1),
            "o": A["Wo"][i], "w1": A["W1"][i], "w2": rows(A["W2"][i]), "bo": column(A["bo"][i]),
            "g1": column(A["ln1_g"][i]), "b1n": column(A["ln1_b"][i]), "b1": column(A["b1"][i]),
            "b2": column(A["b2"][i]), "g2": column(A["ln2_g"][i]), "b2n": column(A["ln2_b"][i])})

    pack("wE", WE, WE_W, {"experts": inputs["L0_ffn_We"].transpose(2, 0, 1), "gate": inputs["L0_ffn_Wg"],
                          "be": inputs["L0_ffn_be"], "bg": inputs["L0_ffn_bg"][None, :]})

    w = inputs["L0_attn_b_w_attn"]
    pack("wR0", WR, WR_W, {"q": w[:, 0:P], "k": w[:, P:2 * P], "v": w[:, 2 * P:3 * P], "o": inputs["L0_attn_b_w_proj"]})
    B = {k[10:]: v for k, v in inputs.items() if k.startswith("L1_attn_a_")}
    pack("wR1", WR, WR_W, {"q": B["Wq"].T, "k": B["Wk"].T, "v": B["Wv"].T, "o": B["Wo"].T, "bq": column(B["bq"]),
                           "bk": column(B["bk"]), "bv": column(B["bv"]), "bo": column(B["bo"])})

    W = {k[7:]: v for k, v in inputs.items() if k.startswith("L1_ffn_")}
    inner = HEADS_W * D_W
    swapped = np.arange(inner).reshape(HEADS_W, 2, D_W // 2)[:, ::-1].reshape(-1)
    for i in range(DEPTH_W):
        q, k, v = (W["wqkv"][i][:, j * inner:(j + 1) * inner] for j in range(3))
        twice = lambda a: column(np.concatenate([a, a]))
        turned = lambda a: np.concatenate([a[D_W // 2:], a[:D_W // 2]])
        pack(f"wW{i}", WW, WW_W, {
            "q": q, "q_rot": q[:, swapped], "k": k, "k_rot": k[:, swapped], "v": v, "o": rows(W["wo"][i]),
            "w1a": W["w1"][i][:, :HID_W], "w1g": W["w1"][i][:, HID_W:], "w2": rows(W["w2"][i]),
            "qs": twice(W["q_scale"][i]), "qs_rot": twice(turned(W["q_scale"][i])),
            "ks": twice(W["k_scale"][i]), "ks_rot": twice(turned(W["k_scale"][i])),
            "g": column(W["ln_g"][i]), "b": column(W["ln_b"][i]),
            "b1a": column(W["b1"][i][:HID_W]), "b1g": column(W["b1"][i][HID_W:]), "b2": column(W["b2"][i])})

    H = {k[10:]: v for k, v in inputs.items() if k.startswith("L1_attn_b_")}
    pack("wH", WH, WH_W, {"q": H["Wq"].T, "k": H["Wk"].T, "v": H["Wv"].T, "o": H["Wo"].T,
                          "kernels": np.concatenate([H["k_kernel"], H["ssm_kernel"]], 1),
                          "bq": column(H["bq"]), "bk": column(H["bk"]), "bv": column(H["bv"]), "bo": column(H["bo"]),
                          "k_D": column(H["k_D"]), "D": column(H["D"])})

    arrays["embk0"] = np.ascontiguousarray(inputs["L0_attn_b_embk"][::-1].T)
    arrays["embk1"] = np.ascontiguousarray(inputs["L1_attn_a_rel_k_emb"][::-1].T)
    arrays["embv0"] = np.ascontiguousarray(inputs["L0_attn_b_embv"][::-1])
    arrays["embv1"] = np.ascontiguousarray(inputs["L1_attn_a_rel_v_emb"][::-1])
    arrays["x"] = np.ascontiguousarray(inputs["L0_attn_a_x"])
    return arrays


def kernel(**inputs):
    import numpy as np
    import concourse.bacc as bacc
    from concourse.bass_utils import run_bass_kernel_spmd

    arrays = lay_out({k: np.asarray(v) for k, v in inputs.items()})
    arrays.update(shape_constants())
    nc = bacc.Bacc("TRN2", target_bir_lowering=False, num_devices=1)
    aps = {name: nc.dram_tensor("in_" + name, a.shape, F32, kind="ExternalInput").ap() for name, a in arrays.items()}
    for pair in ("embk", "embv"):
        aps[pair] = [aps[pair + "0"], aps[pair + "1"]]
    scratch = [nc.dram_tensor(f"embv_padded{w}", (2 * T, D_R), F32, kind="Internal").ap() for w in range(2)]
    out = nc.dram_tensor("out", (C, T, P), F32, kind="ExternalOutput").ap()
    hybrid_network(nc, aps, scratch, out)
    result = run_bass_kernel_spmd(nc, [{"in_" + name: a for name, a in arrays.items()}], core_ids=[0])
    return result.results[0]["out"]
```

```python
from contextlib import ExitStack

import concourse.bass as bass
from concourse import mybir

F32 = mybir.dt.float32
F32R = mybir.dt.float32r
ALU = mybir.AluOpType
ACT = mybir.ActivationFunctionType
AX = mybir.AxisListType

P = 128
C = 4
T = 512
NT = T // P
BANKS = 8
NEG = -1.0e30
EPS = 1e-5

DEPTH_A, DH_A, LOC, BUCKET = 4, 16, 4, 64
NB_A = T // BUCKET
HID_A = 4 * P
HEADS_R, D_R, QG = 16, 8, 8
GROUPS = T // QG
LAST_LAG = 11
CHUNKS = C * GROUPS // 4
ET_W = 2 * T - QG
EV_W = (T - P) + T
EXPERTS = 8
DEPTH_W, HEADS_W, D_W, WIN = 2, 8, 64, 64
PAIRS = HEADS_W // 2
HID_W, HT_W = 341, 3
TAPS, DFT = 256, 384
FT = DFT // P


def columns(parts):
    at, out = 0, {}
    for name, width in parts:
        out[name] = (at, width)
        at += width
    return out, at


CONST, CONST_W = columns([
    ("ident", 128), ("mean", 128), ("ones", 128), ("pair_ones", 128), ("head_mask", 128), ("pick_query", 8),
    ("query_mask", 64), ("spread_mask", 16), ("repeat", 192), ("causal_query", 128), ("causal_rows", 248), ("diag_query", 128), ("local_mask", 256),
    ("swap_mask", 64), ("pick_pair", 32), ("quarter_mask", 32), ("window_mask", 192), ("linear_mask", 64), ("lower", 64), ("eps", 4)])
EXACT_W = sum(CONST[name][1] for name in ("repeat", "causal_query", "causal_rows"))
WORK_W, LOW = 18700, 6912
WA, WA_W = columns([
    ("q_loc", 128), ("k_loc", 128), ("qkv", 256), ("o", 128), ("w1", HID_A), ("w2", HID_A),
    ("bo", 1), ("g1", 1), ("b1n", 1), ("b1", 4), ("b2", 1), ("g2", 1), ("b2n", 1)])
WE, WE_W = columns([("experts", EXPERTS * P), ("gate", EXPERTS), ("be", P), ("bg", EXPERTS)])
WR, WR_W = columns([("q", 128), ("k", 128), ("v", 128), ("o", 128), ("bq", 1), ("bk", 1), ("bv", 1), ("bo", 1)])
WW, WW_W = columns([
    ("q", 512), ("q_rot", 512), ("k", 512), ("k_rot", 512), ("v", 512), ("o", 512),
    ("w1a", HT_W * P), ("w1g", HT_W * P), ("w2", HT_W * P),
    ("qs", 1), ("qs_rot", 1), ("ks", 1), ("ks_rot", 1), ("g", 1), ("b", 1), ("b1a", HT_W), ("b1g", HT_W), ("b2", 1)])
WH, WH_W = columns([("q", 128), ("k", 128), ("v", 128), ("o", 128), ("kernels", 2 * TAPS),
                    ("bq", 1), ("bk", 1), ("bv", 1), ("bo", 1), ("k_D", 1), ("D", 1)])
SLOT = max(WA_W, WE_W, WR_W, WW_W, WH_W)

LOADS = ["A0", "A1", "A2", "A3", "E", "R0", "E", "R1", "W0", "W1", "H", "W0", "W1"]


class Step:

    def __init__(self, kind, n, k, load, stream, norm, updated, shift, affine, rotations, c=0, w=0, i=0, half=0, which=0, conv=0,
                 x="", pt=0, hp=0, src="", via="", dst="", gain=None, table=None, name=""):
        self.kind, self.n, self.k = kind, n, k
        self.load, self.stream, self.norm, self.shift = load, stream, norm, shift
        self.updated = updated
        self.affine, self.rotations = affine, rotations
        self.c, self.w, self.i = c, w, i
        self.half, self.which, self.conv = half, which, conv
        self.x, self.pt, self.hp = x, pt, hp
        self.src, self.via, self.dst = src, via, dst
        self.gain, self.table, self.name = gain, table, name


STREAM = (("stream_done", 1, 1),)


def each(name, per, n=None):
    return tuple((name, per, i + 1) for i in range(n or per))


LAST_READ = {
    "enter": STREAM,
    "norm_mean": (("norm_centered", 1, 1),),
    "norm_scale": (("norm_rstd", 1, 1),),
    "a_project": (("a_local_copied", LOC + 1, LOC), ("a_local_copied", LOC + 1, LOC + 1)) + each("a_token_copied", 2),
    "a_context": (("a_q_turned", 1, 1), ("a_context_read", 1, 1)),
    "a_scores": each("a_scored", LOC),
    "a_turn": (("a_turned_act", 1, 1), ("a_turned_dve", 1, 1)),
    "a_values": (("a_normalised", 1, 1),),
    "a_out": (("a_heads", 1, 1),) + STREAM,
    "a_mlp": each("a_gelu", 4) + STREAM,
    "gate": (("gate_copied", 1, 1),),
    "gate_turn": each("gate_turned", C),
    "expert": tuple(("expert_scaled", 16, 2 * (4 * e + 3) + a + 1) for a in range(2) for e in range(2)),
    "expert_out": STREAM,
    "r_project": (("r_q_copied", 1, 1), ("r_keys_split", 1, 1), ("r_values_copied", 1, 1)),
    "r_out": STREAM,
    "w_rotate": (("w_cos", 1, 1), ("w_sin", 1, 1)),
    "w_length": (("w_inverse", 1, 1),),
    "w_value": each("w_v_copied", NT),
    "w_scores": each("w_scored", 2),
    "w_turn": (("w_turned", 1, 1),),
    "w_values": (("w_normalised", 1, 1),),
    "w_heads": (("w_heads_copied", 1, 1),),
    "w_out": STREAM,
    "w_mlp": tuple((x, HT_W, j + 1) for j in range(HT_W) for x in ("w_gelu", "w_gated")) + STREAM,
    "h_kernels": (("h_taps", 1, 1),) + each("h_spectra", 4),
    "h_project": each("h_projected", 3),
    "h_turn": (("h_turned", 1, 1),),
    "h_forward": each("h_transformed", 2),
    "h_inverse": (("h_convolved", 1, 1),),
    "h_out": STREAM,
    "leave": (("token_out_done", 1, 1),)}


def make_plan():
    plan, seen, released = [], {}, []
    state = {"tile": 0, "stream": 0, "load": -1}
    lane_norm, lane_shift, lane_stream = [-1] * C, [-1] * C, [0] * C

    def add(kind, load=None, **more):
        n = seen.get(kind, 0)
        seen[kind] = n + 1
        lane = more.get("c", 0)
        if kind == "norm_mean":
            lane_norm[lane] += 1
        if kind == "shift":
            lane_shift[lane] += 1
        step = Step(kind, n, state["tile"], load=state["load"] if load is None else load, stream=state["stream"],
                    norm=lane_norm[lane], updated=tuple(lane_stream),
                    shift=lane_shift[lane], affine=seen.get("affine", 0),
                    rotations=seen.get("w_rotate", 0), **more)
        if kind == "norm_scale" and more["gain"]:
            seen["affine"] = seen.get("affine", 0) + 1
        for name, a, b in LAST_READ.get(kind, ()):
            released.append((name, state["stream"] + 1 if name == "stream_done" else a * n + b))
        state["tile"] += len(LAST_READ.get(kind, ()))
        if kind in ("enter", "a_out", "a_mlp", "expert_out", "r_out", "w_out", "w_mlp", "h_out", "fold"):
            state["stream"] += 1
            lane_stream[lane] = state["stream"]
        plan.append(step)
        return step

    def weights():
        state["load"] += 1
        add("weights", name=LOADS[state["load"]])

    def norm(**how):
        for c in range(C):
            add("norm_mean", c=c, **how)
        for c in range(C):
            add("norm_scale", c=c, **how)

    def stage_a():
        first = dict(src="inner", via="norm", dst="normed", gain=("g1", "b1n"), table=WA)
        second = dict(src="inner", via="stream", dst="normed", gain=("g2", "b2n"), table=WA)
        weights()
        norm(**first)
        for layer in range(DEPTH_A):
            load = state["load"]
            for i in range(C * NT + 3):
                c, w = divmod(i, NT)
                if i == 0:
                    add("a_project", c=0)
                if i < C * NT:
                    add("a_scores", c=c, w=w, i=i)
                if i == 0:
                    add("a_linear", c=0)
                if w == 3 and c + 1 < C:
                    add("a_linear", c=c + 1)
                if 1 <= i <= C * NT:
                    add("a_turn", c=(i - 1) // NT, w=(i - 1) % NT, i=i - 1)
                if 2 <= i <= C * NT + 1:
                    add("a_values", c=(i - 2) // NT, w=(i - 2) % NT, i=i - 2)
                if w == 1 and c < C:
                    add("a_context", c=c)
                if w == 2 and c + 1 < C:
                    add("a_project", c=c + 1)
                if w == 2 and 1 <= c:
                    add("a_out", c=c - 1)
                if layer and i == 0:
                    add("norm_scale", c=2, **first)
                    add("norm_mean", c=3, **first)
                if layer and i == 1:
                    add("norm_scale", c=3, **first)
                if w == 3 and 1 <= c:
                    add("norm_mean", c=c - 1, **second)
                if w == 0 and 2 <= c:
                    add("norm_scale", c=c - 2, **second)
            add("norm_mean", c=3, **second)
            add("a_mlp", c=0)
            add("norm_scale", c=3, **second)
            add("a_mlp", c=1)
            if layer < DEPTH_A - 1:
                weights()
                if layer == 0:
                    add("tables", which=0)
                first["via"] = "stream"
                add("norm_mean", c=0, **first)
                add("a_mlp", c=2, load=load)
                add("norm_scale", c=0, **first)
                add("norm_mean", c=1, **first)
                add("a_mlp", c=3, load=load)
                add("norm_scale", c=1, **first)
                add("norm_mean", c=2, **first)
            else:
                add("a_mlp", c=2)
                add("a_mlp", c=3)
        for c in range(C):
            add("fold", c=c)

    def stage_e():
        weights()
        norm(src="outer", via="stream", dst="normed", gain=None, table=None)
        add("gate")
        if seen["gate"] == 2:
            add("tables", which=1)
        for c in range(C):
            for half in range(2):
                add("expert", c=c, half=half)
                if c == 0 and half == 0:
                    add("gate_turn")
            add("expert_out", c=c)

    def stage_r(which):
        weights()
        norm(src="outer", via="stream", dst="normed", gain=None, table=None)
        for c in range(C):
            add("r_project", c=c, which=which)
        add("core", which=which)
        for c in range(C):
            add("r_out", c=c, which=which)

    def stage_w():
        of_shifted = dict(src="shifted", via="shift", dst="normed", gain=("g", "b"), table=WW)
        weights()
        if seen.get("shift", 0) == 0:
            add("tables", which=2)
        for c in range(C):
            add("shift", c=c, via="norm")
        for layer in range(DEPTH_W):
            load = state["load"]
            for c in range(C):
                order = [(x, pt) for pt in range(PAIRS) for x in ("q", "k")]
                for j in range(len(order) + 1):
                    if j < len(order):
                        add("w_rotate", c=c, x=order[j][0], pt=order[j][1])
                    if j:
                        add("w_length", c=c, x=order[j - 1][0], pt=order[j - 1][1])
                if c:
                    add("shift", c=c - 1, via="stream")
                add("w_value", c=c)
                units = [(i, hp) for i in range(NT) for hp in range(PAIRS)]
                for j in range(len(units) + 4):
                    if j < len(units):
                        add("w_scores", c=c, i=units[j][0], hp=units[j][1])
                    if 1 <= j <= len(units):
                        add("w_turn", c=c, i=units[j - 1][0], hp=units[j - 1][1])
                    if 2 <= j <= len(units) + 1:
                        add("w_values", c=c, i=units[j - 2][0], hp=units[j - 2][1])
                    if 3 <= j <= len(units) + 2 and units[j - 3][1] == PAIRS - 1:
                        add("w_heads", c=c, i=units[j - 3][0])
                    if c and j == 3:
                        add("norm_mean", c=c - 1, **of_shifted)
                    if c and j == 9:
                        add("norm_scale", c=c - 1, **of_shifted)
                add("w_out", c=c)
            add("shift", c=3, via="stream")
            add("w_mlp", c=0)
            add("norm_mean", c=3, **of_shifted)
            add("w_mlp", c=1)
            add("norm_scale", c=3, **of_shifted)
            if layer < DEPTH_W - 1:
                weights()
                add("shift", c=0, via="stream")
                add("w_mlp", c=2, load=load)
                add("shift", c=1, via="stream")
                add("w_mlp", c=3, load=load)
                add("shift", c=2, via="stream")
                add("shift", c=3, via="stream")
            else:
                add("w_mlp", c=2)
                add("w_mlp", c=3)
        for c in range(C):
            add("fold", c=c)

    def stage_h():
        weights()
        add("h_kernels")
        norm(src="outer", via="stream", dst="normed", gain=None, table=None)
        for c in range(C):
            add("h_project", c=c)
        for conv in range(2):
            for c in range(C):
                add("h_turn", c=c, conv=conv)
                add("h_forward", c=c, conv=conv)
                if c:
                    add("h_inverse", c=c - 1, conv=conv)
            add("h_inverse", c=C - 1, conv=conv)
        for c in range(C):
            add("h_out", c=c)

    for c in range(C):
        add("enter", c=c)
    norm(src="outer", via="stream", dst="inner", gain=None, table=None)
    stage_a()
    stage_e()
    stage_r(0)
    stage_e()
    stage_r(1)
    norm(src="outer", via="stream", dst="inner", gain=None, table=None)
    stage_w()
    stage_h()
    norm(src="outer", via="stream", dst="inner", gain=None, table=None)
    stage_w()
    for c in range(C):
        add("leave", c=c)
    return plan, released


def segments(which):
    per = GROUPS // NT
    if which == 0:
        return [(per, C, (lambda it, g, b=b: (it, per * b + g)), b + 1) for b in range(NT)]
    return [(per, GROUPS // per, (lambda it, g, c=c: (c, per * it + g, it)), NT) for c in range(C)]


def hybrid_network(nc, ins, scratch, out):
    plan, released = make_plan()
    ctx = ExitStack()
    with ctx:
        def sb(name, shape, dtype=F32):
            return ctx.enter_context(nc.sbuf_tensor(name, shape, dtype))

        sems = {}

        def sem(name):
            if name not in sems:
                sems[name] = ctx.enter_context(nc.semaphore(name))
            return sems[name]

        bank = [ctx.enter_context(nc.psum_tensor(f"bank{b}", [P, T], F32)) for b in range(BANKS)]
        tile_full = sem("tile_full")

        outer = sb("outer", [P, C, T])
        inner = sb("inner", [P, C, T])
        normed = sb("normed", [P, C, T])
        centered = sb("centered", [P, C, T])
        squared = sb("squared", [P, C, T])
        shifted = sb("shifted", [P, C, T])
        const = sb("const", [P, CONST_W])
        slots = [sb(f"slot{s}", [P, SLOT]) for s in range(2)]
        table = sb("table", [P, 8192])
        streams = {"outer": outer, "inner": inner, "normed": normed, "shifted": shifted}
        ET8 = sb("embk_rows", [D_R, 2 * T])
        exact = sb("exact", [P, EXACT_W], F32R)
        with nc.sbuf_tensor("work", [P, WORK_W], F32) as work:
            pass
        low = sb("low", [P, LOW])
        halves = sb("halves", [P, WORK_W - LOW], F32R)

        cursor, place = [0], [work, WORK_W]

        def carve(*shape):
            size = 1
            for s in shape:
                size *= s
            a = place[0][:, cursor[0]:cursor[0] + size]
            cursor[0] += size
            assert cursor[0] <= place[1], cursor[0]
            if len(shape) == 1:
                return a
            names = "abcd"[:len(shape)]
            return a.rearrange(f"p ({' '.join(names)}) -> p {' '.join(names)}",
                               **{n: s for n, s in zip(names[1:], shape[1:])})

        KL = carve(2, T)
        TM = carve(2, NT, 260)
        EB, EE = carve(NT, 128), carve(NT, 128)
        QN, KF = carve(NT, 64), carve(NT, 64)
        QT = carve(T)
        CN = carve(NB_A, 64)
        SA, PA = carve(2, LOC, 256), carve(2, LOC, 256)
        TA = carve(2, 2, T)
        ON = carve(2, NT, P)
        AT = carve(T)
        small_a = carve(16, 16)
        qmax, qsum = carve(16), carve(16)
        kcum = carve(8)
        cursor[0] = max(cursor[0], 8192)
        QL = carve(2, LOC, T)
        HB = work[:, 0:8192].rearrange("p (a b c) -> p a b c", a=4, b=4)
        CN0 = CN
        cursor[0] = 0
        GL, GE, GG = carve(16, 8), carve(16, 8), carve(16, 8)
        CMP, CEQ = carve(16, 64), carve(16, 64)
        gmax, gsum, gsum2 = carve(16), carve(16), carve(16)
        rank = carve(16, 8)
        GS = carve(16, 8)
        GST = carve(C * T)
        ACC = carve(2, NT, P)
        cursor[0] = 0
        place = [low, LOW]
        QR_HI, QR_LO = squared, inner
        VR = carve(C, NT, P + 2 * QG * D_R)
        PR, PTR = carve(2, T), carve(2, T)
        O2M, W2, TZ, ZR = carve(2, 64), carve(2, 8), carve(2, P), carve(2, P)
        NBR, RSR, RIR = carve(4), carve(8), carve(8)
        Z2 = carve(2, 32)
        cursor[0], place = 0, [halves, WORK_W - LOW]
        KR_HI, KR_LO = carve(C, T), carve(C, T)
        A4, AX4 = carve(2, 2, T), carve(2, 2, T)
        B4 = carve(2, T)
        EK_HI, EK_LO = carve(ET_W), carve(ET_W)
        place = [work, WORK_W]
        position_heads = shifted
        key_table = table[:, 0:ET_W]
        value_table = table[:, 1024:1024 + EV_W * D_R]
        value_blocks = value_table.rearrange("p (b x) -> p b x", x=P * D_R)
        cursor[0] = 0
        QW, KW = carve(2, PAIRS, T), carve(PAIRS, T)
        VW = carve(NT, T)
        R1, R2 = carve(2, T), carve(2, T)
        SW, PW = carve(2, 2, 256), carve(2, 2, 256)
        TW = carve(2, T)
        OW = carve(2, T)
        AW = carve(PAIRS, T)
        small_w = carve(4, 8)
        HW = work[:, 2 * PAIRS * T:2 * PAIRS * T + 2 * HT_W * T].rearrange("p (a b c) -> p a b c", a=2, b=HT_W)
        GW = work[:, 2 * PAIRS * T + 2 * HT_W * T:2 * PAIRS * T + 4 * HT_W * T].rearrange("p (a b c) -> p a b c", a=2, b=HT_W)
        SQW = centered
        RNW = squared
        rotary = table[:, 6144:8192].rearrange("p (a t) -> p a t", a=4)
        cursor[0] = 0
        QH, KH, VH = carve(C, T), carve(C, T), carve(C, T)
        KTH = carve(2, NT, P)
        XH = carve(2, 2, DFT)
        M1, M2, YH = carve(2, 2, DFT), carve(2, 2, DFT), carve(2, 2, DFT)
        SPEC = carve(2, 2, DFT)
        KNT = carve(2, T)
        forward_dft = table[:, 0:NT * 2 * DFT].rearrange("p (a f) -> p a f", a=NT)
        inverse_dft = table[:, NT * 2 * DFT:NT * 2 * DFT + 2 * FT * T].rearrange("p (a t) -> p a t", a=2 * FT)
        token_io = squared[:, :, :].rearrange("p c (a f) -> p c a f", a=NT)
        token_out = centered[:, :, :].rearrange("p c (a f) -> p c a f", a=NT)

        def k_(name):
            a, w = CONST[name]
            return const[:, a:a + w]

        ident = k_("ident")
        eps_col = k_("eps")

        def wt(step, table_, name, lo=0, width=None):
            a, w = table_[name]
            s = slots[step.load % 2]
            return s[:, a + lo:a + lo + (w if width is None else width)]

        def bc(ap, shape):
            return ap.broadcast_to(shape)

        def exact_(name):
            a, w = CONST[name]
            return exact[:, a - CONST["repeat"][0]:a - CONST["repeat"][0] + w]

        def whole_words(ap):
            return ap.bitcast(F32)

        def tile_of(k):
            return bank[k % BANKS]

        block = ctx.enter_context(nc.Block())

        def source_ready(eng, s, c):
            if s.via == "shift":
                eng.wait_ge(sem("shift_done"), C * s.shift + c + 1)
            elif s.via == "norm":
                eng.wait_ge(sem("norm_done"), C * (s.norm - (s.kind == "norm_mean")) + c + 1)
            else:
                eng.wait_ge(sem("stream_done"), s.updated[c])

        def reached(eng, name, count):
            if not isinstance(count, int) or count > 0:
                eng.wait_ge(sem(name), count)

        def score_columns(which, g, nk):
            return nk * P if which or g < 2 else (nk - 1) * P + (g + 1) * QG

        def core_steps(eng, which):
            start, before = C * GROUPS * which, None
            for per, rounds, place, nk in segments(which):
                def group(it, g, start=start, per=per, place=place, nk=nk):
                    return start + it * per + g, g, start // 4 + it * (per // 4) + g // 4, place(it, g), nk

                def at(it, g, lag, before=before, per=per, group=group):
                    if g >= lag:
                        return group(it, g - lag)
                    if not isinstance(it, int) or it > 0:
                        return group(it - 1, per + g - lag)
                    return before(g - lag) if before else None

                def st_of(it, g, at=at):
                    def st(work_, lag):
                        d = at(it, g, lag)
                        if d is not None:
                            work_(*d)
                    return st

                for g in range(per):
                    yield st_of(0, g)
                with eng.Fori(1, rounds) as it:
                    for g in range(per):
                        yield st_of(it, g)
                before = lambda back, group=group, rounds=rounds, per=per: group(rounds - 1, per + back)
                start += per * rounds
            for g in range(LAST_LAG):
                def st(work_, lag, g=g):
                    if g < lag:
                        work_(*before(g - lag))
                yield st

        def weights_here(eng, s):
            eng.wait_ge(sem(f"slot{s.load % 2}_loaded"), 16 * (s.load // 2 + 1))

        @block.sync
        def _(sp):
            stage_ends = {}
            for s in plan:
                if s.load >= 0 and s.kind not in ("weights", "tables"):
                    stage_ends[s.load] = s.stream + (s.kind in ("fold", "a_mlp", "expert_out", "r_out", "w_mlp", "h_out"))

            def tables(s):
                if s.which < 2:
                    w = s.which
                    if w == 1:
                        sp.wait_ge(sem("r_head_copied"), CHUNKS)
                        sp.wait_ge(sem("r_key_halves"), 2)
                    rows = ins["embk"][w].shape[1]
                    lo = T - rows if w == 0 else T - 1 - P
                    sp.dma_start(ET8[0:D_R, lo:lo + rows], ins["embk"][w]).then_inc(sem("embk_loaded"), 16)
                    padded = scratch[w]
                    embv = ins["embv"][w]
                    first = lo
                    sp.dma_start(padded[0:first, :], bc(embv[0:1, :], [first, D_R])).then_inc(sem("embv_padded"), 16)
                    sp.dma_start(padded[first:first + rows, :], embv).then_inc(sem("embv_padded"), 16)
                    last = 2 * T - 1 - first - rows
                    sp.dma_start(padded[first + rows:2 * T - 1, :], bc(embv[rows - 1:rows, :], [last, D_R]))\
                        .then_inc(sem("embv_padded"), 16)
                    sp.wait_ge(sem("embk_widened"), 2 * w + 2)
                    for j in range(2 * QG):
                        shift = QG - 1 - j % QG
                        sp.dma_start(key_table[D_R * j:D_R * j + D_R, :], ET8[0:D_R, shift:shift + ET_W])\
                            .then_inc(sem("key_table"), 16)
                    sp.wait_ge(sem("embv_padded"), 48 * (w + 1))
                    sp.dma_start(value_table, bass.AP(padded.tensor, 0, [[D_R, P], [1, EV_W * D_R]]))\
                        .then_inc(sem("value_table"), 16)
                else:
                    sp.wait_ge(sem("r_head_copied"), 2 * CHUNKS)
                    sp.dma_start(table[:, 6144:8192], ins["rotary"]).then_inc(sem("rotary_loaded"), 16)
                    sp.dma_start(table[:, 0:6144], ins["dft"]).then_inc(sem("dft_loaded"), 16)

            def weights(s):
                if s.load >= 2:
                    sp.wait_ge(sem("stream_done"), stage_ends[s.load - 2])
                src = ins["w" + s.name]
                sp.dma_start(slots[s.load % 2][:, 0:src.shape[1]], src).then_inc(sem(f"slot{s.load % 2}_loaded"), 16)

            def enter(s):
                x = ins["x"][s.c].rearrange("(a p) f -> p a f", p=P)
                sp.dma_start(token_io[:, s.c], x).then_inc(sem(f"x_loaded{s.c}"), 16)

            def leave(s):
                sp.wait_ge(sem("token_out_done"), s.n + 1)
                sp.dma_start(out[s.c].rearrange("(a p) f -> p a f", p=P), token_out[:, s.c])\
                    .then_inc(sem("out_written"), 16)

            sp.dma_start(const[:, :], ins["const"]).then_inc(sem("const_loaded"), 16)
            order = [s for s in plan if s.kind == "enter"] + [s for s in plan if s.kind == "weights"][:2]
            order += [s for s in plan if s.kind in ("weights", "tables", "leave") and s not in order]
            for s in order:
                {"tables": tables, "weights": weights, "enter": enter, "leave": leave}[s.kind](s)
            sp.wait_ge(sem("out_written"), 16 * C)

        @block.tensor
        def _(pe):
            def take(k):
                if k >= BANKS:
                    name, count = released[k - BANKS]
                    pe.wait_ge(sem(name), count)
                return tile_of(k)

            def mm(o, l, r, start=True, stop=True):
                return pe.matmul(o, l, r, start=start, stop=stop)

            def enter(s):
                pe.wait_ge(sem(f"x_loaded{s.c}"), 16)
                o = take(s.k)
                for a in range(NT):
                    last = pe.transpose(o[:, a * P:(a + 1) * P], token_io[:, s.c, a, :], ident)
                last.then_inc(tile_full, 1)

            def leave(s):
                pe.wait_ge(sem("stream_done"), s.stream - C + s.c + 1)
                o = take(s.k)
                for a in range(NT):
                    last = pe.transpose(o[:, a * P:(a + 1) * P], outer[:, s.c, a * P:(a + 1) * P], ident)
                last.then_inc(tile_full, 1)

            def norm_mean(s):
                source_ready(pe, s, s.c)
                mm(take(s.k)[:, :], k_("mean"), streams[s.src][:, s.c, :]).then_inc(tile_full, 1)

            def norm_scale(s):
                pe.wait_ge(sem("norm_squared"), s.n + 1)
                mm(take(s.k)[:, :], k_("mean"), squared[:, s.c, :]).then_inc(tile_full, 1)

            def a_project(s):
                pe.wait_ge(sem("norm_done"), C * s.norm + s.c + 1)
                y = normed[:, s.c, :]
                mm(take(s.k)[:, :], wt(s, WA, "q_loc"), y).then_inc(tile_full, 1)
                mm(take(s.k + 1)[:, :], wt(s, WA, "k_loc"), y).then_inc(tile_full, 1)
                for half in range(2):
                    o = take(s.k + 2 + half)
                    for a in range(2):
                        tt = 2 * half + a
                        last = mm(o[:, a * 256:(a + 1) * 256], y[:, tt * P:(tt + 1) * P], wt(s, WA, "qkv"))
                    last.then_inc(tile_full, 1)

            def a_context(s):
                b = s.c % 2
                pe.wait_ge(sem("a_linear_q"), s.n + 1)
                o = take(s.k)
                for a in range(NT):
                    last = pe.transpose(o[0:64, a * P:(a + 1) * P], QN[:, a, :], ident)
                last.then_inc(tile_full, 1)
                pe.wait_ge(sem("a_linear_k"), s.n + 1)
                o = take(s.k + 1)
                for u in range(1, NB_A):
                    dst = o[0:64, (u - 1) * 65:u * 65]
                    for a in range(u // 2):
                        last = mm(dst, KF[:, a, :], TM[:, b, a, 192:257], start=(a == 0), stop=(a == u // 2 - 1 and u % 2 == 0))
                    if u % 2:
                        a = u // 2
                        last = mm(dst, KF[0:64, a, :], TM[0:64, b, a, 192:257], start=(a == 0), stop=True)
                last.then_inc(tile_full, 1)

            def a_scores(s):
                b = s.c % 2
                pe.wait_ge(sem("a_local_copied"), (LOC + 1) * (s.n // NT + 1))
                lo = 0 if s.w else P
                for h in range(LOC):
                    mm(take(s.k + h)[:, lo:256], QL[:, b, h, s.w * P:(s.w + 1) * P],
                       KL[:, b, (s.w - 1) * P + lo:(s.w + 1) * P]).then_inc(tile_full, 1)

            def a_turn(s):
                i = s.i % 2
                pe.wait_ge(sem("a_exp"), s.n + 1)
                for half in range(2):
                    o = take(s.k + half)
                    for a in range(2):
                        for blk in range(0 if s.w else 1, 2):
                            last = pe.transpose(o[:, (2 * a + blk) * P:(2 * a + blk + 1) * P],
                                                PA[:, i, 2 * half + a, blk * P:(blk + 1) * P], ident)
                    last.then_inc(tile_full, 1)

            def a_values(s):
                i, b = s.i % 2, s.c % 2
                pe.wait_ge(sem("a_turned_act"), s.n + 1)
                pe.wait_ge(sem("a_turned_dve"), s.n + 1)
                o = take(s.k)
                for h in range(LOC):
                    for blk in range(0 if s.w else 1, 2):
                        mm(o[:, h * DH_A:(h + 1) * DH_A],
                           TA[:, i, h // 2, (2 * (h % 2) + blk) * P:(2 * (h % 2) + blk + 1) * P],
                           TM[:, b, s.w - 1 + blk, P + h * DH_A:P + (h + 1) * DH_A],
                           start=(blk == (0 if s.w else 1)), stop=(blk == 1))
                pe.wait_ge(sem("a_context_done"), s.n // NT + 1)
                pe.wait_ge(sem("a_q_turned"), s.n // NT + 1)
                for e in range(2):
                    u = 2 * s.w + e
                    last = mm(o[64 * e:64 * e + 64, 64:128], QT[0:64, u * 64:(u + 1) * 64], CN[0:64, u, :])
                last.then_inc(tile_full, 1)

            def a_out(s):
                b = s.c % 2
                pe.wait_ge(sem("a_normalised"), NT * (s.n + 1))
                o = take(s.k)
                for w in range(NT):
                    last = pe.transpose(o[:, w * P:(w + 1) * P], ON[:, b, w, :], ident)
                last.then_inc(tile_full, 1)
                pe.wait_ge(sem("a_heads"), s.n + 1)
                mm(take(s.k + 1)[:, :], wt(s, WA, "o"), AT).then_inc(tile_full, 1)

            def a_mlp(s):
                pe.wait_ge(sem("norm_done"), C * s.norm + s.c + 1)
                for j in range(4):
                    mm(take(s.k + j)[:, :], wt(s, WA, "w1", j * P, P), normed[:, s.c, :]).then_inc(tile_full, 1)
                o = take(s.k + 4)
                for j in range(4):
                    pe.wait_ge(sem("a_gelu"), 4 * s.n + j + 1)
                    last = mm(o[:, :], wt(s, WA, "w2", j * P, P), HB[:, s.c, j, :], start=(j == 0), stop=(j == 3))
                last.then_inc(tile_full, 1)

            def gate(s):
                o = take(s.k)
                for c in range(C):
                    pe.wait_ge(sem("norm_done"), C * s.norm + c + 1)
                    for a in range(NT):
                        dst = o[:, (c * NT + a) * 8:(c * NT + a + 1) * 8]
                        mm(dst, normed[:, c, a * P:(a + 1) * P], wt(s, WE, "gate"), stop=False)
                        last = mm(dst, k_("ones")[0:1, :], wt(s, WE, "bg")[0:1, :], start=False)
                last.then_inc(tile_full, 1)

            def gate_turn(s):
                pe.wait_ge(sem("gate_done"), s.n + 1)
                for c in range(C):
                    o = take(s.k + c)
                    for a in range(NT):
                        last = pe.transpose(o[0:8, a * P:(a + 1) * P], GS[:, c * NT + a, :], ident)
                    last.then_inc(tile_full, 1)

            def expert(s):
                for a in range(2):
                    y = normed[:, s.c, (2 * s.half + a) * P:(2 * s.half + a + 1) * P]
                    for e in range(2):
                        mm(take(s.k + 2 * a + e)[:, :], y, wt(s, WE, "experts", e * T, T)).then_inc(tile_full, 1)

            def expert_out(s):
                o = take(s.k)
                pe.wait_ge(sem("gate_turned"), s.n + 1)
                mm(o[:, :], wt(s, WE, "be"), GST[:, s.c * T:(s.c + 1) * T], stop=False)
                pe.wait_ge(sem("expert_scaled"), 16 * 2 * (s.n + 1))
                for a in range(NT):
                    last = mm(o[:, a * P:(a + 1) * P], ACC[:, s.c % 2, a, :], ident, start=False, stop=(a == NT - 1))
                last.then_inc(tile_full, 1)

            def r_project(s):
                pe.wait_ge(sem("norm_done"), C * s.norm + s.c + 1)
                y = normed[:, s.c, :]
                mm(take(s.k)[:, :], wt(s, WR, "q"), y).then_inc(tile_full, 1)
                mm(take(s.k + 1)[:, :], wt(s, WR, "k"), y).then_inc(tile_full, 1)
                o = take(s.k + 2)
                for a in range(NT):
                    last = mm(o[:, a * P:(a + 1) * P], y[:, a * P:(a + 1) * P], wt(s, WR, "v"))
                last.then_inc(tile_full, 1)

            def core(s):
                for name, count in released[s.k - BANKS:s.k]:
                    pe.wait_ge(sem(name), count)
                pe.wait_ge(sem("r_q_copied"), C * (s.which + 1))
                pe.wait_ge(sem("r_keys_split"), C * (s.which + 1))
                pe.wait_ge(sem("r_values_copied"), C * (s.which + 1))
                pe.wait_ge(sem("r_key_halves"), 2 * (s.which + 1))
                pe.wait_ge(sem("r_constants"), 1)
                keys_hi = KR_HI.rearrange("p a b -> p (a b)")
                keys_lo = KR_LO.rearrange("p a b -> p (a b)")
                wide = P + 2 * QG * D_R
                values_flat = VR.rearrange("p a b c -> p (a b c)")
                two_tables = (EK_HI, EK_LO)

                def turn(G, g, Q, at, nk):
                    pe.wait_ge(sem("r_exp"), G + 1)
                    for b in range(nk):
                        last = pe.transpose(bank[2 + g % 2][:, b * P:(b + 1) * P], PR[:, g % 2, b * P:(b + 1) * P], ident)
                    last.then_inc(sem("r_turned"), 1)

                def values(G, g, Q, at, nk):
                    lane = at[0]
                    pe.wait_ge(sem("r_turn_copied"), G + 1)
                    pe.wait_ge(sem("r_embedded"), G + 1)
                    reached(pe, "r_weighted", G - 1)
                    o = bank[4 + g % 2]
                    width = P + QG * D_R
                    for b in range(nk):
                        last = mm(o[:, 0:width], PTR[:, g % 2, b * P:(b + 1) * P],
                                  values_flat[:, bass.ds((lane * NT + b) * wide + (g % 2) * (QG * D_R), width)],
                                  start=(b == 0), stop=(b == nk - 1))
                    last.then_inc(sem("r_values"), 1)

                def spread(G, g, Q, at, nk):
                    if g % 4 == 0:
                        pe.wait_ge(sem("r_spread"), 2 * Q + 2)
                        if s.which:
                            pe.wait_ge(sem("r_keys_spread"), 2 * (Q - CHUNKS) + 2)
                        rows_ = A4 if s.which == 0 else AX4
                        for half in range(2):
                            to = QG * D_R * (1 - half)
                            last = mm(bank[6][:, :], exact_("repeat")[:, to:to + P], rows_[:, half, (g // 4) % 2, :],
                                      start=(half == 0), stop=(half == 1))
                        last.then_inc(sem("r_repeated"), 1)

                def keys(G, g, Q, at, nk):
                    reached(pe, "r_exp", G - 1)
                    for half, keys_ in ((0, keys_hi), (0, keys_lo), (1, keys_hi)):
                        mm(bank[g % 2][:, 0:nk * P], A4[:, half, (g // 4) % 2, (g % 4) * P:(g % 4 + 1) * P],
                           keys_[:, bass.ds(at[0] * T, nk * P)], start=(half == 0 and keys_ is keys_hi), stop=False)

                def shifts(G, g, Q, at, nk):
                    pe.wait_ge(sem("r_diagonal"), Q + 1)
                    for half in range(2):
                        last = mm(bank[g % 2][:, 0:nk * P], B4[:, (g // 4) % 2, (g % 4) * P:(g % 4 + 1) * P],
                                  two_tables[half][:, bass.ds((T - QG) - at[1] * QG, nk * P)],
                                  start=False, stop=(half == 1 and s.which == 1))
                    if s.which == 0:
                        last = mm(bank[g % 2][:, (nk - 1) * P:nk * P], exact_("causal_query"),
                                  exact_("causal_rows")[:, P - QG - QG * g:2 * P - QG - QG * g], start=False)
                    last.then_inc(sem("r_scores"), 1)

                def heads(G, g, Q, at, nk):
                    pe.wait_ge(sem("r_masked"), G + 1)
                    if g % 4 == 0:
                        reached(pe, "r_head_copied", Q)
                    last = mm(bank[7][:, (g % 4) * QG:(g % 4 + 1) * QG], ZR[:, g % 2, :], k_("pick_query"))
                    if s.which:
                        last = mm(bank[7][32 * at[0]:32 * at[0] + 32, P + 32 * (g % 4):P + 32 * (g % 4) + 32],
                                  Z2[:, g % 2, :], k_("pick_pair"))
                    last.then_inc(sem("r_heads"), 1)

                for st in core_steps(pe, s.which):
                    st(turn, 8)
                    st(heads, 11)
                    st(values, 9)
                    st(spread, 5)
                    st(keys, 6)
                    st(shifts, 6)
                pe.wait_ge(sem("r_head_copied"), CHUNKS * (s.which + 1))

            def r_out(s):
                pe.wait_ge(sem("r_head_copied"), CHUNKS * (s.which + 1))
                o = take(s.k)[:, :]
                last = mm(o, wt(s, WR, "o"), centered[:, s.c, :], stop=not s.which)
                if s.which:
                    last = mm(o, wt(s, WR, "o"), position_heads[:, s.c, :], start=False)
                last.then_inc(tile_full, 1)

            def w_rotate(s):
                pe.wait_ge(sem("shift_done"), C * s.shift + s.c + 1)
                h = shifted[:, s.c, :]
                mm(take(s.k)[:, :], wt(s, WW, s.x, s.pt * P, P), h).then_inc(tile_full, 1)
                mm(take(s.k + 1)[:, :], wt(s, WW, s.x + "_rot", s.pt * P, P), h).then_inc(tile_full, 1)

            def w_length(s):
                pe.wait_ge(sem("w_squared"), s.n + 1)
                mm(take(s.k)[:, :], k_("pair_ones"), SQW[:, s.n % 4, :]).then_inc(tile_full, 1)

            def w_value(s):
                for a in range(NT):
                    mm(take(s.k + a)[:, :], shifted[:, s.c, a * P:(a + 1) * P], wt(s, WW, "v")).then_inc(tile_full, 1)

            def w_scores(s):
                pe.wait_ge(sem("w_scaled"), 8 * (s.n // 16 + 1))
                lo = 0 if s.i else WIN
                for a in range(2):
                    mm(take(s.k + a)[:, WIN + lo:256], QW[:, a, s.hp, s.i * P:(s.i + 1) * P],
                       KW[:, s.hp, s.i * P - WIN + lo:(s.i + 1) * P]).then_inc(tile_full, 1)

            def w_turn(s):
                pe.wait_ge(sem("w_exp"), s.n + 1)
                o = take(s.k)
                for a in range(2):
                    for blk in range(0 if s.i else 1, 2):
                        last = pe.transpose(o[:, (2 * a + blk) * P:(2 * a + blk + 1) * P],
                                            PW[:, s.n % 2, a, blk * P:(blk + 1) * P], ident)
                last.then_inc(tile_full, 1)

            def w_values(s):
                if s.i == 0 and s.hp == 0:
                    pe.wait_ge(sem("w_v_copied"), NT * (s.n // 16 + 1))
                pe.wait_ge(sem("w_turned"), s.n + 1)
                o = take(s.k)
                for a in range(2):
                    h = 2 * s.hp + a
                    for blk in range(0 if s.i else 1, 2):
                        last = mm(o[:, a * 64:(a + 1) * 64], TW[:, s.n % 2, (2 * a + blk) * P:(2 * a + blk + 1) * P],
                                  VW[:, s.i - 1 + blk, h * 64:(h + 1) * 64], start=(blk == (0 if s.i else 1)), stop=(blk == 1))
                last.then_inc(tile_full, 1)

            def w_heads(s):
                pe.wait_ge(sem("w_normalised"), PAIRS * (s.n + 1))
                o = take(s.k)
                for pt in range(PAIRS):
                    last = pe.transpose(o[:, pt * P:(pt + 1) * P], OW[:, s.i % 2, pt * P:(pt + 1) * P], ident)
                last.then_inc(tile_full, 1)

            def w_out(s):
                pe.wait_ge(sem("w_heads_copied"), NT * (s.n + 1))
                o = take(s.k)
                for pt in range(PAIRS):
                    last = mm(o[:, :], wt(s, WW, "o", pt * P, P), AW[:, pt, :], start=(pt == 0), stop=(pt == PAIRS - 1))
                last.then_inc(tile_full, 1)

            def w_mlp(s):
                pe.wait_ge(sem("norm_done"), C * s.norm + s.c + 1)
                for j in range(HT_W):
                    mm(take(s.k + 2 * j)[:, :], wt(s, WW, "w1g", j * P, P), normed[:, s.c, :]).then_inc(tile_full, 1)
                    mm(take(s.k + 2 * j + 1)[:, :], wt(s, WW, "w1a", j * P, P), normed[:, s.c, :]).then_inc(tile_full, 1)
                o = take(s.k + 2 * HT_W)
                for j in range(HT_W):
                    pe.wait_ge(sem("w_gated"), HT_W * s.n + j + 1)
                    last = mm(o[:, :], wt(s, WW, "w2", j * P, P), HW[:, s.n % 2, j, :], start=(j == 0), stop=(j == HT_W - 1))
                last.then_inc(tile_full, 1)

            def h_kernels(s):
                o = take(s.k)
                for a in range(4):
                    last = pe.transpose(o[:, a * P:(a + 1) * P], wt(s, WH, "kernels", a * P, P), ident)
                last.then_inc(tile_full, 1)
                pe.wait_ge(sem("h_taps"), 1)
                pe.wait_ge(sem("dft_loaded"), 16)
                for v in range(2):
                    for part in range(2):
                        o = take(s.k + 1 + 2 * v + part)
                        for f in range(FT):
                            for a in range(2):
                                last = mm(o[:, f * P:(f + 1) * P],
                                          forward_dft[:, a, part * DFT + f * P:part * DFT + (f + 1) * P],
                                          KNT[:, v, a * P:(a + 1) * P], start=(a == 0), stop=(a == 1))
                        last.then_inc(tile_full, 1)

            def h_project(s):
                pe.wait_ge(sem("norm_done"), C * s.norm + s.c + 1)
                for j, x in enumerate("kvq"):
                    mm(take(s.k + j)[:, :], wt(s, WH, x), normed[:, s.c, :]).then_inc(tile_full, 1)

            def h_turn(s):
                if s.conv == 0:
                    pe.wait_ge(sem("h_projected"), 3 * (s.c + 1))
                else:
                    pe.wait_ge(sem("h_kv"), s.c + 1)
                o = take(s.k)
                for a in range(NT):
                    last = pe.transpose(o[:, a * P:(a + 1) * P], KH[:, s.c, a * P:(a + 1) * P], ident)
                last.then_inc(tile_full, 1)

            def h_forward(s):
                pe.wait_ge(sem("h_turned"), s.n + 1)
                for part in range(2):
                    o = take(s.k + part)
                    for f in range(FT):
                        for a in range(NT):
                            last = mm(o[:, f * P:(f + 1) * P],
                                      forward_dft[:, a, part * DFT + f * P:part * DFT + (f + 1) * P],
                                      KTH[:, s.n % 2, a, :], start=(a == 0), stop=(a == NT - 1))
                    last.then_inc(tile_full, 1)

            def h_inverse(s):
                pe.wait_ge(sem("h_product"), 2 * (s.n + 1))
                o = take(s.k)
                for f in range(2 * FT):
                    last = mm(o[:, :], YH[:, s.n % 2, f // FT, (f % FT) * P:(f % FT + 1) * P], inverse_dft[:, f, :],
                              start=(f == 0), stop=(f == 2 * FT - 1))
                last.then_inc(tile_full, 1)

            def h_out(s):
                pe.wait_ge(sem("h_gated"), s.c + 1)
                mm(take(s.k)[:, :], wt(s, WH, "o"), VH[:, s.c, :]).then_inc(tile_full, 1)

            parts = dict(weights=lambda s: weights_here(pe, s), enter=enter, leave=leave, norm_mean=norm_mean, norm_scale=norm_scale, a_project=a_project, a_context=a_context,
                         a_scores=a_scores, a_turn=a_turn, a_values=a_values, a_out=a_out, a_mlp=a_mlp, gate=gate, gate_turn=gate_turn,
                         expert=expert, expert_out=expert_out, r_project=r_project, core=core, r_out=r_out,
                         w_rotate=w_rotate, w_length=w_length, w_value=w_value, w_scores=w_scores, w_turn=w_turn,
                         w_values=w_values, w_heads=w_heads, w_out=w_out, w_mlp=w_mlp, h_kernels=h_kernels,
                         h_project=h_project, h_turn=h_turn, h_forward=h_forward, h_inverse=h_inverse, h_out=h_out)
            pe.wait_ge(sem("const_loaded"), 16)
            for s in plan:
                if s.kind in parts:
                    parts[s.kind](s)

        @block.scalar
        def _(act):
            def full(k):
                act.wait_ge(tile_full, k + 1)
                return tile_of(k)

            def copy(dst, src):
                return act.activation(dst, src, ACT.Identity)

            def norm_mean(s):
                act.wait_ge(sem("norm_centered"), s.n + 1)
                act.activation(squared[:, s.c, :], centered[:, s.c, :], ACT.Square).then_inc(sem("norm_squared"), 1)

            def norm_scale(s):
                variance = full(s.k)[:, :]
                act.activation(variance, variance, ACT.Ln, bias=eps_col[:, 0:1]).then_inc(sem("norm_log"), 1)
                act.wait_ge(sem("norm_log"), s.n + 1)
                act.activation(squared[:, s.c, :], variance, ACT.Exp, scale=-0.5).then_inc(sem("norm_rstd"), 1)

            def a_project(s):
                b = s.c % 2
                if s.n == 0:
                    act.wait_ge(sem("a_q_cleared"), 1)
                for h in range(LOC):
                    r = slice(32 * h, 32 * h + DH_A)
                    copy(QL[r, b, h, :], full(s.k)[r, :]).then_inc(sem("a_local_copied"), 1)
                copy(KL[:, b, :], full(s.k + 1)[:, :]).then_inc(sem("a_local_copied"), 1)
                act.wait_ge(sem("a_shifted"), s.n + 1)
                act.activation(EE[:, :, :], EB[:, :, :], ACT.Exp).then_inc(sem("a_linear_exp"), 1)

            def a_context(s):
                copy(QT[0:64, :], full(s.k)[0:64, :]).then_inc(sem("a_q_turned"), 1)

            def a_scores(s):
                i, lo = s.i % 2, (0 if s.w else P)
                for h in range(LOC):
                    act.wait_ge(sem("a_scored"), LOC * s.n + h + 1)
                    last = act.activation(PA[:, i, h, lo:256], SA[:, i, h, lo:256], ACT.Exp, scale=-1.0,
                                          bias=small_a[:, s.i % 4, h:h + 1], accum_out=small_a[:, 4 + s.i % 4, h:h + 1])
                last.then_inc(sem("a_exp"), 1)

            def a_turn(s):
                i = s.i % 2
                src, dst = full(s.k), TA[:, i, 0, :]
                if s.w:
                    copy(dst, src[:, :]).then_inc(sem("a_turned_act"), 1)
                else:
                    copy(dst.rearrange("p (a b t) -> p a b t", a=2, b=2)[:, :, 1, :],
                         src[:, :].rearrange("p (a b t) -> p a b t", a=2, b=2)[:, :, 1, :]).then_inc(sem("a_turned_act"), 1)

            def a_out(s):
                copy(AT, full(s.k)[:, :]).then_inc(sem("a_heads"), 1)

            def a_mlp(s):
                for j in range(4):
                    act.activation(HB[:, s.c, j, :], full(s.k + j)[:, :], ACT.Gelu, bias=wt(s, WA, "b1", j, 1))\
                        .then_inc(sem("a_gelu"), 1)
                act.preload_act_table_set("natural_log_exp_and_others")

            def gate(s):
                act.wait_ge(sem("gate_shifted"), s.n + 1)
                act.activation(GE, GL, ACT.Exp).then_inc(sem("gate_exp"), 1)

            def gate_turn(s):
                for c in range(C):
                    copy(GST[0:8, c * T:(c + 1) * T], full(s.k + c)[0:8, :]).then_inc(sem("gate_turned"), 1)

            def r_project(s):
                act.wait_ge(tile_full, s.k + 2)
                keys_ = KR_HI[:, s.c, :]
                if s.which == 0:
                    act.activation(keys_, tile_of(s.k + 1)[:, :], ACT.Identity, scale=float(D_R) ** -0.5)\
                        .then_inc(sem("r_keys_copied"), 1)
                else:
                    act.activation(keys_, tile_of(s.k + 1)[:, :], ACT.Identity, bias=wt(s, WR, "bk"))\
                        .then_inc(sem("r_keys_copied"), 1)
                copy(VR[:, s.c, :, QG * D_R:QG * D_R + P], full(s.k + 2)[:, :].rearrange("p (a f) -> p a f", a=NT))\
                    .then_inc(sem("r_values_copied"), 1)

            def core(s):
                def turned(G, g, Q, at, nk):
                    act.wait_ge(sem("r_turned"), G + 1)
                    copy(PTR[:, g % 2, 0:nk * P], bank[2 + g % 2][:, 0:nk * P]).then_inc(sem("r_turn_copied"), 1)

                def exps(G, g, Q, at, nk):
                    act.wait_ge(sem("r_max"), G + 1)
                    n = score_columns(s.which, g, nk)
                    act.activation(PR[:, g % 2, 0:n], bank[g % 2][:, 0:n], ACT.Exp, bias=NBR[:, g % 4:g % 4 + 1],
                                   accum_out=RSR[:, g % 8:g % 8 + 1]).then_inc(sem("r_exp"), 1)

                for st in core_steps(act, s.which):
                    st(turned, 8)
                    st(exps, 6)

            def w_rotate(s):
                if s.c == 0 and s.pt == 0 and s.x == "q":
                    act.wait_ge(sem("norm_done"), C * (s.norm + 1))
                act.wait_ge(tile_full, s.k + 1)
                act.activation(SQW[:, s.n % 4, :], tile_of(s.k)[:, :], ACT.Square).then_inc(sem("w_squared"), 1)

            def w_length(s):
                act.wait_ge(tile_full, s.k + 1)
                act.activation(tile_of(s.k)[:, :], tile_of(s.k)[:, :], ACT.Ln, bias=eps_col[:, 1:2], scale=2.0 ** 30)\
                    .then_inc(sem("w_log"), 1)
                act.wait_ge(sem("w_log"), s.n + 1)
                if s.n >= 4:
                    act.wait_ge(sem("w_scaled"), s.n - 3)
                act.activation(RNW[:, s.n % 4, :], tile_of(s.k)[:, :], ACT.Exp, bias=eps_col[:, 2:3], scale=-0.5)\
                    .then_inc(sem("w_inverse"), 1)

            def w_value(s):
                for a in range(NT):
                    copy(VW[:, a, :], full(s.k + a)[:, :]).then_inc(sem("w_v_copied"), 1)

            def w_scores(s):
                lo = 64 if s.i else P
                for a in range(2):
                    act.wait_ge(sem("w_scored"), 2 * s.n + a + 1)
                    last = act.activation(PW[:, s.n % 2, a, lo:256], SW[:, s.n % 2, a, lo:256], ACT.Exp, scale=-1.0,
                                          bias=small_w[:, s.n % 4, a:a + 1], accum_out=small_w[:, s.n % 4, 2 + a:3 + a])
                last.then_inc(sem("w_exp"), 1)

            def w_turn(s):
                if s.n % 2 == 0:
                    return
                act.wait_ge(tile_full, s.k + 1)
                act.wait_ge(sem("w_turned"), s.n)
                v = "p (a b t) -> p a b t"
                lo = 0 if s.i else 1
                copy(TW[:, s.n % 2, :].rearrange(v, a=2, b=2)[:, :, lo:2, :], tile_of(s.k)[:, :].rearrange(v, a=2, b=2)[:, :, lo:2, :])\
                    .then_inc(sem("w_turned"), 1)

            def w_heads(s):
                copy(AW[:, :, s.i * P:(s.i + 1) * P], full(s.k)[:, :].rearrange("p (a t) -> p a t", a=PAIRS))\
                    .then_inc(sem("w_heads_copied"), 1)

            def w_mlp(s):
                for j in range(HT_W):
                    act.activation(GW[:, s.n % 2, j, :], full(s.k + 2 * j)[:, :], ACT.Gelu, bias=wt(s, WW, "b1g", j, 1))\
                        .then_inc(sem("w_gelu"), 1)
                act.preload_act_table_set("natural_log_exp_and_others")

            def h_kernels(s):
                act.wait_ge(tile_full, s.k + 1)
                copy(KNT[:, :, 0:TAPS], tile_of(s.k)[:, :].rearrange("p (a t) -> p a t", a=2)).then_inc(sem("h_taps"), 1)
                for v in range(2):
                    for part in range(2):
                        copy(SPEC[:, v, part, :], full(s.k + 1 + 2 * v + part)[:, 0:DFT]).then_inc(sem("h_spectra"), 1)

            def h_project(s):
                act.activation(KH[:, s.c, :], full(s.k)[:, :], ACT.Identity, bias=wt(s, WH, "bk")).then_inc(sem("h_projected"), 1)
                act.activation(VH[:, s.c, :], full(s.k + 1)[:, :], ACT.Identity, bias=wt(s, WH, "bv")).then_inc(sem("h_projected"), 1)
                act.activation(QH[:, s.c, :], full(s.k + 2)[:, :], ACT.Identity, bias=wt(s, WH, "bq")).then_inc(sem("h_projected"), 1)

            def h_turn(s):
                copy(KTH[:, s.n % 2, :, :].rearrange("p a t -> p (a t)"), full(s.k)[:, :]).then_inc(sem("h_turned"), 1)

            def h_forward(s):
                for part in range(2):
                    copy(XH[:, s.n % 2, part, :], full(s.k + part)[:, 0:DFT]).then_inc(sem("h_transformed"), 1)

            parts = dict(weights=lambda s: weights_here(act, s), norm_mean=norm_mean, norm_scale=norm_scale, a_project=a_project, a_context=a_context, a_scores=a_scores, a_turn=a_turn,
                         a_out=a_out, a_mlp=a_mlp, gate=gate, gate_turn=gate_turn, r_project=r_project, core=core, w_rotate=w_rotate,
                         w_length=w_length, w_value=w_value, w_scores=w_scores, w_turn=w_turn, w_heads=w_heads,
                         w_mlp=w_mlp, h_kernels=h_kernels, h_project=h_project, h_turn=h_turn, h_forward=h_forward)
            act.preload_act_table_set("natural_log_exp_and_others")
            act.wait_ge(sem("const_loaded"), 16)
            for s in plan:
                if s.kind in parts:
                    parts[s.kind](s)

        @block.vector
        def _(dve):
            chain = [0]

            def link(instruction):
                chain[0] += 1
                instruction.then_inc(sem("vector_chain"), 1)
                dve.wait_ge(sem("vector_chain"), chain[0])

            def full(k):
                dve.wait_ge(tile_full, k + 1)
                return tile_of(k)

            def tables(s):
                if s.which == 2:
                    return
                w = s.which
                rows = ins["embk"][w].shape[1]
                lo = T - rows if w == 0 else T - 1 - P
                dve.wait_ge(sem("embk_loaded"), 16 * (w + 1))
                dve.tensor_copy(ET8[:, 0:lo], bc(ET8[:, lo:lo + 1], [D_R, lo])).then_inc(sem("embk_widened"), 1)
                hi = lo + rows
                dve.tensor_copy(ET8[:, hi:2 * T - 1], bc(ET8[:, hi - 1:hi], [D_R, 2 * T - 1 - hi]))\
                    .then_inc(sem("embk_widened"), 1)

            def enter(s):
                dve.tensor_copy(outer[:, s.c, :], full(s.k)[:, :]).then_inc(sem("stream_done"), 1)

            def leave(s):
                dve.tensor_copy(token_out[:, s.c].rearrange("p a f -> p (a f)"), full(s.k)[:, :])\
                    .then_inc(sem("token_out_done"), 1)

            def add_residual(s, k, stream, bias=None):
                o = full(k)[:, :]
                if bias is None:
                    step = dve.tensor_tensor(stream[:, s.c, :], o, stream[:, s.c, :], ALU.add)
                else:
                    step = dve.scalar_tensor_tensor(out=stream[:, s.c, :], in0=o, scalar=bias, in1=stream[:, s.c, :],
                                                    op0=ALU.add, op1=ALU.add)
                step.then_inc(sem("stream_done"), 1)

            def fold(s):
                dve.wait_ge(sem("stream_done"), s.stream)
                dve.tensor_tensor(outer[:, s.c, :], outer[:, s.c, :], inner[:, s.c, :], ALU.add)\
                    .then_inc(sem("stream_done"), 1)

            def norm_mean(s):
                source_ready(dve, s, s.c)
                dve.tensor_tensor(centered[:, s.c, :], streams[s.src][:, s.c, :], full(s.k)[:, :], ALU.subtract)\
                    .then_inc(sem("norm_centered"), 1)

            def norm_scale(s):
                dst = streams[s.dst][:, s.c, :]
                dve.wait_ge(sem("norm_rstd"), s.n + 1)
                if s.gain:
                    dve.scalar_tensor_tensor(out=dst, in0=centered[:, s.c, :], scalar=wt(s, s.table, s.gain[0]),
                                             in1=squared[:, s.c, :], op0=ALU.mult, op1=ALU.mult)\
                        .then_inc(sem("norm_scaled"), 1)
                else:
                    dve.tensor_tensor(dst, centered[:, s.c, :], squared[:, s.c, :], ALU.mult).then_inc(sem("norm_done"), 1)

            def heads4(a):
                return a.rearrange("p a (h d) -> p a h d", h=4)

            def per_head(a):
                return bc(a.rearrange("p (a h) -> p a h", a=4).unsqueeze(3), [P, 4, 4, DH_A])

            def a_project(s):
                b = s.c % 2
                dve.memset(TM[:, b, :, 256:257], 1.0)
                for half in range(2):
                    dve.tensor_copy(TM[:, b, 2 * half:2 * half + 2, 0:256],
                                    full(s.k + 2 + half)[:, :].rearrange("p (a f) -> p a f", a=2))\
                        .then_inc(sem("a_token_copied"), 1)
                dve.wait_ge(sem("a_token_copied"), 2 * s.n + 2)
                q, k = TM[:, b, :, 0:64], TM[:, b, :, 64:128]
                link(dve.tensor_reduce(out=qmax.rearrange("p (a h) -> p a h", a=4), in_=heads4(q), axis=AX.X, op=ALU.max))
                dve.tensor_tensor(heads4(EB[:, :, 0:64]), heads4(q), per_head(qmax), ALU.subtract)
                dve.tensor_scalar(EB[:, :, 64:128], k, 0.0, None, ALU.min).then_inc(sem("a_shifted"), 1)

            def a_linear(s):
                b = s.c % 2
                dve.wait_ge(sem("a_linear_exp"), s.n + 1)
                link(dve.tensor_reduce(out=qsum.rearrange("p (a h) -> p a h", a=4), in_=heads4(EE[:, :, 0:64]),
                                       axis=AX.X, op=ALU.add))
                link(dve.reciprocal(qsum, qsum))
                dve.tensor_tensor(heads4(QN), heads4(EE[:, :, 0:64]), per_head(qsum), ALU.mult)\
                    .then_inc(sem("a_linear_q"), 1)
                dve.scalar_tensor_tensor(out=KF, in0=TM[:, b, :, 64:128], scalar=0.0, in1=EE[:, :, 64:128],
                                         op0=ALU.max, op1=ALU.add).then_inc(sem("a_linear_k"), 1)

            def a_context(s):
                o = full(s.k + 1)[0:64, 0:455].rearrange("p (u f) -> p u f", u=NB_A - 1)
                dve.memset(CN[0:64, 0, :], 0.0)
                link(dve.tensor_scalar(kcum[0:64, 0:7], o[:, :, 64], 1e-6, None, ALU.add))
                dve.reciprocal(kcum[0:64, 0:7], kcum[0:64, 0:7])
                dve.tensor_tensor(CN[0:64, 1:8, :], o[:, :, 0:64], bc(k_("linear_mask")[0:64].unsqueeze(1), [64, 7, 64]),
                                  ALU.mult).then_inc(sem("a_context_read"), 1)
                dve.wait_ge(sem("a_context_read"), s.n + 1)
                dve.tensor_tensor(CN[0:64, 1:8, :], CN[0:64, 1:8, :], bc(kcum[0:64, 0:7].unsqueeze(2), [64, 7, 64]),
                                  ALU.mult).then_inc(sem("a_context_done"), 1)

            def a_scores(s):
                i, lo = s.i % 2, (0 if s.w else P)
                for h in range(LOC):
                    dve.tensor_tensor_reduce(out=SA[:, i, h, lo:256], in0=full(s.k + h)[:, lo:256],
                                             in1=k_("local_mask")[:, lo:256], scale=-float(DH_A) ** -0.5, scalar=3e38,
                                             op0=ALU.add, op1=ALU.min, accum_out=small_a[:, s.i % 4, h:h + 1])\
                        .then_inc(sem("a_scored"), 1)

            def a_turn(s):
                v = "p (a b t) -> p a b t"
                lo = 0 if s.w else 1
                dve.tensor_copy(TA[:, s.i % 2, 1, :].rearrange(v, a=2, b=2)[:, :, lo:2, :],
                                full(s.k + 1)[:, :].rearrange(v, a=2, b=2)[:, :, lo:2, :])\
                    .then_inc(sem("a_turned_dve"), 1)

            def a_values(s):
                b = s.c % 2
                o = full(s.k)
                inverse = small_a[:, 8 + s.i % 2, 0:LOC]
                link(dve.reciprocal(inverse, small_a[:, 4 + s.i % 4, 0:LOC]))
                dve.tensor_tensor(ON[:, b, s.w, 0:64].rearrange("p (h d) -> p h d", h=LOC),
                                  o[:, 0:64].rearrange("p (h d) -> p h d", h=LOC),
                                  bc(inverse.unsqueeze(2), [P, LOC, DH_A]), ALU.mult)
                dve.tensor_copy(ON[:, b, s.w, 64:128], o[:, 64:128]).then_inc(sem("a_normalised"), 1)

            def a_out(s):
                add_residual(s, s.k + 1, inner, wt(s, WA, "bo"))

            def a_mlp(s):
                add_residual(s, s.k + 4, inner, wt(s, WA, "b2"))

            def gate(s):
                v = "p (t e) -> p t e"
                wide = [P, 16, EXPERTS]
                dve.tensor_copy(GG, full(s.k)[:, 0:P].rearrange(v, t=16)).then_inc(sem("gate_copied"), 1)
                dve.wait_ge(sem("gate_copied"), s.n + 1)
                link(dve.tensor_reduce(out=gmax, in_=GG, axis=AX.X, op=ALU.max))
                dve.tensor_tensor(GL, GG, bc(gmax.unsqueeze(2), wide), ALU.subtract).then_inc(sem("gate_shifted"), 1)
                dve.memset(GST, 0.0)
                dve.wait_ge(sem("gate_exp"), s.n + 1)
                link(dve.tensor_reduce(out=gsum, in_=GE, axis=AX.X, op=ALU.add))
                link(dve.reciprocal(gsum, gsum))
                link(dve.tensor_tensor(GG, GE, bc(gsum.unsqueeze(2), wide), ALU.mult))
                square = [P, 16, EXPERTS, EXPERTS]
                other, own = bc(GG.unsqueeze(2), square), bc(GG.unsqueeze(3), square)
                v4 = "p t (e o) -> p t e o"
                dve.tensor_tensor(CMP.rearrange(v4, e=8), other, own, ALU.is_gt)
                link(dve.tensor_tensor(CEQ.rearrange(v4, e=8), other, own, ALU.is_equal))
                link(dve.tensor_tensor(CEQ, CEQ, bc(k_("lower").unsqueeze(1), [P, 16, 64]), ALU.mult))
                link(dve.tensor_tensor(CMP, CMP, CEQ, ALU.add))
                link(dve.tensor_reduce(out=rank, in_=CMP.rearrange(v4, e=8), axis=AX.X, op=ALU.add))
                link(dve.scalar_tensor_tensor(out=GL, in0=rank, scalar=2.0, in1=GG, op0=ALU.is_lt, op1=ALU.mult))
                link(dve.tensor_reduce(out=gsum2, in_=GL, axis=AX.X, op=ALU.add))
                link(dve.reciprocal(gsum2, gsum2))
                dve.tensor_tensor(GS, GL, bc(gsum2.unsqueeze(2), wide), ALU.mult).then_inc(sem("gate_done"), 1)

            def expert(s):
                if s.half == 0 and s.c == 0:
                    dve.wait_ge(sem("gate_done"), s.n // (2 * C) + 1)
                for e in range(EXPERTS):
                    for a in range(2):
                        tt = 2 * s.half + a
                        o = full(s.k + 2 * a + e // 4)[:, (e % 4) * P:(e % 4 + 1) * P]
                        share = GS[:, s.c * NT + tt, e:e + 1]
                        acc = ACC[:, s.c % 2, tt, :]
                        if e == 0:
                            step = dve.tensor_scalar(acc, o, share, None, ALU.mult)
                        else:
                            dve.wait_ge(sem("expert_scaled"), 16 * s.n + 2 * (e - 1) + a + 1)
                            step = dve.scalar_tensor_tensor(out=acc, in0=o, scalar=share, in1=acc, op0=ALU.mult, op1=ALU.add)
                        step.then_inc(sem("expert_scaled"), 1)

            def expert_out(s):
                add_residual(s, s.k, outer)

            def r_project(s):
                if s.c == 0 and s.which == 0:
                    a = CONST["repeat"][0]
                    dve.tensor_copy(exact[:, :], const[:, a:a + EXACT_W]).then_inc(sem("r_constants"), 1)
                if s.c == 0:
                    dve.wait_ge(sem("key_table"), 16 * 2 * QG * (s.which + 1))
                    dve.tensor_copy(EK_HI, key_table).then_inc(sem("r_key_halves"), 1)
                    dve.wait_ge(sem("r_key_halves"), 2 * s.which + 1)
                    dve.tensor_tensor(EK_LO, key_table, whole_words(EK_HI), ALU.subtract).then_inc(sem("r_key_halves"), 1)
                o = full(s.k)[:, :]
                whole = centered[:, s.c, :]
                if s.which == 0:
                    link(dve.tensor_copy(whole, o))
                else:
                    link(dve.tensor_scalar(whole, o, wt(s, WR, "bq"), float(D_R) ** -0.5, ALU.add, ALU.mult))
                link(dve.tensor_copy(QR_HI[:, s.c, :].bitcast(F32R), whole))
                dve.tensor_tensor(QR_LO[:, s.c, :], whole, QR_HI[:, s.c, :], ALU.subtract).then_inc(sem("r_q_copied"), 1)
                dve.wait_ge(sem("r_keys_copied"), C * s.which + s.c + 1)
                scalar, op = (float(D_R) ** -0.5, ALU.mult) if s.which == 0 else (wt(s, WR, "bk"), ALU.add)
                dve.scalar_tensor_tensor(out=KR_LO[:, s.c, :], in0=tile_of(s.k + 1)[:, :], scalar=scalar,
                                         in1=whole_words(KR_HI[:, s.c, :]), op0=op, op1=ALU.subtract).then_inc(sem("r_keys_split"), 1)

            def core(s):
                out_flat = centered[:, :, :].rearrange("p c t -> p (c t)")

                def diagonal(G, g, Q, at, nk):
                    if g % 4 == 0:
                        dve.wait_ge(sem("r_repeated"), Q + 1)
                        dve.tensor_tensor(B4[:, (g // 4) % 2, :].rearrange("p (a f) -> p a f", a=4),
                                          bank[6][:, :].rearrange("p (a f) -> p a f", a=4),
                                          bc(k_("diag_query").unsqueeze(1), [P, 4, P]), ALU.mult)\
                            .then_inc(sem("r_diagonal"), 1)

                def invert(G, g, Q, at, nk):
                    dve.wait_ge(sem("r_exp"), G + 1)
                    dve.reciprocal(RIR[:, g % 8:g % 8 + 1], RSR[:, g % 8:g % 8 + 1]).then_inc(sem("r_inverted"), 1)

                def own_place(G, g, Q, at, nk):
                    dve.wait_ge(sem("r_inverted"), G + 1)
                    dve.wait_ge(sem("r_values"), G + 1)
                    by_embedding = bank[4 + g % 2][:, P * (g % 2):P * (g % 2) + QG * D_R]
                    dve.scalar_tensor_tensor(out=O2M[:, g % 2, :], in0=by_embedding, scalar=RIR[:, g % 8:g % 8 + 1],
                                             in1=k_("query_mask"), op0=ALU.mult, op1=ALU.mult).then_inc(sem("r_chain"), 1)

                def own_sum(G, g, Q, at, nk):
                    dve.wait_ge(sem("r_chain"), G * 2 + 1)
                    dve.tensor_reduce(out=W2[:, g % 2, :], in_=O2M[:, g % 2, :].rearrange("p (j d) -> p d j", j=QG),
                                      axis=AX.X, op=ALU.add).then_inc(sem("r_chain"), 1)

                def weigh(G, g, Q, at, nk):
                    by_value = bank[4 + g % 2][:, QG * D_R * (1 - g % 2):QG * D_R * (1 - g % 2) + P]
                    inverse = RIR[:, g % 8:g % 8 + 1]
                    dve.wait_ge(sem("r_chain"), G * 2 + 2)
                    if s.which:
                        dve.scalar_tensor_tensor(out=ZR[:, g % 2, :], in0=by_value, scalar=inverse, in1=k_("head_mask"),
                                                 op0=ALU.mult, op1=ALU.mult).then_inc(sem("r_weighted"), 1)
                        return
                    dve.scalar_tensor_tensor(out=TZ[:, g % 2, :].rearrange("p (h d) -> p h d", h=HEADS_R),
                                             in0=by_value.rearrange("p (h d) -> p h d", h=HEADS_R), scalar=inverse,
                                             in1=bc(W2[:, g % 2, :].unsqueeze(1), [P, HEADS_R, D_R]),
                                             op0=ALU.mult, op1=ALU.add).then_inc(sem("r_weighted"), 1)

                def head_copy(G, g, Q, at, nk):
                    if g % 4 < 3:
                        return
                    dve.wait_ge(sem("r_heads"), G + 1)
                    dst = out_flat[:, bass.ds(at[0] * T + (at[1] - 3) * QG, 4 * QG)]
                    src = bank[7][:, 0:4 * QG]
                    if s.which == 0:
                        dve.tensor_copy(dst, src).then_inc(sem("r_head_copied"), 1)
                    else:
                        rows_ = slice(32 * at[0], 32 * at[0] + 32)
                        dve.tensor_copy(position_heads[rows_, :, bass.ds((at[1] - 3) * QG, 4 * QG)].rearrange("p l (q j) -> p l q j", q=4),
                                        bank[7][rows_, P:2 * P].rearrange("p (q l j) -> p l q j", q=4, l=C))
                        dve.tensor_scalar(dst, src, wt(s, WR, "bv"), None, ALU.add).then_inc(sem("r_head_copied"), 1)

                def maxima(G, g, Q, at, nk):
                    dve.wait_ge(sem("r_scores"), G + 1)
                    n = score_columns(s.which, g, nk)
                    dve.tensor_reduce(out=NBR[:, g % 4:g % 4 + 1], in_=bank[g % 2][:, 0:n], axis=AX.X, op=ALU.max,
                                      negate=True).then_inc(sem("r_max"), 1)

                for st in core_steps(dve, s.which):
                    st(head_copy, 11)
                    st(own_place, 9)
                    st(diagonal, 5)
                    st(own_sum, 9)
                    st(invert, 8)
                    st(weigh, 9)
                    st(maxima, 6)

            def r_out(s):
                add_residual(s, s.k, outer, wt(s, WR, "bo") if s.which else None)

            def w_rotate(s):
                t = 0 if s.x == "q" else 2
                if s.n == 0:
                    dve.wait_ge(sem("rotary_loaded"), 16)
                reached(dve, "w_scaled", s.n - 1)
                dve.wait_ge(sem("w_squared"), s.n + 1)
                dve.scalar_tensor_tensor(out=R1[:, s.n % 2, :], in0=full(s.k)[:, :], scalar=wt(s, WW, s.x + "s"),
                                         in1=rotary[:, t, :], op0=ALU.mult, op1=ALU.mult).then_inc(sem("w_cos"), 1)
                dve.scalar_tensor_tensor(out=R2[:, s.n % 2, :], in0=full(s.k + 1)[:, :], scalar=wt(s, WW, s.x + "s_rot"),
                                         in1=rotary[:, t + 1, :], op0=ALU.mult, op1=ALU.mult).then_inc(sem("w_sin"), 1)

            def w_length(s):
                dve.wait_ge(sem("w_added"), s.n + 1)
                dve.wait_ge(sem("w_inverse"), s.n + 1)
                if s.x == "q":
                    to = [(slice(64 * a, 64 * a + 64), QW[64 * a:64 * a + 64, a, s.pt, :]) for a in range(2)]
                else:
                    to = [(slice(0, P), KW[:, s.pt, :])]
                for rows_, dst in to:
                    last = dve.scalar_tensor_tensor(out=dst, in0=RNW[rows_, s.n % 4, :], scalar=1e12,
                                                    in1=R1[rows_, s.n % 2, :], op0=ALU.min, op1=ALU.mult)
                last.then_inc(sem("w_scaled"), 1)

            def w_scores(s):
                lo = 64 if s.i else P
                for a in range(2):
                    dve.tensor_tensor_reduce(out=SW[:, s.n % 2, a, lo:256], in0=full(s.k + a)[:, lo:256],
                                             in1=k_("window_mask")[:, lo - 64:192], scale=-8.0, scalar=3e38,
                                             op0=ALU.add, op1=ALU.min, accum_out=small_w[:, s.n % 4, a:a + 1])\
                        .then_inc(sem("w_scored"), 1)

            def w_turn(s):
                if s.n % 2:
                    return
                v = "p (a b t) -> p a b t"
                lo = 0 if s.i else 1
                o = full(s.k)
                if s.n:
                    dve.wait_ge(sem("w_turned"), s.n)
                dve.tensor_copy(TW[:, s.n % 2, :].rearrange(v, a=2, b=2)[:, :, lo:2, :],
                                o[:, :].rearrange(v, a=2, b=2)[:, :, lo:2, :]).then_inc(sem("w_turned"), 1)

            def w_values(s):
                o = full(s.k)
                inverse = small_w[:, s.n % 4, 4:6]
                link(dve.reciprocal(inverse, small_w[:, s.n % 4, 2:4]))
                dve.tensor_tensor(OW[:, s.i % 2, s.hp * P:(s.hp + 1) * P].rearrange("p (h d) -> p h d", h=2),
                                  o[:, 0:P].rearrange("p (h d) -> p h d", h=2), bc(inverse.unsqueeze(2), [P, 2, D_W]),
                                  ALU.mult).then_inc(sem("w_normalised"), 1)

            def w_out(s):
                add_residual(s, s.k, inner)

            def w_mlp(s):
                for j in range(HT_W):
                    o = full(s.k + 2 * j + 1)[:, :]
                    dve.wait_ge(sem("w_gelu"), HT_W * s.n + j + 1)
                    dve.scalar_tensor_tensor(out=HW[:, s.n % 2, j, :], in0=o, scalar=wt(s, WW, "b1a", j, 1),
                                             in1=GW[:, s.n % 2, j, :], op0=ALU.add, op1=ALU.mult).then_inc(sem("w_gated"), 1)
                add_residual(s, s.k + 2 * HT_W, inner, wt(s, WW, "b2"))

            def h_forward(s):
                dve.wait_ge(sem("h_spectra"), 4)
                dve.wait_ge(sem("h_transformed"), 2 * (s.n + 1))
                for part, m in ((0, M1), (1, M2)):
                    last = dve.tensor_tensor(m[:, s.n % 2], bc(XH[:, s.n % 2, part, :].unsqueeze(1), [P, 2, DFT]),
                                             SPEC[:, s.conv], ALU.mult)
                last.then_inc(sem("h_multiplied"), 1)

            def h_inverse(s):
                k = KH[:, s.c, :]
                dve.scalar_tensor_tensor(out=k, in0=k, scalar=wt(s, WH, "D" if s.conv else "k_D"), in1=full(s.k)[:, :],
                                         op0=ALU.mult, op1=ALU.add).then_inc(sem("h_convolved"), 1)
                dve.wait_ge(sem("h_convolved"), s.n + 1)
                if s.conv == 0:
                    dve.tensor_tensor(k, k, VH[:, s.c, :], ALU.mult).then_inc(sem("h_kv"), 1)
                else:
                    dve.tensor_tensor(VH[:, s.c, :], k, QH[:, s.c, :], ALU.mult).then_inc(sem("h_gated"), 1)

            def h_out(s):
                add_residual(s, s.k, outer, wt(s, WH, "bo"))

            parts = dict(weights=lambda s: weights_here(dve, s), tables=tables, enter=enter, leave=leave, norm_mean=norm_mean, norm_scale=norm_scale, fold=fold, a_project=a_project,
                         a_linear=a_linear, a_context=a_context, a_scores=a_scores, a_turn=a_turn, a_values=a_values,
                         a_out=a_out, a_mlp=a_mlp, gate=gate, expert=expert, expert_out=expert_out, r_project=r_project,
                         core=core, r_out=r_out, w_rotate=w_rotate, w_length=w_length, w_scores=w_scores, w_turn=w_turn,
                         w_values=w_values, w_out=w_out, w_mlp=w_mlp, h_forward=h_forward, h_inverse=h_inverse, h_out=h_out)
            dve.wait_ge(sem("const_loaded"), 16)
            for s in plan:
                if s.kind in parts:
                    parts[s.kind](s)

        @block.gpsimd
        def _(pool):
            half = P // 2

            def norm_scale(s):
                if s.gain:
                    if s.affine == 0:
                        pool.memset(QL, 0.0).then_inc(sem("a_q_cleared"), 1)
                        pool.wait_ge(sem("a_q_cleared"), 1)
                    pool.wait_ge(sem("norm_scaled"), s.affine + 1)
                    a = streams[s.dst][:, s.c, :]
                    pool.tensor_scalar(a, a, wt(s, s.table, s.gain[1]), None, ALU.add).then_inc(sem("norm_done"), 1)
                    pool.wait_ge(sem("norm_done"), C * s.norm + s.c + 1)

            def shift(s):
                reached(pool, "w_added", s.rotations)
                source_ready(pool, s, s.c)
                if s.n == 0:
                    pool.memset(shifted[half:P, :, 0:1], 0.0).then_inc(sem("first_cleared"), 1)
                    pool.wait_ge(sem("first_cleared"), 1)
                if s.c == 0 and s.via == "norm":
                    for lane in range(C):
                        source_ready(pool, s, lane)
                    stage = s.n // (2 * DEPTH_W * C)
                    pool.memset(PW[:, :, :, 0:WIN], 0.0).then_inc(sem("pad_cleared"), 1)
                    pool.wait_ge(sem("pad_cleared"), stage + 1)
                    pool.memset(QW, 0.0).then_inc(sem("q_cleared"), 1)
                    pool.wait_ge(sem("q_cleared"), stage + 1)
                pool.tensor_copy(shifted[0:half, s.c, :], inner[0:half, s.c, :])
                pool.tensor_copy(shifted[half:P, s.c, 1:T], inner[half:P, s.c, 0:T - 1]).then_inc(sem("shift_done"), 1)
                pool.wait_ge(sem("shift_done"), s.n + 1)

            def core(s):
                def spread(G, g, Q, at, nk):
                    half, first = g % 2, at[1] - g % 4
                    queries = (QR_HI, QR_LO)[half]
                    if g % 4 >= 2:
                        one_lane = queries[:, :, :].rearrange("p l t -> p (l t)")[:, bass.ds(at[0] * T + first * QG, 4 * QG)]
                        pool.tensor_tensor(A4[:, half, (g // 4) % 2, :].rearrange("p (t h) -> p t h", h=HEADS_R),
                                           bc(one_lane.unsqueeze(2), [P, 4 * QG, HEADS_R]),
                                           bc(k_("spread_mask").unsqueeze(1), [P, 4 * QG, HEADS_R]), ALU.mult)\
                            .then_inc(sem("r_spread" if s.which == 0 else "r_keys_spread"), 1)
                    elif s.which:
                        if isinstance(Q, int) and Q >= CHUNKS + 2:
                            pool.wait_ge(sem("r_repeated"), Q - 1)
                        by_token = queries[:, :, bass.ds(first * QG, 4 * QG)].rearrange("p l t -> p t l")
                        mask = k_("swap_mask")[:, HEADS_R * at[0]:HEADS_R * (at[0] + 1)].rearrange("p (l m) -> p l m", l=C)
                        wide = [P, 4 * QG, C, HEADS_R // C]
                        pool.tensor_tensor(AX4[:, half, (g // 4) % 2, :].rearrange("p (t l m) -> p t l m", t=4 * QG, l=C),
                                           bc(by_token.unsqueeze(3), wide), bc(mask.unsqueeze(1), wide), ALU.mult)\
                            .then_inc(sem("r_spread"), 1)

                def embed(G, g, Q, at, nk):
                    room = (g % 2) * (P + QG * D_R)
                    if s.which == 0:
                        blocks = slice(NT - nk, NT)
                    else:
                        blocks = bass.ds(NT - 1 - at[2], NT)
                    at_group = (P - QG - QG * g) * D_R
                    dst = VR.rearrange("p l b c -> p (l b) c")[:, bass.ds(at[0] * NT, nk), room:room + QG * D_R]
                    src = value_blocks[:, blocks, at_group:at_group + QG * D_R]
                    pool.tensor_tensor(dst, src, bc(k_("ones")[:, 0:QG * D_R].unsqueeze(1), [P, nk, QG * D_R]), ALU.mult)\
                        .then_inc(sem("r_embedded"), 1)

                def own_head(G, g, Q, at, nk):
                    pool.wait_ge(sem("r_weighted"), G + 1)
                    if s.which:
                        pool.tensor_tensor(Z2[:, g % 2, :].rearrange("p (q d) -> p q d", q=4),
                                           bc(W2[:, g % 2, :].unsqueeze(1), [P, 4, D_R]),
                                           k_("quarter_mask").rearrange("p (q d) -> p q d", q=4), ALU.mult)\
                            .then_inc(sem("r_masked"), 1)
                        return
                    pool.tensor_tensor(ZR[:, g % 2, :], TZ[:, g % 2, :], k_("head_mask"), ALU.mult).then_inc(sem("r_masked"), 1)

                pool.wait_ge(sem("r_q_copied"), C * (s.which + 1))
                pool.wait_ge(sem("value_table"), 16 * (s.which + 1))
                pool.wait_ge(sem("r_values_copied"), C * (s.which + 1))
                for st in core_steps(pool, s.which):
                    st(own_head, 9)
                    st(embed, 7)
                    st(spread, 0)

            def w_rotate(s):
                pool.wait_ge(sem("w_sin"), s.n + 1)
                pool.tensor_tensor(R1[:, s.n % 2, :], R1[:, s.n % 2, :], R2[:, s.n % 2, :], ALU.add).then_inc(sem("w_added"), 1)

            def h_forward(s):
                b = s.n % 2
                pool.wait_ge(sem("h_multiplied"), s.n + 1)
                pool.tensor_tensor(YH[:, b, 0, :], M1[:, b, 0, :], M2[:, b, 1, :], ALU.subtract).then_inc(sem("h_product"), 1)
                pool.tensor_tensor(YH[:, b, 1, :], M1[:, b, 1, :], M2[:, b, 0, :], ALU.add).then_inc(sem("h_product"), 1)

            parts = dict(weights=lambda s: weights_here(pool, s), norm_scale=norm_scale, shift=shift, core=core, w_rotate=w_rotate, h_forward=h_forward)
            pool.wait_ge(sem("const_loaded"), 16)
            for s in plan:
                if s.kind in parts:
                    parts[s.kind](s)


def shape_constants():
    import numpy as np

    p = np.arange(P)
    const = np.zeros((P, CONST_W), np.float32)

    def put(name, a):
        at, w = CONST[name]
        const[:a.shape[0], at:at + w] = a

    put("ident", np.eye(P))
    put("mean", np.full((P, P), 1.0 / P))
    put("ones", np.ones((P, P)))
    put("pair_ones", p[:, None] // D_W == p[None, :] // D_W)
    put("head_mask", p[:, None] % HEADS_R == p[None, :] // D_R)
    put("pick_query", p[:, None] // HEADS_R == np.arange(QG)[None, :])
    put("query_mask", p[:, None] // HEADS_R == QG - 1 - np.arange(64)[None, :] // D_R)
    put("spread_mask", p[:, None] // D_R == np.arange(HEADS_R)[None, :])
    x = np.arange(192)[None, :]
    put("repeat", (p[:, None] % D_R == x % D_R) & (x // 64 == 1))
    put("diag_query", p[:, None] % 64 // D_R == p[None, :] // HEADS_R)
    put("causal_query", p[:, None] == p[None, :] // HEADS_R)
    x = np.arange(2 * P - QG)[None, :]
    put("causal_rows", np.where((x - (P - QG) > p[:, None]) & (p[:, None] < QG), NEG, 0.0))
    lane_head = np.arange(C)[:, None] + 4 * (np.arange(HEADS_R)[None, :] % 4)
    put("swap_mask", p[:, None] // D_R == lane_head.reshape(1, -1))
    lane_query = np.arange(32)[None, :]
    put("pick_pair", (p[:, None] // HEADS_R == lane_query % QG) & (p[:, None] % 4 == lane_query // QG))
    put("quarter_mask", p[:, None] % HEADS_R // 4 == lane_query // D_R)
    s = np.arange(2 * P)
    put("local_mask", np.where(s[None, :] - P > p[:, None], NEG, 0.0))
    back = p[:, None] - (np.arange(P + WIN)[None, :] - WIN)
    put("window_mask", np.where((back < 0) | (back > WIN), NEG, 0.0))
    put("linear_mask", np.arange(64)[:, None] // DH_A == np.arange(64)[None, :] // DH_A)
    e = np.arange(EXPERTS)
    put("lower", np.broadcast_to((e[None, :] < e[:, None]).reshape(1, 64), (P, 64)))
    put("eps", np.broadcast_to(np.array([EPS, 2.0 ** -60, 15 * np.log(2.0), 0.0]), (P, 4)))

    d = p % D_W
    half_idx = (2 * (d % (D_W // 2))).astype(np.float32)
    inv_freq = (np.float32(1.0) / np.float32(10000.0) ** (half_idx / np.float32(D_W))).astype(np.float32)
    t = np.arange(T, dtype=np.float32)
    freqs = (t[None, :] * inv_freq[:, None]).astype(np.float32).astype(np.float64)
    base = (half_idx + 0.4 * D_W) / (1.4 * D_W)
    scale = base.astype(np.float64)[:, None] ** ((t - T // 2) / (WIN // 2))[None, :]
    sign = np.where(d < D_W // 2, -1.0, 1.0)[:, None]
    cos, sin = np.cos(freqs), np.sin(freqs) * sign
    rotary = np.stack([cos * scale, sin * scale, cos / scale, sin / scale], 1).reshape(P, 4 * T).astype(np.float32)

    theta = np.pi * (np.arange(DFT) + 0.5) / DFT
    turn = np.arange(T)[:, None] * theta[None, :]
    forward = np.concatenate([np.cos(turn), -np.sin(turn)], 1).reshape(NT, P, 2 * DFT).transpose(1, 0, 2)
    inverse = np.concatenate([np.cos(turn).T, -np.sin(turn).T], 0) / DFT
    inverse = inverse.reshape(2 * FT, P, T).transpose(1, 0, 2)
    dft = np.concatenate([forward.reshape(P, -1), inverse.reshape(P, -1)], 1).astype(np.float32)
    return {"const": const, "rotary": rotary, "dft": dft}


def lay_out(inputs):
    import numpy as np

    arrays = {}

    def pack(name, names, width, parts):
        a = np.zeros((P, width), np.float32)
        for key, value in parts.items():
            at, w = names[key]
            value = value.reshape(value.shape[0], -1)
            a[:value.shape[0], at:at + value.shape[1]] = value
        arrays[name] = a

    def rows(w):
        tiles = -(-w.shape[0] // P)
        full = np.zeros((tiles * P, w.shape[1]), w.dtype)
        full[:w.shape[0]] = w
        return full.reshape(tiles, P, -1).transpose(1, 0, 2)

    def column(v):
        return rows(v[:, None])[:, :, 0]

    A = {k[10:]: v for k, v in inputs.items() if k.startswith("L0_attn_a_")}
    for i in range(DEPTH_A):
        def spaced(w):
            out = np.zeros((P, LOC, 32), w.dtype)
            out[:, :, :DH_A] = w[:, :LOC * DH_A].reshape(P, LOC, DH_A)
            return out
        linear = slice(LOC * DH_A, P)
        pack(f"wA{i}", WA, WA_W, {
            "q_loc": spaced(A["Wq"][i]), "k_loc": spaced(A["Wk"][i]),
            "qkv": np.concatenate([A["Wq"][i][:, linear], A["Wk"][i][:, linear], A["Wv"][i]], 1),
            "o": A["Wo"][i], "w1": A["W1"][i], "w2": rows(A["W2"][i]), "bo": column(A["bo"][i]),
            "g1": column(A["ln1_g"][i]), "b1n": column(A["ln1_b"][i]), "b1": column(A["b1"][i]),
            "b2": column(A["b2"][i]), "g2": column(A["ln2_g"][i]), "b2n": column(A["ln2_b"][i])})

    pack("wE", WE, WE_W, {"experts": inputs["L0_ffn_We"].transpose(2, 0, 1), "gate": inputs["L0_ffn_Wg"],
                          "be": inputs["L0_ffn_be"], "bg": inputs["L0_ffn_bg"][None, :]})

    w = inputs["L0_attn_b_w_attn"]
    pack("wR0", WR, WR_W, {"q": w[:, 0:P], "k": w[:, P:2 * P], "v": w[:, 2 * P:3 * P], "o": inputs["L0_attn_b_w_proj"]})
    B = {k[10:]: v for k, v in inputs.items() if k.startswith("L1_attn_a_")}
    pack("wR1", WR, WR_W, {"q": B["Wq"].T, "k": B["Wk"].T, "v": B["Wv"].T, "o": B["Wo"].T, "bq": column(B["bq"]),
                           "bk": column(B["bk"]), "bv": column(B["bv"]), "bo": column(B["bo"])})

    W = {k[7:]: v for k, v in inputs.items() if k.startswith("L1_ffn_")}
    inner = HEADS_W * D_W
    swapped = np.arange(inner).reshape(HEADS_W, 2, D_W // 2)[:, ::-1].reshape(-1)
    for i in range(DEPTH_W):
        q, k, v = (W["wqkv"][i][:, j * inner:(j + 1) * inner] for j in range(3))
        twice = lambda a: column(np.concatenate([a, a]))
        turned = lambda a: np.concatenate([a[D_W // 2:], a[:D_W // 2]])
        pack(f"wW{i}", WW, WW_W, {
            "q": q, "q_rot": q[:, swapped], "k": k, "k_rot": k[:, swapped], "v": v, "o": rows(W["wo"][i]),
            "w1a": W["w1"][i][:, :HID_W], "w1g": W["w1"][i][:, HID_W:], "w2": rows(W["w2"][i]),
            "qs": twice(W["q_scale"][i]), "qs_rot": twice(turned(W["q_scale"][i])),
            "ks": twice(W["k_scale"][i]), "ks_rot": twice(turned(W["k_scale"][i])),
            "g": column(W["ln_g"][i]), "b": column(W["ln_b"][i]),
            "b1a": column(W["b1"][i][:HID_W]), "b1g": column(W["b1"][i][HID_W:]), "b2": column(W["b2"][i])})

    H = {k[10:]: v for k, v in inputs.items() if k.startswith("L1_attn_b_")}
    pack("wH", WH, WH_W, {"q": H["Wq"].T, "k": H["Wk"].T, "v": H["Wv"].T, "o": H["Wo"].T,
                          "kernels": np.concatenate([H["k_kernel"], H["ssm_kernel"]], 1),
                          "bq": column(H["bq"]), "bk": column(H["bk"]), "bv": column(H["bv"]), "bo": column(H["bo"]),
                          "k_D": column(H["k_D"]), "D": column(H["D"])})

    arrays["embk0"] = np.ascontiguousarray(inputs["L0_attn_b_embk"][::-1].T)
    arrays["embk1"] = np.ascontiguousarray(inputs["L1_attn_a_rel_k_emb"][::-1].T)
    arrays["embv0"] = np.ascontiguousarray(inputs["L0_attn_b_embv"][::-1])
    arrays["embv1"] = np.ascontiguousarray(inputs["L1_attn_a_rel_v_emb"][::-1])
    arrays["x"] = np.ascontiguousarray(inputs["L0_attn_a_x"])
    return arrays


def kernel(**inputs):
    import numpy as np
    import concourse.bacc as bacc
    from concourse.bass_utils import run_bass_kernel_spmd

    arrays = lay_out({k: np.asarray(v) for k, v in inputs.items()})
    arrays.update(shape_constants())
    nc = bacc.Bacc("TRN2", target_bir_lowering=False, num_devices=1)
    aps = {name: nc.dram_tensor("in_" + name, a.shape, F32, kind="ExternalInput").ap() for name, a in arrays.items()}
    for pair in ("embk", "embv"):
        aps[pair] = [aps[pair + "0"], aps[pair + "1"]]
    scratch = [nc.dram_tensor(f"embv_padded{w}", (2 * T, D_R), F32, kind="Internal").ap() for w in range(2)]
    out = nc.dram_tensor("out", (C, T, P), F32, kind="ExternalOutput").ap()
    hybrid_network(nc, aps, scratch, out)
    result = run_bass_kernel_spmd(nc, [{"in_" + name: a for name, a in arrays.items()}], core_ids=[0])
    return result.results[0]["out"]
```
